# Optimizing a Trainium2 kernel written in Bass

```python
import numpy as np
import jax
import jax.numpy as jnp

def _softmax(x, axis=-1):
    return jax.nn.softmax(x, axis=axis)

def _gelu(x):
    return jax.nn.gelu(x, approximate=True)

def _silu(x):
    return jax.nn.silu(x)

def _sigmoid(x):
    return jax.nn.sigmoid(x)

def _layernorm(x, axis=-1, eps=1e-05):
    m = jnp.mean(x, axis=axis, keepdims=True)
    v = jnp.var(x, axis=axis, keepdims=True)
    return (x - m) / jnp.sqrt(v + eps)

def _scatter_add(tgt, idx, src, axis=0):
    return tgt.at[idx].add(src)

def _segment_sum(src, seg, n):
    return jax.ops.segment_sum(src, seg, n)
kernel_name = 'mk_decoder_preln_d1_seqx_r8_849fda'

def setup_inputs(seed: int=0):
    np.random.seed(seed)
    _w = jnp.asarray

    def _rec_inputs():
        import jax
        import jax.numpy as jnp
        _rk = jax.random.key(seed)
        x = 7.22e-05 + 1 * jax.random.normal(jax.random.fold_in(_rk, 1), (64, 64, 256), jnp.float32)
        _lenS = 64 - jax.random.randint(jax.random.fold_in(_rk, 7), (64,), 0, max(1, 64 // 4) + 1, jnp.int32)
        _lenS2 = 64 - jax.random.randint(jax.random.fold_in(_rk, 8), (64,), 0, max(1, 64 // 4) + 1, jnp.int32)
        _ctx_2048P = jax.random.normal(jax.random.fold_in(_rk, 11), (64, 16, 256), jnp.float32)
        _ctx_2048c = jax.random.dirichlet(jax.random.fold_in(_rk, 511), 0.3 * jnp.ones((16,), jnp.float32), (64, 64))
        _ctx_2048t = jnp.einsum('bsk,bkd->bsd', _ctx_2048c, _ctx_2048P)
        _ctx_2048t = _ctx_2048t * jax.lax.rsqrt(jnp.mean(jnp.square(_ctx_2048t)) + 1e-12) * 0.953939
        ctx_2048 = 4.13588e-05 + 0.999923 * (_ctx_2048t + 0.3 * jax.random.normal(jax.random.fold_in(_rk, 611), (64, 64, 256), jnp.float32))
        return (x, ctx_2048)
    x, ctx_2048 = _rec_inputs()

    def _L0_attn_setup():
        import jax, jax.numpy as jnp
        import numpy as np
        B, S, D = (4, 512, 256)
        IDENTITY_WEIGHT = 0.5
        ROT_DIM = D // 2

        def _layernorm(x, gamma, beta, eps=1e-05):
            mu = jnp.mean(x, axis=-1, keepdims=True)
            var = jnp.var(x, axis=-1, keepdims=True)
            return (x - mu) * jax.lax.rsqrt(var + eps) * gamma + beta

        def _rotary(t, rot_dim, theta=10000.0):
            seq = t.shape[-2]
            inv_freq = 1.0 / theta ** (jnp.arange(0, rot_dim, 2, dtype=jnp.float32) / rot_dim)
            freqs = jnp.arange(seq, dtype=jnp.float32)[:, None] * inv_freq[None, :]
            freqs = jnp.repeat(freqs, 2, axis=-1)
            cos, sin = (jnp.cos(freqs), jnp.sin(freqs))
            t_rot, t_pass = (t[..., :rot_dim], t[..., rot_dim:])
            x1, x2 = (t_rot[..., 0::2], t_rot[..., 1::2])
            rot_half = jnp.stack([-x2, x1], axis=-1).reshape(t_rot.shape)
            return jnp.concatenate([t_rot * cos + rot_half * sin, t_pass], axis=-1)

        def _cos_sim(x):
            return x / jnp.linalg.norm(x, axis=-1, keepdims=True)
        key = jax.random.key(seed)
        ks = jax.random.split(key, 3)
        scale = 0.02
        return {'X': jax.random.normal(ks[0], (B, S, D), jnp.float32), 'W_in': jax.random.normal(ks[1], (D, 3 * D), jnp.float32) * scale, 'b_in': jnp.zeros((3 * D,), jnp.float32), 'W_out': jax.random.normal(ks[2], (D, D), jnp.float32) * scale, 'b_out': jnp.zeros((D,), jnp.float32), 'gamma': jnp.ones((D,), jnp.float32), 'beta': jnp.zeros((D,), jnp.float32)}
    _L0_attn_all = _L0_attn_setup()
    _L0_attn_in = {k: v for k, v in _L0_attn_all.items() if k in ('W_in', 'b_in', 'W_out', 'b_out', 'gamma', 'beta')}
    del _L0_attn_all

    def _L0_xattn_setup():
        import jax, jax.numpy as jnp
        import numpy as np
        N_HEAD = 8
        key = jax.random.key(seed)
        k1, k2, k3 = jax.random.split(key, 3)
        B, D, L = (4, 128, 256)
        q = jax.random.normal(k1, (B, D, L), dtype=jnp.float32)
        k = jax.random.normal(k2, (B, D, L), dtype=jnp.float32)
        v = jax.random.normal(k3, (B, D, L), dtype=jnp.float32)
        gamma = jnp.ones((), dtype=jnp.float32)
        return {'q': q, 'k': k, 'v': v, 'gamma': gamma}
    _L0_xattn_all = _L0_xattn_setup()
    _L0_xattn_in = {k: v for k, v in _L0_xattn_all.items() if k in ('gamma',)}
    del _L0_xattn_all

    def _L0_ffn_setup():
        import jax, jax.numpy as jnp
        import numpy as np
        import math
        D_MODEL = 256
        D_FF = 1024
        NUM_EXPERTS = 8
        TOP_K = 2
        CAPACITY_FACTOR = 1.25
        BATCH, SEQ = (4, 256)

        def _moe_forward(x, Wg, w1, w2):
            B, T, d = x.shape
            S = B * T
            E, K = (NUM_EXPERTS, TOP_K)
            C = math.ceil(CAPACITY_FACTOR * S * K / E)
            xr = x.reshape(S, d)
            probs = jax.nn.softmax(xr @ Wg, axis=-1)
            gate_vals, expert_idx = jax.lax.top_k(probs, K)
            flat_e = expert_idx.reshape(-1)
            oh = jax.nn.one_hot(flat_e, E, dtype=jnp.int32)
            pos = jnp.sum((jnp.cumsum(oh, axis=0) - 1) * oh, axis=1)
            kept = pos < C
            i = jnp.arange(S * K)
            slot = i % K * S + i // K
            sentinel = S * K
            pos_w = jnp.where(kept, pos, C)
            dispatch_mask = jnp.full((E, C), sentinel, dtype=jnp.int32)
            dispatch_mask = dispatch_mask.at[flat_e, pos_w].set(slot.astype(jnp.int32), mode='drop')
            combine_weights = (gate_vals * kept.reshape(S, K)).T
            dispatched = xr[dispatch_mask.reshape(-1) % S].reshape(E, C, d)
            h = jax.nn.relu(jnp.einsum('ecd,edf->ecf', dispatched, w1))
            expert_out = jnp.einsum('ecf,efd->ecd', h, w2)
            rerouted = jnp.zeros((S * K + 1, d), dtype=expert_out.dtype)
            rerouted = rerouted.at[dispatch_mask.reshape(-1)].set(expert_out.reshape(-1, d))
            rerouted = rerouted[:-1].reshape(K, S, d)
            out = jnp.einsum('ks,ksm->sm', combine_weights, rerouted)
            return out.reshape(B, T, d)
        key = jax.random.key(seed)
        k1, k2, k3, k4 = jax.random.split(key, 4)
        x = jax.random.normal(k1, (BATCH, SEQ, D_MODEL), dtype=jnp.float32)
        Wg = jax.random.normal(k2, (D_MODEL, NUM_EXPERTS), dtype=jnp.float32) * 0.02
        w1 = jax.random.normal(k3, (NUM_EXPERTS, D_MODEL, D_FF), dtype=jnp.float32) * 0.02
        w2 = jax.random.normal(k4, (NUM_EXPERTS, D_FF, D_MODEL), dtype=jnp.float32) * 0.02
        return {'x': x, 'Wg': Wg, 'w1': w1, 'w2': w2}
    _L0_ffn_all = _L0_ffn_setup()
    _L0_ffn_in = {k: v for k, v in _L0_ffn_all.items() if k in ('Wg', 'w1', 'w2')}
    del _L0_ffn_all
    return {'x': x, 'ctx_2048': ctx_2048, 'L0_attn_W_in': _L0_attn_in['W_in'], 'L0_attn_b_in': _L0_attn_in['b_in'], 'L0_attn_W_out': _L0_attn_in['W_out'], 'L0_attn_b_out': _L0_attn_in['b_out'], 'L0_attn_gamma': _L0_attn_in['gamma'], 'L0_attn_beta': _L0_attn_in['beta'], 'L0_xattn_gamma': _L0_xattn_in['gamma'], 'L0_ffn_Wg': _L0_ffn_in['Wg'], 'L0_ffn_w1': _L0_ffn_in['w1'], 'L0_ffn_w2': _L0_ffn_in['w2']}

def reference(x, ctx_2048, L0_attn_W_in, L0_attn_b_in, L0_attn_W_out, L0_attn_b_out, L0_attn_gamma, L0_attn_beta, L0_xattn_gamma, L0_ffn_Wg, L0_ffn_w1, L0_ffn_w2):
    import jax
    import jax.numpy as jnp

    def _L0_attn_ref(X, W_in, b_in, W_out, b_out, gamma, beta):
        import jax, jax.numpy as jnp
        import numpy as np
        B, S, D = (4, 512, 256)
        IDENTITY_WEIGHT = 0.5
        ROT_DIM = D // 2

        def _layernorm(x, gamma, beta, eps=1e-05):
            mu = jnp.mean(x, axis=-1, keepdims=True)
            var = jnp.var(x, axis=-1, keepdims=True)
            return (x - mu) * jax.lax.rsqrt(var + eps) * gamma + beta

        def _rotary(t, rot_dim, theta=10000.0):
            seq = t.shape[-2]
            inv_freq = 1.0 / theta ** (jnp.arange(0, rot_dim, 2, dtype=jnp.float32) / rot_dim)
            freqs = jnp.arange(seq, dtype=jnp.float32)[:, None] * inv_freq[None, :]
            freqs = jnp.repeat(freqs, 2, axis=-1)
            cos, sin = (jnp.cos(freqs), jnp.sin(freqs))
            t_rot, t_pass = (t[..., :rot_dim], t[..., rot_dim:])
            x1, x2 = (t_rot[..., 0::2], t_rot[..., 1::2])
            rot_half = jnp.stack([-x2, x1], axis=-1).reshape(t_rot.shape)
            return jnp.concatenate([t_rot * cos + rot_half * sin, t_pass], axis=-1)

        def _cos_sim(x):
            return x / jnp.linalg.norm(x, axis=-1, keepdims=True)
        Xn = _layernorm(X, gamma, beta)
        QKV = Xn @ W_in + b_in
        Q, K, V = jnp.split(QKV, 3, axis=-1)
        K = _rotary(K, ROT_DIM)
        V = _rotary(V, ROT_DIM)
        A = jnp.sum(_cos_sim(K) * _cos_sim(V), axis=-2)
        A = (1.0 - IDENTITY_WEIGHT) * A + IDENTITY_WEIGHT
        Y = A[:, None, :] * Q
        Y = Y @ W_out + b_out
        return Y + X

    def _L0_xattn_ref(q, k, v, gamma):
        import jax, jax.numpy as jnp
        import numpy as np
        N_HEAD = 8
        B, Dq, Lq = q.shape
        Dv, Lk = (v.shape[-2], v.shape[-1])
        h = N_HEAD
        dq = Dq // h
        dv = Dv // h
        qh = q.reshape(B, h, dq, Lq)
        kh = k.reshape(B, h, dq, Lk)
        vh = v.reshape(B, h, dv, Lk)
        scale = 1.0 / jnp.sqrt(jnp.asarray(dq, dtype=q.dtype))
        qk = jnp.einsum('bhdq,bhdl->bhql', qh, kh) * scale
        sm = jax.nn.softmax(qk, axis=-1)
        ret = jnp.einsum('bhql,bhdl->bhdq', sm, vh)
        ret = ret.reshape(B, Dv, Lq)
        return gamma * ret

    def _L0_ffn_ref(x, Wg, w1, w2):
        import jax, jax.numpy as jnp
        import numpy as np
        import math
        D_MODEL = 256
        D_FF = 1024
        NUM_EXPERTS = 8
        TOP_K = 2
        CAPACITY_FACTOR = 1.25
        BATCH, SEQ = (4, 256)

        def _moe_forward(x, Wg, w1, w2):
            B, T, d = x.shape
            S = B * T
            E, K = (NUM_EXPERTS, TOP_K)
            C = math.ceil(CAPACITY_FACTOR * S * K / E)
            xr = x.reshape(S, d)
            probs = jax.nn.softmax(xr @ Wg, axis=-1)
            gate_vals, expert_idx = jax.lax.top_k(probs, K)
            flat_e = expert_idx.reshape(-1)
            oh = jax.nn.one_hot(flat_e, E, dtype=jnp.int32)
            pos = jnp.sum((jnp.cumsum(oh, axis=0) - 1) * oh, axis=1)
            kept = pos < C
            i = jnp.arange(S * K)
            slot = i % K * S + i // K
            sentinel = S * K
            pos_w = jnp.where(kept, pos, C)
            dispatch_mask = jnp.full((E, C), sentinel, dtype=jnp.int32)
            dispatch_mask = dispatch_mask.at[flat_e, pos_w].set(slot.astype(jnp.int32), mode='drop')
            combine_weights = (gate_vals * kept.reshape(S, K)).T
            dispatched = xr[dispatch_mask.reshape(-1) % S].reshape(E, C, d)
            h = jax.nn.relu(jnp.einsum('ecd,edf->ecf', dispatched, w1))
            expert_out = jnp.einsum('ecf,efd->ecd', h, w2)
            rerouted = jnp.zeros((S * K + 1, d), dtype=expert_out.dtype)
            rerouted = rerouted.at[dispatch_mask.reshape(-1)].set(expert_out.reshape(-1, d))
            rerouted = rerouted[:-1].reshape(K, S, d)
            out = jnp.einsum('ks,ksm->sm', combine_weights, rerouted)
            return out.reshape(B, T, d)
        return _moe_forward(x, Wg, w1, w2)
    x = x + _L0_attn_ref(_layernorm(x, axis=-1), L0_attn_W_in, L0_attn_b_in, L0_attn_W_out, L0_attn_b_out, L0_attn_gamma, L0_attn_beta)
    x = x + _L0_xattn_ref(_layernorm(x, axis=-1), ctx_2048, ctx_2048, L0_xattn_gamma)
    x = x + _L0_ffn_ref(_layernorm(x, axis=-1), L0_ffn_Wg, L0_ffn_w1, L0_ffn_w2)
    return x

_drawn_inputs = setup_inputs


def setup_inputs(seed=0):
    import zlib

    import numpy as np

    out = dict(_drawn_inputs(seed))
    spreads = {'L0_attn_b_in': (0.0, 0.772),
     'L0_attn_b_out': (0.0, 0.1),
     'L0_attn_gamma': (1.0, 0.6),
     'L0_attn_beta': (0.0, 0.8)}
    factors = {'L0_ffn_Wg': 4.296, 'L0_ffn_w1': 4.436, 'L0_ffn_w2': 3.687}
    for name, (base, spread) in spreads.items():
        noise = np.random.default_rng([zlib.crc32(name.encode()), seed]).standard_normal(out[name].shape)
        drawn = base * np.exp(spread * noise) if base else spread * noise
        out[name] = jnp.asarray(drawn.astype(out[name].dtype))
    for name, factor in factors.items():
        out[name] = (out[name] * factor).astype(out[name].dtype)
    return out
```

```python
import concourse.bass as bass
from concourse import mybir
from contextlib import ExitStack

P = 128
D = 256
HALVES = D // P
SEQ = 64
HEADS = 8
DH = SEQ // HEADS
PAIRS = HEADS
TERMS = 6
OPK = TERMS * DH
EPS = 1e-5
RING = 4
SKEW = 5
PROBS = 8
EXPERTS = 8
TOP_K = 2
D_FF = 1024
FF = D_FF // P
TOKEN_ID = D
GATES = D + 1
ROW = GATES + EXPERTS
Y_RING = 5
FAR = 1.0e6


class Tile:

    def __init__(self, it, c):
        self.it, self.c = it, c

    def __add__(self, n):
        return Tile(self.it, self.c + n)

    def exists(self, tiles):
        return self.it is not None or 0 <= self.c < tiles

    def number(self):
        return self.c if self.it is None else self.it * RING + self.c

    def count(self, per_tile, n):
        fixed = per_tile * self.c + n
        return fixed if self.it is None else self.it * (RING * per_tile) + fixed

    def loads(self, dmas):
        fixed = 16 * dmas * (self.c // 2 + 1)
        return fixed if self.it is None else self.it * (16 * dmas * RING // 2) + fixed


def run_steps(engine, tiles, skew, step):
    for s in range(2 * RING):
        step(Tile(None, s))
    with engine.Fori(2, tiles // RING - 1) as it:
        for c in range(RING):
            step(Tile(it, c))
    for s in range(tiles - RING, tiles + skew):
        step(Tile(None, s))


def decoder_block(nc, tiles, x, ctx_in, w_in, b_in, w_out, b_out, ln_gamma, ln_beta, xattn_gamma, wg, w1, w2,
                  consts, route_consts, out):
    F32, BF16 = mybir.dt.float32, mybir.dt.bfloat16
    ALU, ACT, AX = mybir.AluOpType, mybir.ActivationFunctionType, mybir.AxisListType

    x_tiles = x.rearrange("(t b) s d -> t (b s) d", b=2)
    ctx_tiles = ctx_in.rearrange("(t b) s d -> t (b s) d", b=2)
    out_tiles = out.rearrange("(t p) d -> t p d", p=P)
    w_in_v = w_in.rearrange("(c p) n -> p c n", p=P)
    w_out_v = w_out.rearrange("(c p) n -> p c n", p=P)
    half_rows = "(c p) -> p c"

    def dram(name, shape, dtype):
        return nc.dram_tensor(name, shape, dtype, kind="Internal").ap()

    q_terms = [dram(f"q_terms{i}", (P, TERMS, D), BF16) for i in range(2)]
    k_terms = [dram(f"k_terms{i}", (P, TERMS, D), BF16) for i in range(2)]
    attended = [dram(f"attended{i}", (2 * HEADS, DH + 1, D), F32) for i in range(2)]
    inverses = [dram(f"inverses{i}", (2 * HEADS, D), F32) for i in range(2)]

    ctx = ExitStack()
    with ctx:
        def sb(name, shape, dt=F32):
            return ctx.enter_context(nc.sbuf_tensor(name, shape, dt))

        def pb(name, shape, dt=F32):
            return ctx.enter_context(nc.psum_tensor(name, shape, dt))

        def sem(name):
            return ctx.enter_context(nc.semaphore(name))

        capacity = -(-5 * tiles * P * TOP_K // (4 * EXPERTS))
        blocks = capacity // P
        assert blocks * P == capacity and blocks % Y_RING == 0 and tiles % 8 == 0
        groups = [(b, min(4, blocks - b)) for b in range(0, blocks, 4)]
        n_slots = EXPERTS * capacity
        slots_dram = dram("slots_dram", (n_slots, ROW), F32)

        rows_all = sb("rows_all", [P, tiles, ROW])
        w1_sb = [sb(f"w1_sb{i}", [P, HALVES, D_FF]) for i in range(2)]
        w2_sb = [sb(f"w2_sb{i}", [P, FF, D]) for i in range(2)]
        route_sb = sb("route_sb", [P, P + EXPERTS * tiles + 2 * EXPERTS + tiles])
        earlier = route_sb[:, 0:P]
        not_first = route_sb[:, P:P + EXPERTS * tiles]
        expert_no = route_sb[:, P + EXPERTS * tiles:P + EXPERTS * (tiles + 1)]
        expert_base = route_sb[:, P + EXPERTS * (tiles + 1):P + EXPERTS * (tiles + 2)]
        token_no = route_sb[:, P + EXPERTS * (tiles + 2):P + EXPERTS * (tiles + 2) + tiles]
        ones = sb("ones", [P, P])
        wg_sb = sb("wg_sb", [P, HALVES, 32])
        ident_keep = sb("ident_keep", [P, P])
        empty_row = sb("empty_row", [P, ROW])

        phase1 = ctx.enter_context(ExitStack())

        def sb(name, shape, dt=F32):
            return phase1.enter_context(nc.sbuf_tensor(name, shape, dt))

        const_sb = sb("const_sb", [P, 128 + 256 + 256 + 2])
        ident = const_sb[:, 0:128]
        cos_kv = const_sb[:, 128:384].rearrange("p (a d) -> p a d", a=2)
        sin_kv = const_sb[:, 384:640].rearrange("p (a d) -> p a d", a=2)
        row_mask = const_sb[:, 640:642]
        ident_bf = sb("ident_bf", [P, P], BF16)
        w_in_raw = sb("w_in_raw", [P, HALVES, 3 * D])
        w_in_g = sb("w_in_g", [P, HALVES, 3 * D])
        w_out_sb = sb("w_out_sb", [P, HALVES, D])
        gamma_col = sb("gamma_col", [P, HALVES])
        beta_col = sb("beta_col", [P, HALVES])
        beta_wide = sb("beta_wide", [P, HALVES, P])
        bias_kv_raw = sb("bias_kv_raw", [P, 2 * D])
        bias_kv = sb("bias_kv", [P, 2 * D])
        bias_q_raw = sb("bias_q_raw", [P, HALVES])
        bias_q = sb("bias_q", [P, HALVES, 2])
        b_out_sb = sb("b_out_sb", [P, D])
        xgamma = sb("xgamma", [P, 1])
        minus_half = sb("minus_half", [P, 2])

        x_in = [sb(f"x_in{i}", [P, D]) for i in range(2)]
        c_in = [sb(f"c_in{i}", [P, D]) for i in range(2)]
        x_stats = [sb(f"x_stats{i}", [P, 6]) for i in range(2)]
        x_mv = [sb(f"x_mv{i}", [P, 2]) for i in range(2)]
        x_var = [sb(f"x_var{i}", [P, 2]) for i in range(2)]
        x_nmean = [sb(f"x_nmean{i}", [P, 1]) for i in range(2)]
        x_rstd = [sb(f"x_rstd{i}", [P, 2]) for i in range(2)]
        base_affine = [sb(f"base_affine{i}", [P, 2]) for i in range(2)]
        xn = [sb(f"xn{i}", [P, D]) for i in range(2)]
        base0 = [sb(f"base0{i}", [P, D]) for i in range(2)]
        base = [sb(f"base{i}", [P, D]) for i in range(2)]
        xnT = [sb(f"xnT{i}", [P, HALVES, P]) for i in range(2)]
        kv = [sb(f"kv{i}", [P, 2, D]) for i in range(2)]
        rot_cos = sb("rot_cos", [P, 2, P])
        rot_sin = sb("rot_sin", [P, 2, P])
        rot = [sb(f"rot{i}", [P, 2, P]) for i in range(2)]
        kv_prod = [sb(f"kv_prod{i}", [P, D]) for i in range(2)]
        squares = [sb(f"squares{i}", [P, 2, D]) for i in range(2)]
        norms2 = [sb(f"norms2{i}", [P, 2]) for i in range(2)]
        inv_norms = [sb(f"inv_norms{i}", [P, 2]) for i in range(2)]
        row_weight = [sb(f"row_weight{i}", [P, 2]) for i in range(2)]
        a_scale = [sb(f"a_scale{i}", [P, HALVES, 2]) for i in range(2)]
        a_bias = [sb(f"a_bias{i}", [P, HALVES, 2]) for i in range(2)]
        yT = [sb(f"yT{i}", [P, HALVES, P]) for i in range(2)]

        x1 = [sb(f"x1{i}", [P, D]) for i in range(RING)]
        q_stats = sb("q_stats", [P, 6])
        q_mv = sb("q_mv", [P, 2])
        q_var = [sb(f"q_var{i}", [P, 1]) for i in range(2)]
        q_nmean = [sb(f"q_nmean{i}", [P, 1]) for i in range(2)]
        q_rstd = [sb(f"q_rstd{i}", [P, 1]) for i in range(2)]
        q_full = [sb(f"q_full{i}", [P, D]) for i in range(2)]
        q_rest = [sb(f"q_rest{i}", [P, D]) for i in range(2)]
        q_parts = [sb(f"q_parts{i}", [P, 3, D], BF16) for i in range(2)]
        c_rest = [sb(f"c_rest{i}", [P, D]) for i in range(2)]
        c_parts = [sb(f"c_parts{i}", [P, 3, D], BF16) for i in range(2)]
        q_op = [sb(f"q_op{i}", [P, PAIRS, D], BF16) for i in range(2)]
        k_op = [sb(f"k_op{i}", [P, PAIRS, D], BF16) for i in range(2)]
        vT = [sb(f"vT{i}", [P, 2, 2 * HEADS, 32]) for i in range(RING)]
        neg_max = [sb(f"neg_max{i}", [P, 2, 4]) for i in range(2)]
        max_parts = [sb(f"max_parts{i}", [P, 2, 2, 4], BF16) for i in range(2)]
        max_rows = [sb(f"max_rows{i}", [16, P], BF16) for i in range(2)]
        probs = [sb(f"probs{i}", [P, 2, D]) for i in range(PROBS)]
        pv_sb = [sb(f"pv_sb{i}", [P, 4, D]) for i in range(2)]
        sums = [sb(f"sums{i}", [P, 32]) for i in range(2)]
        inv_sums = [sb(f"inv_sums{i}", [P, 32]) for i in range(2)]
        numer = [sb(f"numer{i}", [P, D]) for i in range(2)]
        inv_wide = [sb(f"inv_wide{i}", [P, D]) for i in range(2)]
        attn = [sb(f"attn{i}", [P, D]) for i in range(2)]
        x2 = [sb(f"x2{i}", [P, D]) for i in range(2)]
        m_stats = sb("m_stats", [P, 6])
        m_mv = sb("m_mv", [P, 2])
        m_var = [sb(f"m_var{i}", [P, 1]) for i in range(2)]
        m_nmean = [sb(f"m_nmean{i}", [P, 1]) for i in range(2)]
        m_rstd = [sb(f"m_rstd{i}", [P, 1]) for i in range(2)]

        scores = [pb(f"scores{i}", [P, 2, D]) for i in range(2)]
        scoresT = [pb(f"scoresT{i}", [P, 2, D]) for i in range(3)]
        pv_ps = pb("pv_ps", [P, 2, D])
        work = pb("work", [P, 2, D])
        work_a, work_b = work[:, 0, :], work[:, 1, :]
        turn_ps = pb("turn_ps", [P, 2, D])
        max_ps = turn_ps[:, 1, 0:64].bitcast(BF16)[0:16, 0:P]

        phase1.close()

        def sb(name, shape, dt=F32):
            return ctx.enter_context(nc.sbuf_tensor(name, shape, dt))

        mT = [sb(f"mT{i}", [P, HALVES, 2, P]) for i in range(2)]
        logitsT = sb("logitsT", [P, tiles // 8, 2, P])
        route = {n: sb(f"r_{n}", [P, tiles, EXPERTS]) for n in
                 ("logit", "miss", "key", "hot0", "rest", "hot1", "both", "prob", "pos", "slot", "t0", "t1", "p0", "p1",
                  "e0", "e1", "g0", "g1")}
        per_expert = {n: sb(f"x_{n}", [P, EXPERTS, tiles]) for n in ("total", "through", "before")}
        flat = {n: sb(f"f_{n}", [P, tiles]) for n in
                ("top0", "top1", "id0", "id1", "z", "rz", "pos0", "pos1", "slot0", "slot1", "full0", "full1", "x0", "x1",
                 "p0", "p1", "g0", "g1")}
        slot_no = [sb(f"slot_no{k}", [P, tiles], mybir.dt.int32) for k in range(TOP_K)]
        slots_in = [sb(f"slots_in{i}", [P, blocks, ROW]) for i in range(2)]
        xT = [sb(f"xT{i}", [P, HALVES, capacity]) for i in range(2)]
        hT = [sb(f"hT{i}", [P, FF, 4 * P]) for i in range(2)]
        y_id = [sb(f"y_id{i}", [P, blocks], mybir.dt.int32) for i in range(2)]
        y_gate = [sb(f"y_gate{i}", [P, blocks]) for i in range(2)]
        y = [sb(f"y{i}", [P, D]) for i in range(Y_RING)]
        banks = [b[:, :, :].rearrange("p a d -> p (a d)") for b in
                 (scores[0], scores[1], scoresT[0], scoresT[1], scoresT[2], pv_ps, work, turn_ps)]

        names = ["setup_in", "setup_dve", "setup_pe", "setup_pool", "x_bn", "x_mv_ok", "x_var_ok", "x_rstd_ok", "affine_ok",
                 "xn_ok", "base0_ok", "base_ok", "xnT_mm", "xnT_ok", "kv_mm", "kv_ok", "qT_mm",
                 "rot_cos_ok", "rot_sin_ok", "rot_ok", "kv_prod_ok", "norms_ok", "inv_norms_ok", "row_weight_ok",
                 "a_mm", "a_scale_ok", "a_bias_ok", "y_ok", "wo_mm", "x1_ok", "q_bn", "q_mv_ok", "q_var_ok",
                 "q_rstd_ok", "q_full_ok", "q_hi_ok", "q_rest_ok", "q_mid_ok", "q_parts_ok", "c_hi_ok", "c_rest_ok",
                 "c_mid_ok", "c_parts_ok", "cT_mm", "vT_ok", "scores_mm", "row_max_ok", "max_hi_ok", "max_mid_ok",
                 "max_mm", "max_rows_ok", "scoresT_mm", "probs_ok", "pv_mm", "pv_ok", "inv_sums_ok", "attn_ok",
                 "x2_ok", "m_bn", "m_mv_ok", "m_var_ok", "m_rstd_ok", "m_ok",
                 "phase1_pe", "phase1_act", "phase1_dve", "phase1_pool", "blank_ok", "blank_dma", "wg_dma",
                 "mT_mm", "mT_act", "mT_dve", "logitsT_mm", "logitsT_ok", "logit_mm", "route_dve", "prob_ok", "count_mm",
                 "slot_ok", "scatter_dma", "xT_mm", "xT_act", "xT_dve", "meta_ok", "h_mm", "h_act", "h_dve", "y_mm",
                 "y_act", "y_dve"]
        S = {n: sem(n) for n in names}
        pair_names = ["x_dma", "c_dma", "q_terms_dma", "k_terms_dma", "q_op_dma", "k_op_dma", "max_dma",
                      "attended_dma", "sums_dma", "inverses_dma", "back_dma", "x2_dma"]
        D2 = {n: [sem(f"{n}{i}") for i in range(2)] for n in pair_names}
        w_dma = [sem(f"w_dma{i}") for i in range(2)]
        slots_dma = [sem(f"slots_dma{i}") for i in range(2)]
        add_dma = [sem(f"add_dma{i}") for i in range(Y_RING)]

        block = ctx.enter_context(nc.Block())

        def c_stage(s, p):
            return (s + -3, p - 4) if p >= 4 else (s + -4, p + 4)

        def max_group(s, p):
            return (s + -3, p // 2 - 1) if p >= 2 else (s + -4, 3)

        SETUP_LOADS = 11
        before_exp, before_count = 7, 13
        xT_parts = [(b, min(2, blocks - b)) for b in range(0, blocks, 2)]
        y_chunks = [(b, min(2, first + size - b)) for first, size in groups for b in range(first, first + size, 2)]
        n_xT = [(len(xT_parts) + 1) // 2, len(xT_parts) // 2]
        n_h = len(groups) * FF // 2
        n_y = [sum(size for _, size in y_chunks[side::2]) for side in range(2)]
        y_uses = blocks // Y_RING

        def y_before(q):
            return sum(size for _, size in y_chunks[q % 2:q:2])

        def chunks_of(g):
            return [(q, first, size) for q, (first, size) in enumerate(y_chunks)
                    if groups[g][0] <= first < groups[g][0] + groups[g][1]]

        def hT_free(e, g):
            if g >= 2:
                return e * len(y_chunks) + (chunks_of(g - 2)[-1][0] + 1)
            before = max(i for i in range(len(groups)) if i % 2 == g % 2)
            return (e - 1) * len(y_chunks) + (chunks_of(before)[-1][0] + 1)

        def run_experts(engine, expert):
            for par in range(2):
                expert(0, par, par, True)
            with engine.Fori(1, EXPERTS // 2 - 1) as it:
                for par in range(2):
                    expert(it, it * 2 + par, par, True)
            for par in range(2):
                expert(EXPERTS // 2 - 1, EXPERTS - 2 + par, par, par == 0)

        def wait_past(engine, sem, value):
            if not isinstance(value, int) or value > 0:
                engine.wait_ge(sem, value)

        def wait_apart(engine, sem, value):
            if not isinstance(value, int):
                value = engine.to_reg(value)
                engine.wait_ge(S["setup_in"], 16 * SETUP_LOADS)
            engine.wait_ge(sem, value)

        def phase1_over(engine):
            engine.wait_ge(S["m_ok"], tiles)
            for last in (tiles - 2, tiles - 1):
                engine.wait_ge(D2["x2_dma"][last % 2], Tile(None, last).loads(1))

        @block.sync
        def _(sp):
            def need(name, t, per_tile=1, n=1):
                wait_apart(sp, S[name], t.count(per_tile, n))

            def landed(name, t, dmas):
                wait_apart(sp, D2[name][t.c % 2], t.loads(dmas))

            def put(name, t, dst, src):
                sp.dma_start(dst, src).then_inc(D2[name][t.c % 2], 16)

            for dst, src in ((const_sb[:, :], consts), (w_in_raw[:, :, :], w_in_v), (w_out_sb[:, :, :], w_out_v),
                             (gamma_col[:, :], ln_gamma.rearrange(half_rows, p=P)),
                             (beta_col[:, :], ln_beta.rearrange(half_rows, p=P)),
                             (bias_kv_raw[:, :], b_in[D:3 * D].partition_broadcast(P)),
                             (bias_q_raw[:, :], b_in[0:D].rearrange(half_rows, p=P)),
                             (b_out_sb[:, :], b_out.partition_broadcast(P)),
                             (xgamma[:, :], xattn_gamma.partition_broadcast(P)), (route_sb[:, :], route_consts),
                             (ident_keep[:, :], consts[:, 0:P])):
                with nc.allow_non_contiguous_dma(reason="vectors laid out over the partitions, once"):
                    sp.dma_start(dst, src).then_inc(S["setup_in"], 16)

            def write_terms(name, t, terms, parts, slots):
                for first, part, repeat in slots:
                    m = repeat if repeat > 0 else -repeat
                    src = parts[:, part:part + m, :] if repeat > 0 else \
                        parts[:, part:part + 1, :].broadcast_to([P, m, D])
                    put(name, t, terms[:, first:first + m, :], src)

            def max_rows_out(s, p):
                t, g = max_group(s, p)
                if t.exists(tiles):
                    need("max_rows_ok", t, 4, g + 1)
                    for j in range(2):
                        sp.dma_start(q_op[t.c % 2][64 * j + OPK:64 * j + OPK + 2, 2 * g:2 * g + 2, :],
                                     max_rows[g % 2][8 * j:8 * j + 8, :]).then_inc(D2["max_dma"][g % 2], 16)

            def load_inputs(u):
                if (u + -2).exists(tiles):
                    need("base0_ok", u + -2)
                    need("xn_ok", u + -2)
                    need("c_parts_ok", u + -2)
                    need("cT_mm", u + -2)
                put("x_dma", u, x_in[u.c % 2][:, :], x_tiles[u.number()])
                put("c_dma", u, c_in[u.c % 2][:, :], ctx_tiles[u.number()])

            load_inputs(Tile(None, 0))

            def load_weights(i, e):
                sp.dma_start(w1_sb[i][:, :, :], w1.rearrange("e (c p) f -> e p c f", p=P)[e]).then_inc(w_dma[i], 16)
                sp.dma_start(w2_sb[i][:, :, :], w2.rearrange("e (c p) n -> e p c n", p=P)[e]).then_inc(w_dma[i], 16)

            def step(s):
                t, v, w = s + -5, s + -2, s + -4
                if s.it is None and s.c < EXPERTS:
                    sp.wait_ge(S["blank_ok"], 1)
                    sp.dma_start(slots_dram[capacity * s.c:capacity * (s.c + 1), :].rearrange("(b p) n -> p b n", p=P),
                                 empty_row[:, :].rearrange("p (o n) -> p o n", o=1).broadcast_to([P, blocks, ROW])
                                 ).then_inc(S["blank_dma"], 16)
                    if s.c < 2:
                        load_weights(s.c, s.c)
                if s.it is None and s.c == 2:
                    with nc.allow_non_contiguous_dma(reason="the router's weights, once"):
                        sp.dma_start(wg_sb[:, :, 0:EXPERTS], wg.rearrange("(c p) n -> p c n", p=P)
                                     ).then_inc(S["wg_dma"], 16)
                max_rows_out(s, 0)
                if t.exists(tiles):
                    need("inv_sums_ok", t)
                    if (t + -2).exists(tiles):
                        landed("back_dma", t + -2, 2)
                    put("inverses_dma", t, inverses[t.c % 2].rearrange("h (c f) -> h c f", c=8),
                        inv_sums[t.c % 2][:, :])
                    landed("inverses_dma", t, 1)
                    if (t + -2).exists(tiles):
                        need("attn_ok", t + -2)
                    put("back_dma", t, numer[t.c % 2][:, :], attended[t.c % 2][:, 0:DH, :])
                    put("back_dma", t, inv_wide[t.c % 2][:, :],
                        inverses[t.c % 2].rearrange("h (o f) -> h o f", o=1).broadcast_to([2 * HEADS, DH, D]))
                if (s + 1).exists(tiles):
                    load_inputs(s + 1)
                max_rows_out(s, 2)
                if v.exists(tiles):
                    need("q_parts_ok", v)
                    if (v + -2).exists(tiles):
                        landed("q_op_dma", v + -2, 2)
                    write_terms("q_terms_dma", v, q_terms[v.c % 2], q_parts[v.c % 2],
                                ((0, 0, -3), (3, 1, -2), (5, 2, 1)))
                    if (v + -2).exists(tiles):
                        need("scoresT_mm", v + -2, 16, 16)
                    landed("k_terms_dma", v, 3)
                    for j in range(2):
                        put("k_op_dma", v, k_op[v.c % 2][64 * j:64 * j + OPK, :, :],
                            k_terms[v.c % 2][64 * j:64 * j + 64].rearrange("(h d) m f -> (d m) h f", d=DH))
                    landed("q_terms_dma", v, 3)
                    for j in range(2):
                        put("q_op_dma", v, q_op[v.c % 2][64 * j:64 * j + OPK, :, :],
                            q_terms[v.c % 2][64 * j:64 * j + 64].rearrange("(h d) m f -> (d m) h f", d=DH))
                max_rows_out(s, 4)
                if w.exists(tiles):
                    need("pv_ok", w, 2, 2)
                    if (w + -2).exists(tiles):
                        landed("back_dma", w + -2, 2)
                        landed("sums_dma", w + -2, 1)
                    for c in range(4):
                        dst = attended[w.c % 2].rearrange("(j g q) r f -> j g q r f", j=2, q=2)[c % 2, :, c // 2]
                        put("attended_dma", w, dst.rearrange("g r f -> r g f"),
                            pv_sb[w.c % 2][32 * c:32 * c + DH + 1, :, :])
                max_rows_out(s, 6)
                if w.exists(tiles):
                    landed("attended_dma", w, 4)
                    put("sums_dma", w, sums[w.c % 2][:, :],
                        attended[w.c % 2][:, DH, :].rearrange("h (c f) -> h c f", c=8))
                if s.exists(tiles):
                    need("c_parts_ok", s)
                    if (s + -2).exists(tiles):
                        landed("k_op_dma", s + -2, 2)
                    write_terms("k_terms_dma", s, k_terms[s.c % 2], c_parts[s.c % 2],
                                ((0, 0, 3), (3, 0, 2), (5, 0, 1)))
                if t.exists(tiles):
                    need("x2_ok", t)
                    put("x2_dma", t, out_tiles[t.number()], x2[t.c % 2][:, :])

            run_steps(sp, tiles, SKEW, step)
            for last in (tiles - 2, tiles - 1):
                landed("x2_dma", Tile(None, last), 1)

            def load_slots(i, e):
                sp.dma_start(slots_in[i][:, :, :],
                             slots_dram[bass.ds(e * capacity, capacity), :].rearrange("(b p) n -> p b n", p=P)
                             ).then_inc(slots_dma[i], 16)

            sp.wait_ge(S["scatter_dma"], 16 * TOP_K * tiles)
            load_slots(0, 0)

            def expert(k, e, par, more):
                if more:
                    wait_apart(sp, S["meta_ok"], e + 1)
                    wait_apart(sp, S["xT_mm"], (e + 1) * len(xT_parts))
                    load_slots(1 - par, e + 1)
                if not (isinstance(k, int) and k == EXPERTS // 2 - 1):
                    wait_apart(sp, S["y_mm"], (e + 1) * len(y_chunks))
                    load_weights(par, e + 2)

            run_experts(sp, expert)
            for r in range(Y_RING):
                sp.wait_ge(add_dma[r], 16 * y_uses * EXPERTS)

        @block.gpsimd
        def _(pool):
            def need(name, t, per_tile=1, n=1):
                pool.wait_ge(S[name], t.count(per_tile, n))

            def need_apart(name, t):
                wait_apart(pool, S[name], t.count(1, 1))

            def done(ins, name):
                ins.then_inc(S[name], 1)

            g = nc.gpsimd
            g.memset(minus_half[:, :], -0.5)
            for i in range(2):
                g.memset(k_op[i][:, :, :], 1.0)
            for i in range(RING):
                g.memset(vT[i][:, :, :, :], 1.0)
            g.memset(ones[:, :], 1.0)
            g.memset(wg_sb[:, :, :], 0.0)
            g.memset(empty_row[:, :], 0.0)
            done(g.memset(base_affine[0][:, :], 0.0), "setup_pool")
            pool.wait_ge(S["setup_pool"], 1)
            pool.wait_ge(S["setup_in"], 16 * SETUP_LOADS)
            done(g.memset(empty_row[:, TOKEN_ID:TOKEN_ID + 1], float(tiles * P)), "blank_ok")

            def split(t, full, rest, parts, pre):
                done(g.tensor_scalar(parts[:, 0, :], full[:, :], 1.0, 1.0, ALU.mult, ALU.mult), pre + "_hi_ok")
                need(pre + "_hi_ok", t)
                done(g.tensor_tensor(rest[:, :], full[:, :], parts[:, 0, :], ALU.subtract), pre + "_rest_ok")
                need_apart(pre + "_rest_ok", t)
                done(g.tensor_scalar(parts[:, 1, :], rest[:, :], 1.0, 1.0, ALU.mult, ALU.mult), pre + "_mid_ok")
                need(pre + "_mid_ok", t)
                done(g.tensor_tensor(parts[:, 2, :], rest[:, :], parts[:, 1, :], ALU.subtract), pre + "_parts_ok")

            def step(s):
                if s.exists(tiles):
                    i = s.c % 2
                    need("x_var_ok", s)
                    done(g.tensor_tensor(x_rstd[i][:, :], x_var[i][:, :], minus_half[:, :], ALU.pow), "x_rstd_ok")
                    need_apart("x_rstd_ok", s)
                    if (s + -2).exists(tiles):
                        need_apart("xnT_mm", s + -2)
                    done(g.tensor_scalar(xn[i][:, :], x_in[i][:, :], x_nmean[i][:, :], x_rstd[i][:, 1:2],
                                         ALU.add, ALU.mult), "xn_ok")
                v = s + -2
                if v.exists(tiles):
                    i = v.c % 2
                    need("q_var_ok", v)
                    done(g.tensor_tensor(q_rstd[i][:, :], q_var[i][:, :], minus_half[:, 0:1], ALU.pow), "q_rstd_ok")
                    need_apart("q_rstd_ok", v)
                    done(g.tensor_scalar(q_full[i][:, :], x1[v.c % RING][:, :], q_nmean[i][:, :], q_rstd[i][:, :],
                                         ALU.add, ALU.mult), "q_full_ok")
                    if (v + -2).exists(tiles):
                        wait_apart(pool, D2["q_terms_dma"][i], (v + -2).loads(3))
                    need_apart("q_full_ok", v)
                    split(v, q_full[i], q_rest[i], q_parts[i], "q")
                u = s + -1
                if u.exists(tiles):
                    i = u.c % 2
                    need("kv_ok", u)
                    turned = kv[i][:, :, 0:P].rearrange("p a (n e) -> p a n e", e=2)
                    sines = sin_kv.rearrange("p a (n e) -> p a n e", e=2)
                    target = rot_sin[:, :, :].rearrange("p a (n e) -> p a n e", e=2)
                    if (u + -1).exists(tiles):
                        need("rot_ok", u + -1)
                    done(g.tensor_tensor(rot_cos[:, :, :], kv[i][:, :, 0:P], cos_kv, ALU.mult), "rot_cos_ok")
                    for e in range(2):
                        last = g.tensor_tensor(target[:, :, :, e], turned[:, :, :, 1 - e], sines[:, :, :, e], ALU.mult)
                    done(last, "rot_sin_ok")
                    if (u + -2).exists(tiles):
                        need("a_mm", u + -2)
                    g.tensor_tensor(kv_prod[i][:, P:D], kv[i][:, 0, P:D], kv[i][:, 1, P:D], ALU.mult)
                    need("rot_cos_ok", u)
                    need("rot_sin_ok", u)
                    done(g.tensor_tensor(rot[i][:, :, :], rot_cos[:, :, :], rot_sin[:, :, :], ALU.add), "rot_ok")
                    need("norms_ok", u)
                    done(g.tensor_tensor(inv_norms[i][:, :], norms2[i][:, :], minus_half[:, :], ALU.pow), "inv_norms_ok")
                    need("rot_ok", u)
                    done(g.tensor_tensor(kv_prod[i][:, 0:P], rot[i][:, 0, :], rot[i][:, 1, :], ALU.mult), "kv_prod_ok")
                    need_apart("inv_norms_ok", u)
                    done(g.tensor_scalar(row_weight[i][:, :], row_mask, inv_norms[i][:, 0:1], inv_norms[i][:, 1:2],
                                         ALU.mult, ALU.mult), "row_weight_ok")
                t = s + -5
                if t.exists(tiles):
                    i = t.c % 2
                    pool.wait_ge(D2["back_dma"][i], t.loads(2))
                    if (t + -2).exists(tiles):
                        need("x2_ok", t + -2)
                    done(g.tensor_tensor(attn[i][:, :], numer[i][:, :], inv_wide[i][:, :], ALU.mult), "attn_ok")
                if s.exists(tiles):
                    i = s.c % 2
                    g.tensor_scalar(base_affine[i][:, 0:1], x_rstd[i][:, 0:1], 1.0, 1.0, ALU.mult, ALU.add)
                    done(g.tensor_tensor(base_affine[i][:, 1:2], x_rstd[i][:, 0:1], x_nmean[i][:, :], ALU.mult),
                         "affine_ok")
                    wait_apart(pool, D2["c_dma"][i], s.loads(1))
                    if (s + -2).exists(tiles):
                        need_apart("x1_ok", s + -2)
                        wait_apart(pool, D2["k_terms_dma"][i], (s + -2).loads(3))
                    need_apart("affine_ok", s)
                    done(g.tensor_scalar(base0[i][:, :], x_in[i][:, :], base_affine[i][:, 0:1],
                                         base_affine[i][:, 1:2], ALU.mult, ALU.add), "base0_ok")
                    split(s, c_in[i], c_rest[i], c_parts[i], "c")
                    need("base0_ok", s)
                    done(g.tensor_tensor(base[i][:, :], base0[i][:, :], b_out_sb[:, :], ALU.add), "base_ok")
                if t.exists(tiles):
                    i = t.c % 2
                    need("m_var_ok", t)
                    done(g.tensor_tensor(m_rstd[i][:, :], m_var[i][:, :], minus_half[:, 0:1], ALU.pow), "m_rstd_ok")

            run_steps(pool, tiles, SKEW, step)

            pool.wait_ge(S["blank_dma"], 16 * EXPERTS)
            pool.wait_ge(S["slot_ok"], 1)
            for k in range(TOP_K):
                for t in range(tiles):
                    g.indirect_dma_start(
                        out=slots_dram[:, :], out_offset=bass.IndirectOffsetOnAxis(ap=slot_no[k][:, t:t + 1], axis=0),
                        in_=rows_all[:, t, :], in_offset=None, bounds_check=n_slots - 1, oob_is_err=False
                    ).then_inc(S["scatter_dma"], 16)
            for last in (tiles - 2, tiles - 1):
                pool.wait_ge(D2["x2_dma"][last % 2], Tile(None, last).loads(1))

            def expert(k, e, par, more):
                for r in range(Y_RING):
                    wait_past(pool, add_dma[r], e * (16 * y_uses))
                pool.wait_ge(S["meta_ok"], e + 1)
                for q, (first, size) in enumerate(y_chunks):
                    for b in range(size):
                        n = first + b
                        wait_apart(pool, S[("y_act", "y_dve")[q % 2]], e * n_y[q % 2] + (y_before(q) + b + 1))
                        g.indirect_dma_start(
                            out=out[:, :], out_offset=bass.IndirectOffsetOnAxis(ap=y_id[par][:, n:n + 1], axis=0),
                            in_=y[n % Y_RING][:, :], in_offset=None, bounds_check=tiles * P - 1, oob_is_err=False,
                            compute_op=ALU.add).then_inc(add_dma[n % Y_RING], 16)

            run_experts(pool, expert)

        @block.scalar
        def _(act):
            def need(name, t, per_tile=1, n=1):
                act.wait_ge(S[name], t.count(per_tile, n))

            def done(ins, name):
                ins.then_inc(S[name], 1)

            a = nc.scalar

            act.wait_ge(S["setup_pool"], 1)

            def step(s):
                for p in range(PAIRS):
                    t, pc = c_stage(s, p)
                    if t.exists(tiles):
                        for j in range(2):
                            n = 2 * pc + j
                            if t.it is not None or 16 * t.c + n >= PROBS:
                                before, m = (t, n - PROBS) if n >= PROBS else (t + -1, n - PROBS + 16)
                                need("pv_mm", before, 4, m // 4 + 1)
                            need("scoresT_mm", t, 16, n + 1)
                            done(a.activation(probs[n % PROBS][:, :, :], scoresT[n % 3][:, :, :], ACT.Exp), "probs_ok")
                    w = s + -4
                    if p in (1, 5) and w.exists(tiles):
                        h = p // 4
                        need("pv_mm", w, 4, 2 * h + 2)
                        if (w + -2).exists(tiles):
                            act.wait_ge(D2["attended_dma"][w.c % 2], (w + -2).loads(4))
                        done(a.copy(pv_sb[w.c % 2][:, 2 * h:2 * h + 2, :], pv_ps[:, :, :]), "pv_ok")
                    if p == 2 and s.exists(tiles):
                        need("xnT_mm", s)
                        if (s + -2).exists(tiles):
                            need("qT_mm", s + -2)
                        done(a.copy(xnT[s.c % 2][:, :, :], work_a.rearrange("p (h t) -> p h t", h=HALVES)), "xnT_ok")
                    if p == 4 and s.exists(tiles):
                        i = s.c % 2
                        need("kv_ok", s)
                        if (s + -2).exists(tiles):
                            need("inv_norms_ok", s + -2)
                        a.activation(squares[i][:, 0, :], kv[i][:, 0, :], ACT.Square, accum_out=norms2[i][:, 0:1])
                        done(a.activation(squares[i][:, 1, :], kv[i][:, 1, :], ACT.Square,
                                          accum_out=norms2[i][:, 1:2]), "norms_ok")
                    if p == 5 and s.exists(tiles):
                        need("cT_mm", s)
                        if (s + -4).exists(tiles):
                            need("pv_mm", s + -4, 4, 4)
                        done(a.copy(vT[s.c % RING][:, :, :, 0:DH],
                                    turn_ps[:, 0, :].rearrange("p (l h d) -> p l h d", l=2, d=DH)), "vT_ok")
                    v = s + -1
                    if p == 6 and v.exists(tiles):
                        i = v.c % 2
                        need("qT_mm", v)
                        need("a_bias_ok", v)
                        if (v + -2).exists(tiles):
                            need("wo_mm", v + -2)
                        for h in range(HALVES):
                            for b in range(2):
                                last = a.activation(yT[i][:, h, SEQ * b:SEQ * (b + 1)],
                                                    work_a[:, P * h + SEQ * b:P * h + SEQ * (b + 1)], ACT.Identity,
                                                    bias=a_bias[i][:, h, b:b + 1], scale=a_scale[i][:, h, b:b + 1])
                        done(last, "y_ok")

            run_steps(act, tiles, SKEW, step)

            phase1_over(act)
            for n in range(0, tiles // 2, 2):
                act.wait_ge(S["mT_mm"], n + 1)
                if n >= 2:
                    act.wait_ge(S["logitsT_mm"], n - 1)
                done(a.copy(mT[0][:, :, :, :].rearrange("p h b t -> p (h b t)"), banks[0]), "mT_act")
            act.wait_ge(S["logitsT_mm"], tiles // 2)
            for half in range(tiles // 16):
                done(a.copy(logitsT[:, :, :, :].rearrange("p s b t -> p (s b t)")[:, 512 * half:512 * (half + 1)],
                            banks[2 + half]), "logitsT_ok")
            act.wait_ge(S["route_dve"], before_exp)
            done(a.activation(route["prob"][:, :, :], route["p0"][:, :, :], ACT.Exp), "prob_ok")

            def turn(e, par):
                for n in range(0, len(xT_parts), 2):
                    first, size = xT_parts[n]
                    act.wait_ge(S["xT_mm"], e * len(xT_parts) + (n + 1))
                    done(a.copy(xT[par][:, :, P * first:P * (first + size)],
                                banks[6][:, 0:HALVES * P * size].rearrange("p (h t) -> p h t", h=HALVES)), "xT_act")

            def hidden(e, par, g):
                first, size = groups[g]
                for f in range(0, FF, 2):
                    m = g * FF + f
                    act.wait_ge(S["h_mm"], e * (len(groups) * FF) + (m + 1))
                    if f == 0:
                        wait_past(act, S["y_mm"], hT_free(e, g))
                    done(a.activation(hT[g % 2][:, f, 0:P * size], banks[m % 4][:, 0:P * size], ACT.Relu), "h_act")

            def outputs(e, par, g):
                for q, first, size in chunks_of(g):
                    if q % 2 == 0:
                        act.wait_ge(S["y_mm"], e * len(y_chunks) + (q + 1))
                        act.wait_ge(S["meta_ok"], e + 1)
                        for b in range(size):
                            n = first + b
                            wait_past(act, add_dma[n % Y_RING], e * (16 * y_uses) + 16 * (n // Y_RING))
                            done(a.activation(y[n % Y_RING][:, :], banks[4][:, D * b:D * (b + 1)], ACT.Copy,
                                              scale=y_gate[par][:, n:n + 1]), "y_act")

            def expert(k, e, par, more):
                hidden(e, par, 0)
                for g in range(1, len(groups)):
                    hidden(e, par, g)
                    outputs(e, par, g - 1)
                    if g == 1 and more:
                        turn(e + 1, 1 - par)
                outputs(e, par, len(groups) - 1)

            turn(0, 0)
            run_experts(act, expert)

        @block.vector
        def _(dve):
            def need(name, t, per_tile=1, n=1):
                dve.wait_ge(S[name], t.count(per_tile, n))

            def done(ins, name):
                ins.then_inc(S[name], 1)

            v = nc.vector

            dve.wait_ge(S["setup_in"], 16 * SETUP_LOADS)
            v.tensor_copy(ident_bf[:, :], ident)
            for h in range(HALVES):
                v.tensor_scalar(w_in_g[:, h, :], w_in_raw[:, h, :], gamma_col[:, h:h + 1], None, ALU.mult)
                last = v.tensor_copy(beta_wide[:, h, :], beta_col[:, h:h + 1].broadcast_to([P, P]))
            done(last, "setup_dve")
            dve.wait_ge(S["setup_pe"], 1)
            v.tensor_tensor(bias_kv[:, :], scores[0][:, :, :].rearrange("p a d -> p (a d)"), bias_kv_raw[:, :], ALU.add)
            for b in range(2):
                last = v.tensor_tensor(bias_q[:, :, b], scores[1][:, 0, 0:HALVES], bias_q_raw[:, :], ALU.add)
            done(last, "setup_dve")
            dve.wait_ge(S["setup_dve"], 2)

            def stats(t, src, ok, pre, s_t, m_t):
                need(ok, t)
                done(v.bn_stats(s_t[:, :], src), pre + "_bn")
                wait_apart(dve, S[pre + "_bn"], t.count(1, 1))
                done(v.bn_aggr(m_t[:, :], s_t[:, :]), pre + "_mv_ok")
                need(pre + "_mv_ok", t)

            def reduce_head(t, p, j):
                n = 2 * p + j + 1
                q = (p // 2) % 2
                need("scores_mm", t, 16, n)
                done(v.tensor_reduce(neg_max[q][:, j, 2 * (p % 2):2 * (p % 2) + 2], scores[j][:, :, :], AX.X, ALU.max,
                                     negate=True), "row_max_ok")

            def step(s):
                B = s + -3
                for p in range(PAIRS):
                    if p == 0 and (s + -2).exists(tiles):
                        t = s + -2
                        i = t.c % 2
                        need("wo_mm", t)
                        need("base_ok", t)
                        done(v.tensor_tensor(x1[t.c % RING][:, :], work_a, base[i][:, :], ALU.add), "x1_ok")
                        stats(t, x1[t.c % RING][:, :], "x1_ok", "q", q_stats, q_mv)
                        if (t + -2).exists(tiles):
                            need("q_full_ok", t + -2)
                        v.tensor_scalar(q_var[i][:, :], q_mv[:, 1:2], float(DH), DH * EPS, ALU.mult, ALU.add)
                        done(v.tensor_scalar(q_nmean[i][:, :], q_mv[:, 0:1], -1.0, None, ALU.mult), "q_var_ok")
                    if p == 0 and s.exists(tiles):
                        i = s.c % 2
                        dve.wait_ge(D2["x_dma"][i], s.loads(1))
                        if (s + -2).exists(tiles):
                            need("affine_ok", s + -2)
                            need("xn_ok", s + -2)
                        done(v.bn_stats(x_stats[i][:, :], x_in[i][:, :]), "x_bn")
                        wait_apart(dve, S["x_bn"], s.count(1, 1))
                        done(v.bn_aggr(x_mv[i][:, :], x_stats[i][:, :]), "x_mv_ok")
                        need("x_mv_ok", s)
                        v.tensor_scalar(x_var[i][:, 0:1], x_mv[i][:, 1:2], 1.0, EPS, ALU.mult, ALU.add)
                        v.tensor_scalar(x_var[i][:, 1:2], x_mv[i][:, 1:2], 1.0 + EPS, EPS * EPS, ALU.mult, ALU.add)
                        done(v.tensor_scalar(x_nmean[i][:, :], x_mv[i][:, 0:1], -1.0, None, ALU.mult), "x_var_ok")
                    if p == 6 and (s + -1).exists(tiles):
                        t = s + -1
                        i = t.c % 2
                        need("a_mm", t)
                        if (t + -2).exists(tiles):
                            need("y_ok", t + -2)
                        done(v.tensor_scalar(a_scale[i][:, :, :], work_b[:, 0:4].rearrange("p (h b) -> p h b", h=HALVES),
                                             0.5, 0.5, ALU.mult, ALU.add), "a_scale_ok")
                        need("a_scale_ok", t)
                        done(v.tensor_tensor(a_bias[i][:, :, :], a_scale[i][:, :, :], bias_q[:, :, :], ALU.mult),
                             "a_bias_ok")
                    if p == 4 and s.exists(tiles):
                        i = s.c % 2
                        if (s + -2).exists(tiles):
                            need("kv_prod_ok", s + -2)
                            need("norms_ok", s + -2)
                        need("kv_mm", s)
                        done(v.tensor_tensor(kv[i][:, :, :], work[:, :, :], bias_kv[:, :].rearrange(
                            "p (a d) -> p a d", a=2), ALU.add), "kv_ok")
                    if p % 2 == 0:
                        t, g = max_group(s, p)
                        if t.exists(tiles):
                            need("max_mm", t, 4, g + 1)
                            if t.it is not None or 4 * t.c + g >= 2:
                                before, gb = (t, g - 2) if g >= 2 else (t + -1, g + 2)
                                dve.wait_ge(D2["max_dma"][g % 2], before.count(64, 32 * (gb // 2 + 1)))
                            done(v.tensor_copy(max_rows[g % 2][:, :], max_ps), "max_rows_ok")
                    if B.exists(tiles):
                        reduce_head(B, p, 0)
                        reduce_head(B, p, 1)
                        if p % 2:
                            g = p // 2
                            need("row_max_ok", B, 16, 2 * p + 2)
                            if B.it is not None or 4 * B.c + g >= 2:
                                before, gb = (B, g - 2) if g >= 2 else (B + -1, g + 2)
                                need("max_mm", before, 4, gb + 1)
                            done(v.tensor_copy(max_parts[g % 2][:, :, 0, :], neg_max[g % 2][:, :, :]), "max_hi_ok")
                            need("max_hi_ok", B, 4, g + 1)
                            done(v.tensor_tensor(max_parts[g % 2][:, :, 1, :], neg_max[g % 2][:, :, :],
                                                 max_parts[g % 2][:, :, 0, :], ALU.subtract), "max_mid_ok")
                    if p == 4 and (s + -5).exists(tiles):
                        t = s + -5
                        i = t.c % 2
                        need("attn_ok", t)
                        if (t + -2).exists(tiles):
                            dve.wait_ge(D2["x2_dma"][i], (t + -2).loads(1))
                        done(v.scalar_tensor_tensor(x2[i][:, :], attn[i][:, :], xgamma[:, :], x1[t.c % RING][:, :],
                                                    ALU.mult, ALU.add), "x2_ok")
                        stats(t, x2[i][:, :], "x2_ok", "m", m_stats, m_mv)
                        v.tensor_scalar(m_var[i][:, :], m_mv[:, 1:2], 1.0, EPS, ALU.mult, ALU.add)
                        done(v.tensor_scalar(m_nmean[i][:, :], m_mv[:, 0:1], -1.0, None, ALU.mult), "m_var_ok")
                    if p == 7:
                        t = s + -5
                        if t.exists(tiles):
                            need("m_rstd_ok", t)
                            done(v.tensor_scalar(rows_all[:, t.number(), 0:D], x2[t.c % 2][:, :], m_nmean[t.c % 2][:, :],
                                                 m_rstd[t.c % 2][:, :], ALU.add, ALU.mult), "m_ok")
                        t = s + -4
                        if t.exists(tiles):
                            i = t.c % 2
                            dve.wait_ge(D2["sums_dma"][i], t.loads(1))
                            if (t + -2).exists(tiles):
                                dve.wait_ge(D2["inverses_dma"][i], (t + -2).loads(1))
                            done(v.reciprocal(inv_sums[i][:, :], sums[i][:, :]), "inv_sums_ok")

            run_steps(dve, tiles, SKEW, step)

            phase1_over(dve)
            for n in range(1, tiles // 2, 2):
                dve.wait_ge(S["mT_mm"], n + 1)
                if n >= 2:
                    dve.wait_ge(S["logitsT_mm"], n - 1)
                done(v.tensor_copy(mT[1][:, :, :, :].rearrange("p h b t -> p (h b t)"), banks[1]), "mT_dve")

            links = [0]

            def link(ins):
                links[0] += 1
                ins.then_inc(S["route_dve"], 1)
                dve.wait_ge(S["route_dve"], links[0])

            def wide(name):
                return flat[name][:, :].rearrange("p (t o) -> p t o", o=1).broadcast_to([P, tiles, EXPERTS])

            def per_token(row):
                return row.rearrange("p (o e) -> p o e", o=1).broadcast_to([P, tiles, EXPERTS])

            r = {n: route[n][:, :, :] for n in route}
            v.tensor_copy(rows_all[:, :, TOKEN_ID], token_no)
            dve.wait_ge(S["logit_mm"], 1)
            for slot in range(tiles // 8):
                ps = banks[4 + slot // 2][:, D * (slot % 2):D * (slot % 2 + 1)].rearrange("p (b c e) -> p b c e", b=2, c=4)
                last = v.tensor_copy(route["logit"][:, 8 * slot:8 * slot + 8, :].rearrange("p (c b) e -> p b c e", b=2),
                                     ps[:, :, :, 0:EXPERTS])
            link(last)
            for k, (src, hot) in enumerate((("logit", "hot0"), ("rest", "hot1"))):
                link(v.tensor_reduce(flat[f"top{k}"][:, :], r[src], AX.X, ALU.max))
                link(v.tensor_tensor(r["t0"], r[src], wide(f"top{k}"), ALU.is_equal))
                link(v.scalar_tensor_tensor(r["key"], r["t0"], -100.0, per_token(expert_no), ALU.mult, ALU.add))
                link(v.tensor_reduce(flat[f"id{k}"][:, :], r["key"], AX.X, ALU.min))
                link(v.tensor_tensor(r[hot], r["key"], wide(f"id{k}"), ALU.is_equal))
                if k == 0:
                    v.tensor_tensor(r["p0"], r["logit"], wide("top0"), ALU.subtract)
                    link(v.scalar_tensor_tensor(r["rest"], r["hot0"], -3.0e38, r["logit"], ALU.mult, ALU.add))
            link(v.tensor_tensor(r["both"], r["hot0"], r["hot1"], ALU.add))
            assert links[0] == before_count
            dve.wait_ge(S["prob_ok"], 1)
            v.tensor_reduce(flat["z"][:, :], r["prob"], AX.X, ALU.add)
            link(v.tensor_tensor(r["g0"], r["both"], r["prob"], ALU.mult))
            link(v.reciprocal(flat["rz"][:, :], flat["z"][:, :]))
            v.tensor_tensor(rows_all[:, :, GATES:ROW], r["g0"], wide("rz"), ALU.mult)
            dve.wait_ge(S["count_mm"], 1)
            link(v.tensor_copy(per_expert["total"][:, :, :],
                               banks[1][:, 0:EXPERTS * tiles].rearrange("p (t e) -> p e t", e=EXPERTS)))
            link(v.tensor_tensor_scan(per_expert["through"][:, :, :].rearrange("p e t -> p (e t)"), not_first,
                                      per_expert["total"][:, :, :].rearrange("p e t -> p (e t)"), 0.0,
                                      ALU.mult, ALU.add))
            link(v.tensor_tensor(per_expert["before"][:, :, :], per_expert["through"][:, :, :],
                                 per_expert["total"][:, :, :], ALU.subtract))
            link(v.tensor_tensor(r["pos"], banks[0][:, 0:EXPERTS * tiles].rearrange("p (t e) -> p t e", e=EXPERTS),
                                 per_expert["before"][:, :, :].rearrange("p e t -> p t e"), ALU.add))
            v.tensor_tensor(r["slot"], r["pos"], per_token(expert_base), ALU.add)
            link(v.tensor_scalar(r["e0"], r["pos"], float(capacity), FAR, ALU.is_ge, ALU.mult))
            link(v.tensor_tensor(r["e1"], r["e0"], r["slot"], ALU.add))
            v.tensor_tensor(r["t0"], r["hot0"], r["e1"], ALU.mult)
            link(v.tensor_tensor(r["t1"], r["hot1"], r["e1"], ALU.mult))
            for k in range(TOP_K):
                last = v.tensor_reduce(flat[f"slot{k}"][:, :], r[f"t{k}"], AX.X, ALU.add)
            link(last)
            for k in range(TOP_K):
                last = v.tensor_copy(slot_no[k][:, :], flat[f"slot{k}"][:, :])
            done(last, "slot_ok")

            def turn(k, e, par):
                dve.wait_ge(slots_dma[par], 16 * k + 16)
                for i in range(Y_RING):
                    wait_past(dve, add_dma[i], (e - 1) * (16 * y_uses))
                wait_past(dve, S["y_act"], (e - 1) * n_y[0])
                v.tensor_copy(y_id[par][:, :], slots_in[par][:, :, TOKEN_ID])
                done(v.tensor_copy(y_gate[par][:, :], slots_in[par][:, :, bass.ds(GATES + e, 1)].rearrange(
                    "p n o -> p (n o)")), "meta_ok")
                for n in range(1, len(xT_parts), 2):
                    first, size = xT_parts[n]
                    dve.wait_ge(S["xT_mm"], e * len(xT_parts) + (n + 1))
                    done(v.tensor_copy(xT[par][:, :, P * first:P * (first + size)],
                                       banks[7][:, 0:HALVES * P * size].rearrange("p (h t) -> p h t", h=HALVES)), "xT_dve")

            def hidden(e, par, g):
                first, size = groups[g]
                for f in range(1, FF, 2):
                    m = g * FF + f
                    dve.wait_ge(S["h_mm"], e * (len(groups) * FF) + (m + 1))
                    if f == 1:
                        wait_past(dve, S["y_mm"], hT_free(e, g))
                    done(v.tensor_scalar(hT[g % 2][:, f, 0:P * size], banks[m % 4][:, 0:P * size], 0.0, None, ALU.max),
                         "h_dve")

            def outputs(e, par, g):
                for q, first, size in chunks_of(g):
                    if q % 2:
                        dve.wait_ge(S["y_mm"], e * len(y_chunks) + (q + 1))
                        dve.wait_ge(S["meta_ok"], e + 1)
                        for b in range(size):
                            n = first + b
                            wait_past(dve, add_dma[n % Y_RING], e * (16 * y_uses) + 16 * (n // Y_RING))
                            done(v.tensor_scalar(y[n % Y_RING][:, :], banks[5][:, D * b:D * (b + 1)],
                                                 y_gate[par][:, n:n + 1], None, ALU.mult), "y_dve")

            def expert(k, e, par, more):
                hidden(e, par, 0)
                for g in range(1, len(groups)):
                    hidden(e, par, g)
                    outputs(e, par, g - 1)
                    if g == 1 and more:
                        turn(k + par, e + 1, 1 - par)
                outputs(e, par, len(groups) - 1)

            turn(0, 0, 0)
            run_experts(dve, expert)

        @block.tensor
        def _(pe):
            def need(name, t, per_tile=1, n=1):
                pe.wait_ge(S[name], t.count(per_tile, n))

            def done(ins, name):
                ins.then_inc(S[name], 1)

            mm = nc.tensor.matmul

            pe.wait_ge(S["setup_dve"], 1)
            for h in range(HALVES):
                mm(scores[0][:, :, :].rearrange("p a d -> p (a d)"), beta_wide[:, h, :], w_in_raw[:, h, D:3 * D],
                   start=h == 0, stop=h == HALVES - 1)
            for o in range(HALVES):
                for h in range(HALVES):
                    last = mm(scores[1][:, 0, o:o + 1], w_in_raw[:, h, P * o:P * (o + 1)], beta_col[:, h:h + 1],
                              start=h == 0, stop=h == HALVES - 1)
            done(last, "setup_pe")
            pe.wait_ge(S["setup_pool"], 1)
            pe.wait_ge(S["setup_dve"], 2)

            def step(s):
                B = s + -3
                for p in range(PAIRS):
                    if p % 2 == 0:
                        t, g = max_group(s, p)
                        if t.exists(tiles):
                            need("max_mid_ok", t, 4, g + 1)
                            if t.it is not None or 4 * t.c + g >= 1:
                                before, gb = (t, g - 1) if g else (t + -1, 3)
                                need("max_rows_ok", before, 4, gb + 1)
                            if p == 6 and s.exists(tiles):
                                need("vT_ok", s)
                            done(nc.tensor.transpose(max_ps, max_parts[g % 2][:, :, :, :].rearrange(
                                "p j m q -> p (j m q)"), ident_bf[:, :]), "max_mm")
                    if B.exists(tiles):
                        if p == 0:
                            pe.wait_ge(D2["q_op_dma"][B.c % 2], B.loads(2))
                            pe.wait_ge(D2["k_op_dma"][B.c % 2], B.loads(2))
                        q_t, k_t = q_op[B.c % 2], k_op[B.c % 2]
                        for j in range(2):
                            if B.it is not None or B.c > 0 or p > 0:
                                need("row_max_ok", B, 16, 2 * p + j - 1)
                            rows = slice(64 * j, 64 * j + OPK)
                            for h in range(2):
                                last = mm(scores[j][:, h, :], q_t[rows, p, P * h:P * (h + 1)], k_t[rows, p, :],
                                          start=True, stop=True)
                            done(last, "scores_mm")
                    t, pc = c_stage(s, p)
                    if t.exists(tiles):
                        q_t, k_t = q_op[t.c % 2], k_op[t.c % 2]
                        if pc % 2 == 0:
                            g = pc // 2
                            pe.wait_ge(D2["max_dma"][g % 2], t.count(64, 32 * (g // 2 + 1)))
                        for j in range(2):
                            n = 2 * pc + j
                            if n >= 3:
                                need("probs_ok", t, 16, n - 2)
                            elif (t + -1).exists(tiles):
                                need("probs_ok", t + -1, 16, (16, 14, 15)[n])
                            rows = slice(64 * j, 64 * j + OPK + 2)
                            for h in range(2):
                                last = mm(scoresT[n % 3][:, h, :], k_t[rows, pc, P * h:P * (h + 1)],
                                          q_t[rows, pc, :], start=True, stop=True)
                            done(last, "scoresT_mm")
                    if p == 2 and s.exists(tiles):
                        i = s.c % 2
                        need("xn_ok", s)
                        if (s + -2).exists(tiles):
                            need("x1_ok", s + -2)
                        for h in range(HALVES):
                            last = nc.tensor.transpose(work_a[:, P * h:P * (h + 1)], xn[i][:, P * h:P * (h + 1)], ident)
                        done(last, "xnT_mm")
                    if p == 3 and s.exists(tiles):
                        i = s.c % 2
                        need("xnT_ok", s)
                        for h in range(HALVES):
                            last = mm(work[:, :, :].rearrange("p a d -> p (a d)"), xnT[i][:, h, :],
                                      w_in_g[:, h, D:3 * D], start=h == 0, stop=h == 1)
                        done(last, "kv_mm")
                    if p == 5 and s.exists(tiles):
                        i = s.c % 2
                        pe.wait_ge(D2["c_dma"][i], s.loads(1))
                        if B.exists(tiles):
                            need("max_rows_ok", B, 4, 2)
                        for h in range(HALVES):
                            last = nc.tensor.transpose(turn_ps[:, 0, P * h:P * (h + 1)], c_in[i][:, P * h:P * (h + 1)],
                                                       ident)
                        done(last, "cT_mm")
                    v = s + -1
                    if p == 5 and v.exists(tiles):
                        i = v.c % 2
                        if s.exists(tiles):
                            need("kv_ok", s)
                        for o in range(HALVES):
                            for h in range(HALVES):
                                last = mm(work_a[:, P * o:P * (o + 1)], w_in_g[:, h, P * o:P * (o + 1)], xnT[i][:, h, :],
                                          start=h == 0, stop=h == 1)
                        done(last, "qT_mm")
                        need("kv_prod_ok", v)
                        need("row_weight_ok", v)
                        for h in range(HALVES):
                            last = mm(work_b[:, 2 * h:2 * h + 2], kv_prod[i][:, P * h:P * (h + 1)], row_weight[i][:, :],
                                      start=True, stop=True)
                        done(last, "a_mm")
                    if p == 7 and v.exists(tiles):
                        i = v.c % 2
                        need("y_ok", v)
                        for h in range(HALVES):
                            last = mm(work_a, yT[i][:, h, :], w_out_sb[:, h, :], start=h == 0, stop=h == 1)
                        done(last, "wo_mm")
                    if p % 2 == 0:
                        t, pc = c_stage(s, p)
                        t, g = (t, pc // 2 - 1) if pc >= 2 else (t + -1, 3)
                        if t.exists(tiles):
                            need("probs_ok", t, 16, 4 * g + 4)
                            need("vT_ok", t)
                            if g % 2 == 0 and (t.it is not None or 2 * t.c + g // 2 >= 1):
                                need("pv_ok", t, 2, g // 2)
                            for h in range(2):
                                for c in range(4):
                                    j, pair = c % 2, 2 * g + c // 2
                                    last = mm(pv_ps[32 * c:32 * c + 32, g % 2, :], vT[t.c % RING][:, h, HEADS * j + pair, :],
                                              probs[(2 * pair + j) % PROBS][:, h, :], start=h == 0, stop=h == 1,
                                              skip_group_check=True)
                            done(last, "pv_mm")

            run_steps(pe, tiles, SKEW, step)

            transpose = nc.tensor.transpose
            phase1_over(pe)
            pe.wait_ge(S["wg_dma"], 16)
            mT_sems = (S["mT_act"], S["mT_dve"])
            for n in range(tiles // 2 + 1):
                if n < tiles // 2:
                    if n >= 2:
                        pe.wait_ge(mT_sems[n % 2], n // 2)
                    for h in range(HALVES):
                        for b in range(2):
                            last = transpose(banks[n % 2][:, D * h + P * b:D * h + P * (b + 1)],
                                             rows_all[:, 2 * n + b, P * h:P * (h + 1)], ident_keep[:, :])
                    done(last, "mT_mm")
                if n > 0:
                    m = n - 1
                    pe.wait_ge(mT_sems[m % 2], m // 2 + 1)
                    c, slot = m % 4, m // 4
                    for h in range(HALVES):
                        last = mm(banks[2 + slot // 2][32 * c:32 * c + 32, D * (slot % 2):D * (slot % 2 + 1)],
                                  wg_sb[:, h, :], mT[m % 2][:, h, :, :].rearrange("p b t -> p (b t)"),
                                  start=h == 0, stop=h == 1, skip_group_check=True)
                    done(last, "logitsT_mm")
            pe.wait_ge(S["logitsT_ok"], tiles // 16)
            for slot in range(tiles // 8):
                for b in range(2):
                    last = transpose(banks[4 + slot // 2][:, D * (slot % 2) + P * b:D * (slot % 2) + P * (b + 1)],
                                     logitsT[:, slot, b, :], ident_keep[:, :])
            done(last, "logit_mm")
            pe.wait_ge(S["route_dve"], before_count)
            for i, which in enumerate((earlier, ones[:, :])):
                last = mm(banks[i][:, 0:EXPERTS * tiles], which, route["both"][:, :, :].rearrange("p t e -> p (t e)"),
                          start=True, stop=True)
            done(last, "count_mm")

            def turn(k, e, par):
                pe.wait_ge(slots_dma[par], 16 * k + 16)
                for n, (first, size) in enumerate(xT_parts):
                    wait_past(pe, S[("xT_act", "xT_dve")[n % 2]], e * n_xT[n % 2] + n // 2)
                    for h in range(HALVES):
                        for b in range(size):
                            last = transpose(banks[6 + n % 2][:, P * (size * h + b):P * (size * h + b + 1)],
                                             slots_in[par][:, first + b, P * h:P * (h + 1)], ident_keep[:, :])
                    done(last, "xT_mm")

            def hidden(e, par, g):
                first, size = groups[g]
                for f in range(FF):
                    m = g * FF + f
                    wait_past(pe, S[("h_act", "h_dve")[f % 2]], e * n_h + (m // 2 - 1))
                    for h in range(HALVES):
                        last = mm(banks[m % 4][:, 0:P * size], w1_sb[par][:, h, P * f:P * (f + 1)],
                                  xT[par][:, h, P * first:P * (first + size)], start=h == 0, stop=h == 1)
                    done(last, "h_mm")

            def outputs(e, par, g):
                for name in ("h_act", "h_dve"):
                    pe.wait_ge(S[name], e * n_h + (g + 1) * FF // 2)
                for q, first, size in chunks_of(g):
                    wait_past(pe, S[("y_act", "y_dve")[q % 2]], e * n_y[q % 2] + y_before(q))
                    for b in range(size):
                        o = P * (first + b - groups[g][0])
                        for f in range(FF):
                            last = mm(banks[4 + q % 2][:, D * b:D * (b + 1)], hT[g % 2][:, f, o:o + P],
                                      w2_sb[par][:, f, :], start=f == 0, stop=f == FF - 1)
                    done(last, "y_mm")

            def expert(k, e, par, more):
                pe.wait_ge(w_dma[par], 32 * k + 32)
                pe.wait_ge(S["xT_act"], (e + 1) * n_xT[0])
                pe.wait_ge(S["xT_dve"], (e + 1) * n_xT[1])
                hidden(e, par, 0)
                for g in range(1, len(groups)):
                    hidden(e, par, g)
                    outputs(e, par, g - 1)
                    if g == 1 and more:
                        turn(k + par, e + 1, 1 - par)
                outputs(e, par, len(groups) - 1)

            turn(0, 0, 0)
            run_experts(pe, expert)


_INS = ["x", "ctx_2048", "L0_attn_W_in", "L0_attn_b_in", "L0_attn_W_out", "L0_attn_b_out", "L0_attn_gamma",
        "L0_attn_beta", "L0_xattn_gamma", "L0_ffn_Wg", "L0_ffn_w1", "L0_ffn_w2"]


def constants():
    import numpy as np
    rot = D // 2
    inv_freq = (1.0 / 10000.0 ** (np.arange(0, rot, 2, dtype=np.float32) / rot)).astype(np.float32)
    angles = np.repeat(np.arange(SEQ, dtype=np.float32)[:, None] * inv_freq[None, :], 2, axis=-1)
    cos, sin = np.cos(angles).astype(np.float32), np.sin(angles).astype(np.float32)
    sin[:, 0::2] *= -1
    both = lambda a: np.tile(np.concatenate([a, a], axis=1), (2, 1))
    mask = np.zeros((P, 2), np.float32)
    mask[:SEQ, 0] = mask[SEQ:, 1] = 1.0
    return np.ascontiguousarray(np.concatenate([np.eye(P, dtype=np.float32), both(cos), both(sin), mask], axis=1))


def route_constants(tiles):
    import numpy as np
    capacity = -(-5 * tiles * P * TOP_K // (4 * EXPERTS))
    row = np.arange(P)[:, None]
    earlier = row < np.arange(P)[None, :]
    not_first = np.tile(np.arange(tiles) > 0, EXPERTS)[None, :].repeat(P, 0)
    experts = np.arange(EXPERTS)[None, :].repeat(P, 0)
    return np.ascontiguousarray(np.concatenate([earlier, not_first, experts, experts * capacity,
                                                row + P * np.arange(tiles)[None, :]], axis=1).astype(np.float32))


def kernel(**inputs):
    import numpy as np
    import concourse.bacc as bacc
    from concourse.bass_utils import run_bass_kernel_spmd

    nc = bacc.Bacc("TRN2", target_bir_lowering=False, num_devices=1)
    tiles = inputs["x"].shape[0] * SEQ // P
    laid_out = {name: np.ascontiguousarray(inputs[name]) for name in _INS}
    laid_out["L0_xattn_gamma"] = laid_out["L0_xattn_gamma"].reshape(1)
    laid_out["constants"] = constants()
    laid_out["route_constants"] = route_constants(tiles)
    arrays, args = {}, []
    for name, a in laid_out.items():
        arrays[f"in_{name}"] = a
        args.append(nc.dram_tensor(f"in_{name}", a.shape, mybir.dt.from_np(a.dtype), kind="ExternalInput").ap())
    args.append(nc.dram_tensor("out_0", (tiles * P, D), mybir.dt.float32, kind="ExternalOutput").ap())
    decoder_block(nc, tiles, *args)
    r = run_bass_kernel_spmd(nc, [arrays], core_ids=[0])
    return r.results[0]["out_0"].reshape(inputs["x"].shape)
```

```python
import concourse.bass as bass
from concourse import mybir
from contextlib import ExitStack

P = 128
D = 256
HALVES = D // P
SEQ = 64
HEADS = 8
DH = SEQ // HEADS
PAIRS = HEADS
TERMS = 6
OPK = TERMS * DH
EPS = 1e-5
RING = 4
SKEW = 6
PROBS = 8
EXPERTS = 8
TOP_K = 2
D_FF = 1024
FF = D_FF // P
TOKEN_ID = D
GATES = D + 1
ROW = GATES + EXPERTS
Y_RING = 5
FAR = 1.0e6


class Tile:

    def __init__(self, it, c):
        self.it, self.c = it, c

    def __add__(self, n):
        return Tile(self.it, self.c + n)

    def exists(self, tiles):
        return self.it is not None or 0 <= self.c < tiles

    def number(self):
        return self.c if self.it is None else self.it * RING + self.c

    def count(self, per_tile, n):
        fixed = per_tile * self.c + n
        return fixed if self.it is None else self.it * (RING * per_tile) + fixed

    def loads(self, dmas):
        fixed = 16 * dmas * (self.c // 2 + 1)
        return fixed if self.it is None else self.it * (16 * dmas * RING // 2) + fixed


def run_steps(engine, tiles, skew, step):
    for s in range(2 * RING):
        step(Tile(None, s))
    with engine.Fori(2, tiles // RING - 1) as it:
        for c in range(RING):
            step(Tile(it, c))
    for s in range(tiles - RING, tiles + skew):
        step(Tile(None, s))


def decoder_block(nc, tiles, x, ctx_in, w_in, b_in, w_out, b_out, ln_gamma, ln_beta, xattn_gamma, wg, w1, w2,
                  consts, route_consts, out):
    F32, BF16 = mybir.dt.float32, mybir.dt.bfloat16
    ALU, ACT, AX = mybir.AluOpType, mybir.ActivationFunctionType, mybir.AxisListType

    x_tiles = x.rearrange("(t b) s d -> t (b s) d", b=2)
    ctx_tiles = ctx_in.rearrange("(t b) s d -> t (b s) d", b=2)
    out_tiles = out.rearrange("(t p) d -> t p d", p=P)
    w_in_v = w_in.rearrange("(c p) n -> p c n", p=P)
    w_out_v = w_out.rearrange("(c p) n -> p c n", p=P)
    half_rows = "(c p) -> p c"

    def dram(name, shape, dtype):
        return nc.dram_tensor(name, shape, dtype, kind="Internal").ap()

    q_terms = [dram(f"q_terms{i}", (P, TERMS, D), BF16) for i in range(2)]
    k_terms = [dram(f"k_terms{i}", (P, TERMS, D), BF16) for i in range(2)]
    attended = [dram(f"attended{i}", (2 * HEADS, DH + 1, D), F32) for i in range(2)]
    inverses = [dram(f"inverses{i}", (2 * HEADS, D), F32) for i in range(2)]

    ctx = ExitStack()
    with ctx:
        def sb(name, shape, dt=F32):
            return ctx.enter_context(nc.sbuf_tensor(name, shape, dt))

        def pb(name, shape, dt=F32):
            return ctx.enter_context(nc.psum_tensor(name, shape, dt))

        def sem(name):
            return ctx.enter_context(nc.semaphore(name))

        capacity = -(-5 * tiles * P * TOP_K // (4 * EXPERTS))
        blocks = capacity // P
        assert blocks * P == capacity and blocks % Y_RING == 0 and tiles % 8 == 0
        groups = [(b, min(4, blocks - b)) for b in range(0, blocks, 4)]
        n_slots = EXPERTS * capacity
        slots_dram = dram("slots_dram", (n_slots, ROW), F32)

        rows_all = sb("rows_all", [P, tiles, ROW])
        route_sb = sb("route_sb", [P, P + EXPERTS * tiles + 2 * EXPERTS + tiles])
        earlier = route_sb[:, 0:P]
        not_first = route_sb[:, P:P + EXPERTS * tiles]
        expert_no = route_sb[:, P + EXPERTS * tiles:P + EXPERTS * (tiles + 1)]
        expert_base = route_sb[:, P + EXPERTS * (tiles + 1):P + EXPERTS * (tiles + 2)]
        token_no = route_sb[:, P + EXPERTS * (tiles + 2):P + EXPERTS * (tiles + 2) + tiles]
        ones = sb("ones", [P, P])
        wg_sb = sb("wg_sb", [P, HALVES, 32])
        ident_keep = sb("ident_keep", [P, P])
        empty_row = sb("empty_row", [P, ROW])

        phase1 = ctx.enter_context(ExitStack())

        def sb(name, shape, dt=F32):
            return phase1.enter_context(nc.sbuf_tensor(name, shape, dt))

        const_sb = sb("const_sb", [P, 128 + 256 + 256 + 2])
        ident = const_sb[:, 0:128]
        cos_kv = const_sb[:, 128:384].rearrange("p (a d) -> p a d", a=2)
        sin_kv = const_sb[:, 384:640].rearrange("p (a d) -> p a d", a=2)
        row_mask = const_sb[:, 640:642]
        ident_bf = sb("ident_bf", [P, P], BF16)
        w_in_raw = sb("w_in_raw", [P, HALVES, 3 * D])
        w_in_g = sb("w_in_g", [P, HALVES, 3 * D])
        w_out_sb = sb("w_out_sb", [P, HALVES, D])
        gamma_col = sb("gamma_col", [P, HALVES])
        beta_col = sb("beta_col", [P, HALVES])
        beta_wide = sb("beta_wide", [P, HALVES, P])
        bias_kv_raw = sb("bias_kv_raw", [P, 2 * D])
        bias_kv = sb("bias_kv", [P, 2 * D])
        bias_q_raw = sb("bias_q_raw", [P, HALVES])
        bias_q = sb("bias_q", [P, HALVES, 2])
        b_out_sb = sb("b_out_sb", [P, D])
        xgamma = sb("xgamma", [P, 1])
        minus_half = sb("minus_half", [P, 2])

        x_in = [sb(f"x_in{i}", [P, D]) for i in range(2)]
        c_in = [sb(f"c_in{i}", [P, D]) for i in range(RING)]
        x_stats = [sb(f"x_stats{i}", [P, 6]) for i in range(2)]
        x_mv = [sb(f"x_mv{i}", [P, 2]) for i in range(2)]
        x_var = [sb(f"x_var{i}", [P, 2]) for i in range(2)]
        x_nmean = [sb(f"x_nmean{i}", [P, 1]) for i in range(2)]
        x_rstd = [sb(f"x_rstd{i}", [P, 2]) for i in range(2)]
        base_affine = [sb(f"base_affine{i}", [P, 2]) for i in range(2)]
        xn = [sb(f"xn{i}", [P, D]) for i in range(2)]
        base0 = [sb(f"base0{i}", [P, D]) for i in range(2)]
        base = [sb(f"base{i}", [P, D]) for i in range(2)]
        xnT = [sb(f"xnT{i}", [P, HALVES, P]) for i in range(2)]
        kv = [sb(f"kv{i}", [P, 2, D]) for i in range(2)]
        rot_cos = sb("rot_cos", [P, 2, P])
        rot_sin = sb("rot_sin", [P, 2, P])
        rot = [sb(f"rot{i}", [P, 2, P]) for i in range(2)]
        kv_prod = [sb(f"kv_prod{i}", [P, D]) for i in range(2)]
        squares = [sb(f"squares{i}", [P, 2, D]) for i in range(2)]
        norms2 = [sb(f"norms2{i}", [P, 2]) for i in range(2)]
        inv_norms = [sb(f"inv_norms{i}", [P, 2]) for i in range(2)]
        row_weight = [sb(f"row_weight{i}", [P, 2]) for i in range(2)]
        a_scale = [sb(f"a_scale{i}", [P, HALVES, 2]) for i in range(2)]
        a_bias = [sb(f"a_bias{i}", [P, HALVES, 2]) for i in range(2)]
        yT = [sb(f"yT{i}", [P, HALVES, P]) for i in range(2)]

        x1 = [sb(f"x1{i}", [P, D]) for i in range(2)]
        q_stats = sb("q_stats", [P, 6])
        q_mv = sb("q_mv", [P, 2])
        q_var = [sb(f"q_var{i}", [P, 1]) for i in range(2)]
        q_nmean = [sb(f"q_nmean{i}", [P, 1]) for i in range(2)]
        q_rstd = [sb(f"q_rstd{i}", [P, 1]) for i in range(2)]
        q_full = [sb(f"q_full{i}", [P, D]) for i in range(2)]
        q_rest = [sb(f"q_rest{i}", [P, D]) for i in range(2)]
        q_parts = [sb(f"q_parts{i}", [P, 3, D], BF16) for i in range(2)]
        c_rest = [sb(f"c_rest{i}", [P, D]) for i in range(2)]
        c_parts = [sb(f"c_parts{i}", [P, 3, D], BF16) for i in range(2)]
        q_op = [sb(f"q_op{i}", [P, PAIRS, D], BF16) for i in range(RING)]
        k_op = [[sb(f"k_op{i}_{j}", [P, PAIRS, D], BF16) for j in range(2)] for i in range(RING)]
        vT = [sb(f"vT{i}", [P, 2, 2 * HEADS, 32]) for i in range(RING)]
        neg_max = [sb(f"neg_max{i}", [P, 2, 8]) for i in range(2)]
        max_parts = [sb(f"max_parts{i}", [P, 2, 2, 8], BF16) for i in range(2)]
        max_rows = [sb(f"max_rows{i}", [32, P], BF16) for i in range(2)]
        probs = [sb(f"probs{i}", [P, 2, D]) for i in range(PROBS)]
        pv_sb = [sb(f"pv_sb{i}", [P, 4, D]) for i in range(2)]
        sums = [sb(f"sums{i}", [P, 32]) for i in range(2)]
        inv_sums = [sb(f"inv_sums{i}", [P, 32]) for i in range(2)]
        numer = [sb(f"numer{i}", [P, D]) for i in range(2)]
        inv_wide = [sb(f"inv_wide{i}", [P, D]) for i in range(2)]
        attn = [sb(f"attn{i}", [P, D]) for i in range(2)]
        x2 = [sb(f"x2{i}", [P, D]) for i in range(2)]
        m_stats = sb("m_stats", [P, 6])
        m_mv = sb("m_mv", [P, 2])
        m_var = [sb(f"m_var{i}", [P, 1]) for i in range(2)]
        m_nmean = [sb(f"m_nmean{i}", [P, 1]) for i in range(2)]
        m_rstd = [sb(f"m_rstd{i}", [P, 1]) for i in range(2)]

        scores = [pb(f"scores{i}", [P, 2, D]) for i in range(2)]
        scoresT = [pb(f"scoresT{i}", [P, 2, D]) for i in range(3)]
        pv_ps = pb("pv_ps", [P, 2, D])
        work = pb("work", [P, 2, D])
        work_a, work_b = work[:, 0, :], work[:, 1, :]
        turn_ps = pb("turn_ps", [P, 2, D])
        max_ps = turn_ps[:, 1, 0:64].bitcast(BF16)[0:32, 0:P]

        phase1.close()

        def sb(name, shape, dt=F32):
            return ctx.enter_context(nc.sbuf_tensor(name, shape, dt))

        mT = [sb(f"mT{i}", [P, HALVES, 2, P]) for i in range(2)]
        logitsT = sb("logitsT", [P, tiles // 8, 2, P])
        route = {n: sb(f"r_{n}", [P, tiles, EXPERTS]) for n in
                 ("logit", "miss", "key", "hot0", "rest", "hot1", "both", "prob", "pos", "slot", "t0", "t1", "p0", "p1",
                  "e0", "e1", "g0", "g1")}
        per_expert = {n: sb(f"x_{n}", [P, EXPERTS, tiles]) for n in ("total", "through", "before")}
        flat = {n: sb(f"f_{n}", [P, tiles]) for n in
                ("top0", "top1", "id0", "id1", "z", "rz", "pos0", "pos1", "slot0", "slot1", "full0", "full1", "x0", "x1",
                 "p0", "p1", "g0", "g1")}
        slot_no = [sb(f"slot_no{k}", [P, tiles], mybir.dt.int32) for k in range(TOP_K)]
        w1_sb = [sb(f"w1_sb{i}", [P, HALVES, D_FF]) for i in range(2)]
        w2_sb = [sb(f"w2_sb{i}", [P, FF, D]) for i in range(2)]
        slots_in = [sb(f"slots_in{i}", [P, blocks, ROW]) for i in range(2)]
        xT = [sb(f"xT{i}", [P, HALVES, capacity]) for i in range(2)]
        hT = [sb(f"hT{i}", [P, FF, 4 * P]) for i in range(2)]
        y_id = [sb(f"y_id{i}", [P, blocks], mybir.dt.int32) for i in range(2)]
        y_gate = [sb(f"y_gate{i}", [P, blocks]) for i in range(2)]
        y = [sb(f"y{i}", [P, D]) for i in range(Y_RING)]
        banks = [b[:, :, :].rearrange("p a d -> p (a d)") for b in
                 (scores[0], scores[1], scoresT[0], scoresT[1], scoresT[2], pv_ps, work, turn_ps)]

        names = ["setup_in", "setup_dve", "setup_pe", "setup_pool", "x_bn", "x_mv_ok", "x_var_ok", "x_rstd_ok", "affine_ok",
                 "xn_ok", "base0_ok", "base_ok", "xnT_mm", "xnT_ok", "kv_mm", "kv_ok", "qT_mm",
                 "rot_cos_ok", "rot_sin_ok", "rot_ok", "kv_prod_ok", "norms_ok", "inv_norms_ok", "row_weight_ok",
                 "a_mm", "a_scale_ok", "a_bias_ok", "y_ok", "wo_mm", "x1_ok", "x1_kept", "q_bn", "q_mv_ok", "q_var_ok",
                 "q_rstd_ok", "q_full_ok", "q_hi_ok", "q_rest_ok", "q_mid_ok", "q_parts_ok", "c_hi_ok", "c_rest_ok",
                 "c_mid_ok", "c_parts_ok", "cT_mm", "vT_ok", "scores_mm", "row_max_ok", "max_hi_ok", "max_mid_ok",
                 "max_mm", "max_rows_ok", "scoresT_mm", "probs_ok", "pv_mm", "pv_ok", "inv_sums_ok", "attn_ok",
                 "x2_ok", "m_bn", "m_mv_ok", "m_var_ok", "m_rstd_ok", "m_ok",
                 "phase1_pe", "phase1_act", "phase1_dve", "phase1_pool", "blank_ok", "blank_dma", "wg_dma",
                 "mT_mm", "mT_act", "mT_dve", "logitsT_mm", "logitsT_ok", "logit_mm", "route_dve", "prob_ok", "count_mm",
                 "slot_ok", "scatter_dma", "xT_mm", "xT_act", "xT_dve", "meta_ok", "h_mm", "h_act", "h_dve", "y_mm",
                 "y_act", "y_dve"]
        S = {n: sem(n) for n in names}
        pair_names = ["x_dma", "c_dma", "q_terms_dma", "k_terms_dma", "q_op_dma", "k_op_dma", "max_dma",
                      "attended_dma", "sums_dma", "inverses_dma", "back_dma", "x2_dma"]
        D2 = {n: [sem(f"{n}{i}") for i in range(2)] for n in pair_names}
        w_dma = [sem(f"w_dma{i}") for i in range(2)]
        slots_dma = [sem(f"slots_dma{i}") for i in range(2)]
        add_dma = [sem(f"add_dma{i}") for i in range(Y_RING)]

        block = ctx.enter_context(nc.Block())

        def max_group(s, p):
            return (s + -3, 0) if p else (s + -4, 1)

        SETUP_LOADS = 11
        before_exp, before_count = 7, 13
        xT_parts = [(b, min(2, blocks - b)) for b in range(0, blocks, 2)]
        y_chunks = [(b, min(2, first + size - b)) for first, size in groups for b in range(first, first + size, 2)]
        n_xT = [(len(xT_parts) + 1) // 2, len(xT_parts) // 2]
        n_h = len(groups) * FF // 2
        n_y = [sum(size for _, size in y_chunks[side::2]) for side in range(2)]
        y_uses = blocks // Y_RING

        def y_before(q):
            return sum(size for _, size in y_chunks[q % 2:q:2])

        def chunks_of(g):
            return [(q, first, size) for q, (first, size) in enumerate(y_chunks)
                    if groups[g][0] <= first < groups[g][0] + groups[g][1]]

        def hT_free(e, g):
            if g >= 2:
                return e * len(y_chunks) + (chunks_of(g - 2)[-1][0] + 1)
            before = max(i for i in range(len(groups)) if i % 2 == g % 2)
            return (e - 1) * len(y_chunks) + (chunks_of(before)[-1][0] + 1)

        def run_experts(engine, expert):
            for par in range(2):
                expert(0, par, par, True)
            with engine.Fori(1, EXPERTS // 2 - 1) as it:
                for par in range(2):
                    expert(it, it * 2 + par, par, True)
            for par in range(2):
                expert(EXPERTS // 2 - 1, EXPERTS - 2 + par, par, par == 0)

        def wait_past(engine, sem, value):
            if not isinstance(value, int) or value > 0:
                engine.wait_ge(sem, value)

        def wait_apart(engine, sem, value):
            if not isinstance(value, int):
                value = engine.to_reg(value)
                engine.wait_ge(S["setup_in"], 16 * SETUP_LOADS)
            engine.wait_ge(sem, value)

        def phase1_over(engine):
            engine.wait_ge(S["m_ok"], tiles)
            for last in (tiles - 2, tiles - 1):
                engine.wait_ge(D2["x2_dma"][last % 2], Tile(None, last).loads(1))

        @block.sync
        def _(sp):
            def need(name, t, per_tile=1, n=1):
                wait_apart(sp, S[name], t.count(per_tile, n))

            def landed(name, t, dmas):
                wait_apart(sp, D2[name][t.c % 2], t.loads(dmas))

            def put(name, t, dst, src):
                sp.dma_start(dst, src).then_inc(D2[name][t.c % 2], 16)

            for dst, src in ((const_sb[:, :], consts), (w_in_raw[:, :, :], w_in_v), (w_out_sb[:, :, :], w_out_v),
                             (gamma_col[:, :], ln_gamma.rearrange(half_rows, p=P)),
                             (beta_col[:, :], ln_beta.rearrange(half_rows, p=P)),
                             (bias_kv_raw[:, :], b_in[D:3 * D].partition_broadcast(P)),
                             (bias_q_raw[:, :], b_in[0:D].rearrange(half_rows, p=P)),
                             (b_out_sb[:, :], b_out.partition_broadcast(P)),
                             (xgamma[:, :], xattn_gamma.partition_broadcast(P)), (route_sb[:, :], route_consts),
                             (ident_keep[:, :], consts[:, 0:P])):
                with nc.allow_non_contiguous_dma(reason="vectors laid out over the partitions, once"):
                    sp.dma_start(dst, src).then_inc(S["setup_in"], 16)

            def write_terms(name, t, terms, parts, slots):
                for first, part, repeat in slots:
                    m = repeat if repeat > 0 else -repeat
                    src = parts[:, part:part + m, :] if repeat > 0 else \
                        parts[:, part:part + 1, :].broadcast_to([P, m, D])
                    put(name, t, terms[:, first:first + m, :], src)

            def max_rows_out(s, p):
                t, g = max_group(s, p)
                if t.exists(tiles):
                    need("max_rows_ok", t, 2, g + 1)
                    for j in range(2):
                        sp.dma_start(q_op[t.c % RING][64 * j + OPK:64 * j + OPK + 2, 4 * g:4 * g + 4, :],
                                     max_rows[g][16 * j:16 * j + 16, :]).then_inc(D2["max_dma"][g], 16)

            def load_inputs(u):
                if (u + -2).exists(tiles):
                    need("base0_ok", u + -2)
                    need("xn_ok", u + -2)
                    need("c_parts_ok", u + -2)
                if (u + -4).exists(tiles):
                    need("cT_mm", u + -4)
                put("x_dma", u, x_in[u.c % 2][:, :], x_tiles[u.number()])
                put("c_dma", u, c_in[u.c % RING][:, :], ctx_tiles[u.number()])

            load_inputs(Tile(None, 0))

            def load_weights(i, e):
                sp.dma_start(w1_sb[i][:, :, :], w1.rearrange("e (c p) f -> e p c f", p=P)[e]).then_inc(w_dma[i], 16)
                sp.dma_start(w2_sb[i][:, :, :], w2.rearrange("e (c p) n -> e p c n", p=P)[e]).then_inc(w_dma[i], 16)

            def step(s):
                t, v, w = s + -6, s + -2, s + -5
                if s.it is None and s.c < EXPERTS:
                    sp.wait_ge(S["blank_ok"], 1)
                    sp.dma_start(slots_dram[capacity * s.c:capacity * (s.c + 1), :].rearrange("(b p) n -> p b n", p=P),
                                 empty_row[:, :].rearrange("p (o n) -> p o n", o=1).broadcast_to([P, blocks, ROW])
                                 ).then_inc(S["blank_dma"], 16)
                if s.it is None and s.c == 2:
                    with nc.allow_non_contiguous_dma(reason="the router's weights, once"):
                        sp.dma_start(wg_sb[:, :, 0:EXPERTS], wg.rearrange("(c p) n -> p c n", p=P)
                                     ).then_inc(S["wg_dma"], 16)
                if (s + 1).exists(tiles):
                    load_inputs(s + 1)
                max_rows_out(s, 0)
                if w.exists(tiles):
                    need("pv_ok", w, 2, 2)
                    if (w + -2).exists(tiles):
                        landed("back_dma", w + -2, 2)
                        landed("sums_dma", w + -2, 1)
                    for c in range(4):
                        dst = attended[w.c % 2].rearrange("(j g q) r f -> j g q r f", j=2, q=2)[c % 2, :, c // 2]
                        put("attended_dma", w, dst.rearrange("g r f -> r g f"),
                            pv_sb[w.c % 2][32 * c:32 * c + DH + 1, :, :])
                if w.exists(tiles):
                    landed("attended_dma", w, 4)
                    put("sums_dma", w, sums[w.c % 2][:, :],
                        attended[w.c % 2][:, DH, :].rearrange("h (c f) -> h c f", c=8))
                max_rows_out(s, 4)
                if v.exists(tiles):
                    need("q_parts_ok", v)
                    if (v + -2).exists(tiles):
                        landed("q_op_dma", v + -2, 2)
                    write_terms("q_terms_dma", v, q_terms[v.c % 2], q_parts[v.c % 2],
                                ((0, 0, -3), (3, 1, -2), (5, 2, 1)))
                    if (v + -4).exists(tiles):
                        need("scoresT_mm", v + -4, 16, 16)
                    landed("k_terms_dma", v, 3)
                    if v.it is None:
                        sp.wait_ge(S["setup_dve"], 1)
                    for j in range(2):
                        put("k_op_dma", v, k_op[v.c % RING][j][64 * j:64 * j + OPK, :, :],
                            k_terms[v.c % 2][64 * j:64 * j + 64].rearrange("(h d) m f -> (d m) h f", d=DH))
                if w.exists(tiles):
                    need("inv_sums_ok", w)
                    put("inverses_dma", w, inverses[w.c % 2].rearrange("h (c f) -> h c f", c=8),
                        inv_sums[w.c % 2][:, :])
                if v.exists(tiles):
                    landed("q_terms_dma", v, 3)
                    for j in range(2):
                        put("q_op_dma", v, q_op[v.c % RING][64 * j:64 * j + OPK, :, :],
                            q_terms[v.c % 2][64 * j:64 * j + 64].rearrange("(h d) m f -> (d m) h f", d=DH))
                if w.exists(tiles):
                    landed("inverses_dma", w, 1)
                    if (w + -2).exists(tiles):
                        need("attn_ok", w + -2)
                    put("back_dma", w, numer[w.c % 2][:, :], attended[w.c % 2][:, 0:DH, :])
                    put("back_dma", w, inv_wide[w.c % 2][:, :],
                        inverses[w.c % 2].rearrange("h (o f) -> h o f", o=1).broadcast_to([2 * HEADS, DH, D]))
                if s.exists(tiles):
                    need("c_parts_ok", s)
                    if (s + -2).exists(tiles):
                        landed("k_op_dma", s + -2, 2)
                    write_terms("k_terms_dma", s, k_terms[s.c % 2], c_parts[s.c % 2],
                                ((0, 0, 3), (3, 0, 2), (5, 0, 1)))
                if t.exists(tiles):
                    need("x2_ok", t)
                    put("x2_dma", t, out_tiles[t.number()], x2[t.c % 2][:, :])

            run_steps(sp, tiles, SKEW, step)
            for last in (tiles - 2, tiles - 1):
                landed("x2_dma", Tile(None, last), 1)

            phase1_over(sp)
            sp.wait_ge(S["mT_mm"], 1)
            for e in range(2):
                load_weights(e, e)

            def load_slots(i, e):
                sp.dma_start(slots_in[i][:, :, :],
                             slots_dram[bass.ds(e * capacity, capacity), :].rearrange("(b p) n -> p b n", p=P)
                             ).then_inc(slots_dma[i], 16)

            sp.wait_ge(S["scatter_dma"], 16 * TOP_K * tiles)
            load_slots(0, 0)

            def expert(k, e, par, more):
                if more:
                    wait_apart(sp, S["meta_ok"], e + 1)
                    wait_apart(sp, S["xT_mm"], (e + 1) * len(xT_parts))
                    load_slots(1 - par, e + 1)
                if not (isinstance(k, int) and k == EXPERTS // 2 - 1):
                    wait_apart(sp, S["y_mm"], (e + 1) * len(y_chunks))
                    load_weights(par, e + 2)

            run_experts(sp, expert)
            for r in range(Y_RING):
                sp.wait_ge(add_dma[r], 16 * y_uses * EXPERTS)

        @block.gpsimd
        def _(pool):
            def need(name, t, per_tile=1, n=1):
                pool.wait_ge(S[name], t.count(per_tile, n))

            def need_apart(name, t):
                wait_apart(pool, S[name], t.count(1, 1))

            def done(ins, name):
                ins.then_inc(S[name], 1)

            g = nc.gpsimd
            g.memset(minus_half[:, :], -0.5)
            for i in range(RING):
                g.memset(vT[i][:, :, :, :], 1.0)
            g.memset(ones[:, :], 1.0)
            g.memset(wg_sb[:, :, :], 0.0)
            g.memset(empty_row[:, :], 0.0)
            done(g.memset(base_affine[0][:, :], 0.0), "setup_pool")
            pool.wait_ge(S["setup_pool"], 1)
            pool.wait_ge(S["setup_in"], 16 * SETUP_LOADS)
            done(g.memset(empty_row[:, TOKEN_ID:TOKEN_ID + 1], float(tiles * P)), "blank_ok")

            def split(t, full, rest, parts, pre):
                done(g.tensor_scalar(parts[:, 0, :], full[:, :], 1.0, 1.0, ALU.mult, ALU.mult), pre + "_hi_ok")
                need(pre + "_hi_ok", t)
                done(g.tensor_tensor(rest[:, :], full[:, :], parts[:, 0, :], ALU.subtract), pre + "_rest_ok")
                need_apart(pre + "_rest_ok", t)
                done(g.tensor_scalar(parts[:, 1, :], rest[:, :], 1.0, 1.0, ALU.mult, ALU.mult), pre + "_mid_ok")
                need(pre + "_mid_ok", t)
                done(g.tensor_tensor(parts[:, 2, :], rest[:, :], parts[:, 1, :], ALU.subtract), pre + "_parts_ok")

            def step(s):
                if s.exists(tiles):
                    i = s.c % 2
                    need("x_var_ok", s)
                    done(g.tensor_tensor(x_rstd[i][:, :], x_var[i][:, :], minus_half[:, :], ALU.pow), "x_rstd_ok")
                    need_apart("x_rstd_ok", s)
                    if (s + -2).exists(tiles):
                        need_apart("xnT_mm", s + -2)
                    done(g.tensor_scalar(xn[i][:, :], x_in[i][:, :], x_nmean[i][:, :], x_rstd[i][:, 1:2],
                                         ALU.add, ALU.mult), "xn_ok")
                u = s + -1
                if u.exists(tiles):
                    i = u.c % 2
                    need("kv_ok", u)
                    turned = kv[i][:, :, 0:P].rearrange("p a (n e) -> p a n e", e=2)
                    sines = sin_kv.rearrange("p a (n e) -> p a n e", e=2)
                    target = rot_sin[:, :, :].rearrange("p a (n e) -> p a n e", e=2)
                    if (u + -1).exists(tiles):
                        need("rot_ok", u + -1)
                    done(g.tensor_tensor(rot_cos[:, :, :], kv[i][:, :, 0:P], cos_kv, ALU.mult), "rot_cos_ok")
                    for e in range(2):
                        last = g.tensor_tensor(target[:, :, :, e], turned[:, :, :, 1 - e], sines[:, :, :, e], ALU.mult)
                    done(last, "rot_sin_ok")
                    if (u + -2).exists(tiles):
                        need("a_mm", u + -2)
                    g.tensor_tensor(kv_prod[i][:, P:D], kv[i][:, 0, P:D], kv[i][:, 1, P:D], ALU.mult)
                    need("rot_cos_ok", u)
                    need("rot_sin_ok", u)
                    done(g.tensor_tensor(rot[i][:, :, :], rot_cos[:, :, :], rot_sin[:, :, :], ALU.add), "rot_ok")
                    need("norms_ok", u)
                    done(g.tensor_tensor(inv_norms[i][:, :], norms2[i][:, :], minus_half[:, :], ALU.pow), "inv_norms_ok")
                    need("rot_ok", u)
                    done(g.tensor_tensor(kv_prod[i][:, 0:P], rot[i][:, 0, :], rot[i][:, 1, :], ALU.mult), "kv_prod_ok")
                    need_apart("inv_norms_ok", u)
                    done(g.tensor_scalar(row_weight[i][:, :], row_mask, inv_norms[i][:, 0:1], inv_norms[i][:, 1:2],
                                         ALU.mult, ALU.mult), "row_weight_ok")
                v = s + -2
                if v.exists(tiles):
                    i = v.c % 2
                    need("q_var_ok", v)
                    done(g.tensor_tensor(q_rstd[i][:, :], q_var[i][:, :], minus_half[:, 0:1], ALU.pow), "q_rstd_ok")
                    need_apart("q_rstd_ok", v)
                    done(g.tensor_scalar(q_full[i][:, :], x1[i][:, :], q_nmean[i][:, :], q_rstd[i][:, :],
                                         ALU.add, ALU.mult), "q_full_ok")
                    if (v + -2).exists(tiles):
                        wait_apart(pool, D2["q_terms_dma"][i], (v + -2).loads(3))
                    need_apart("q_full_ok", v)
                    split(v, q_full[i], q_rest[i], q_parts[i], "q")
                t = s + -6
                if t.exists(tiles):
                    i = t.c % 2
                    pool.wait_ge(D2["back_dma"][i], t.loads(2))
                    if (t + -2).exists(tiles):
                        need("x2_ok", t + -2)
                    done(g.tensor_tensor(attn[i][:, :], numer[i][:, :], inv_wide[i][:, :], ALU.mult), "attn_ok")
                if s.exists(tiles):
                    i = s.c % 2
                    g.tensor_scalar(base_affine[i][:, 0:1], x_rstd[i][:, 0:1], 1.0, 1.0, ALU.mult, ALU.add)
                    done(g.tensor_tensor(base_affine[i][:, 1:2], x_rstd[i][:, 0:1], x_nmean[i][:, :], ALU.mult),
                         "affine_ok")
                    wait_apart(pool, D2["c_dma"][i], s.loads(1))
                    if (s + -2).exists(tiles):
                        need_apart("x1_ok", s + -2)
                        wait_apart(pool, D2["k_terms_dma"][i], (s + -2).loads(3))
                    need_apart("affine_ok", s)
                    done(g.tensor_scalar(base0[i][:, :], x_in[i][:, :], base_affine[i][:, 0:1],
                                         base_affine[i][:, 1:2], ALU.mult, ALU.add), "base0_ok")
                    split(s, c_in[s.c % RING], c_rest[i], c_parts[i], "c")
                    need("base0_ok", s)
                    done(g.tensor_tensor(base[i][:, :], base0[i][:, :], b_out_sb[:, :], ALU.add), "base_ok")
                if t.exists(tiles):
                    i = t.c % 2
                    need("m_var_ok", t)
                    done(g.tensor_tensor(m_rstd[i][:, :], m_var[i][:, :], minus_half[:, 0:1], ALU.pow), "m_rstd_ok")

            run_steps(pool, tiles, SKEW, step)

            pool.wait_ge(S["blank_dma"], 16 * EXPERTS)
            pool.wait_ge(S["slot_ok"], 1)
            for k in range(TOP_K):
                for t in range(tiles):
                    g.indirect_dma_start(
                        out=slots_dram[:, :], out_offset=bass.IndirectOffsetOnAxis(ap=slot_no[k][:, t:t + 1], axis=0),
                        in_=rows_all[:, t, :], in_offset=None, bounds_check=n_slots - 1, oob_is_err=False
                    ).then_inc(S["scatter_dma"], 16)
            for last in (tiles - 2, tiles - 1):
                pool.wait_ge(D2["x2_dma"][last % 2], Tile(None, last).loads(1))

            def expert(k, e, par, more):
                for r in range(Y_RING):
                    wait_past(pool, add_dma[r], e * (16 * y_uses))
                pool.wait_ge(S["meta_ok"], e + 1)
                for q, (first, size) in enumerate(y_chunks):
                    for b in range(size):
                        n = first + b
                        wait_apart(pool, S[("y_act", "y_dve")[q % 2]], e * n_y[q % 2] + (y_before(q) + b + 1))
                        g.indirect_dma_start(
                            out=out[:, :], out_offset=bass.IndirectOffsetOnAxis(ap=y_id[par][:, n:n + 1], axis=0),
                            in_=y[n % Y_RING][:, :], in_offset=None, bounds_check=tiles * P - 1, oob_is_err=False,
                            compute_op=ALU.add).then_inc(add_dma[n % Y_RING], 16)

            run_experts(pool, expert)

        @block.scalar
        def _(act):
            def need(name, t, per_tile=1, n=1):
                act.wait_ge(S[name], t.count(per_tile, n))

            def done(ins, name):
                ins.then_inc(S[name], 1)

            a = nc.scalar

            act.wait_ge(S["setup_pool"], 1)

            def exp_head(t, n):
                if t.exists(tiles):
                    if t.it is not None or 16 * t.c + n >= PROBS:
                        before, m = (t, n - PROBS) if n >= PROBS else (t + -1, n - PROBS + 16)
                        need("pv_mm", before, 4, m // 4 + 1)
                    need("scoresT_mm", t, 16, n + 1)
                    done(a.activation(probs[n % PROBS][:, :, :], scoresT[n % 3][:, :, :], ACT.Exp), "probs_ok")

            def step(s):
                v = s + -1
                for p in range(PAIRS):
                    exp_head(s + -4, 2 * p)
                    if p == 7 and v.exists(tiles):
                        i = v.c % 2
                        need("qT_mm", v)
                        need("a_bias_ok", v)
                        if (v + -2).exists(tiles):
                            need("wo_mm", v + -2)
                        for h in range(HALVES):
                            for b in range(2):
                                last = a.activation(yT[i][:, h, SEQ * b:SEQ * (b + 1)],
                                                    work_a[:, P * h + SEQ * b:P * h + SEQ * (b + 1)], ACT.Identity,
                                                    bias=a_bias[i][:, h, b:b + 1], scale=a_scale[i][:, h, b:b + 1])
                        done(last, "y_ok")
                    exp_head(s + -4, 2 * p + 1)
                    w, h = (s + -5, 1) if p == 1 else (s + -4, 0)
                    if p in (1, 5) and w.exists(tiles):
                        need("pv_mm", w, 4, 2 * h + 2)
                        if (w + -2).exists(tiles):
                            act.wait_ge(D2["attended_dma"][w.c % 2], (w + -2).loads(4))
                        done(a.copy(pv_sb[w.c % 2][:, 2 * h:2 * h + 2, :], pv_ps[:, :, :]), "pv_ok")
                    if p == 0 and v.exists(tiles):
                        i = v.c % 2
                        need("kv_ok", v)
                        if (v + -2).exists(tiles):
                            need("inv_norms_ok", v + -2)
                        a.activation(squares[i][:, 0, :], kv[i][:, 0, :], ACT.Square, accum_out=norms2[i][:, 0:1])
                        done(a.activation(squares[i][:, 1, :], kv[i][:, 1, :], ACT.Square,
                                          accum_out=norms2[i][:, 1:2]), "norms_ok")
                    if p == 3 and (s + -2).exists(tiles):
                        need("x1_ok", s + -2)
                        done(a.copy(rows_all[:, (s + -2).number(), 0:D], x1[s.c % 2][:, :]), "x1_kept")
                    if p == 2 and s.exists(tiles):
                        need("xnT_mm", s)
                        if (s + -2).exists(tiles):
                            need("qT_mm", s + -2)
                        done(a.copy(xnT[s.c % 2][:, :, :], work_a.rearrange("p (h t) -> p h t", h=HALVES)), "xnT_ok")
                    if p == 6 and v.exists(tiles):
                        need("cT_mm", v)
                        if (v + -4).exists(tiles):
                            need("pv_mm", v + -4, 4, 4)
                        done(a.copy(vT[v.c % RING][:, :, :, 0:DH],
                                    turn_ps[:, 0, :].rearrange("p (l h d) -> p l h d", l=2, d=DH)), "vT_ok")

            run_steps(act, tiles, SKEW, step)

            phase1_over(act)
            for n in range(0, tiles // 2, 2):
                act.wait_ge(S["mT_mm"], n + 1)
                if n >= 2:
                    act.wait_ge(S["logitsT_mm"], n - 1)
                done(a.copy(mT[0][:, :, :, :].rearrange("p h b t -> p (h b t)"), banks[0]), "mT_act")
            act.wait_ge(S["logitsT_mm"], tiles // 2)
            for half in range(tiles // 16):
                done(a.copy(logitsT[:, :, :, :].rearrange("p s b t -> p (s b t)")[:, 512 * half:512 * (half + 1)],
                            banks[2 + half]), "logitsT_ok")
            act.wait_ge(S["route_dve"], before_exp)
            done(a.activation(route["prob"][:, :, :], route["p0"][:, :, :], ACT.Exp), "prob_ok")

            def turn(e, par):
                for n in range(0, len(xT_parts), 2):
                    first, size = xT_parts[n]
                    act.wait_ge(S["xT_mm"], e * len(xT_parts) + (n + 1))
                    done(a.copy(xT[par][:, :, P * first:P * (first + size)],
                                banks[6][:, 0:HALVES * P * size].rearrange("p (h t) -> p h t", h=HALVES)), "xT_act")

            def hidden(e, par, g):
                first, size = groups[g]
                for f in range(0, FF, 2):
                    m = g * FF + f
                    act.wait_ge(S["h_mm"], e * (len(groups) * FF) + (m + 1))
                    if f == 0:
                        wait_past(act, S["y_mm"], hT_free(e, g))
                    done(a.activation(hT[g % 2][:, f, 0:P * size], banks[m % 4][:, 0:P * size], ACT.Relu), "h_act")

            def outputs(e, par, g):
                for q, first, size in chunks_of(g):
                    if q % 2 == 0:
                        act.wait_ge(S["y_mm"], e * len(y_chunks) + (q + 1))
                        act.wait_ge(S["meta_ok"], e + 1)
                        for b in range(size):
                            n = first + b
                            wait_past(act, add_dma[n % Y_RING], e * (16 * y_uses) + 16 * (n // Y_RING))
                            done(a.activation(y[n % Y_RING][:, :], banks[4][:, D * b:D * (b + 1)], ACT.Copy,
                                              scale=y_gate[par][:, n:n + 1]), "y_act")

            def expert(k, e, par, more):
                hidden(e, par, 0)
                for g in range(1, len(groups)):
                    hidden(e, par, g)
                    outputs(e, par, g - 1)
                    if g == 1 and more:
                        turn(e + 1, 1 - par)
                outputs(e, par, len(groups) - 1)

            turn(0, 0)
            run_experts(act, expert)

        @block.vector
        def _(dve):
            def need(name, t, per_tile=1, n=1):
                dve.wait_ge(S[name], t.count(per_tile, n))

            def done(ins, name):
                ins.then_inc(S[name], 1)

            v = nc.vector

            for i in range(RING):
                v.memset(q_op[i][:, :, :], 0.0)
                for j in range(2):
                    v.memset(k_op[i][j][64 * j:64 * j + 64, :, :], 1.0)
                    v.memset(k_op[i][j][64 - 64 * j:128 - 64 * j, :, :], 0.0)
            dve.wait_ge(S["setup_in"], 16 * SETUP_LOADS)
            v.tensor_copy(ident_bf[:, :], ident)
            for h in range(HALVES):
                v.tensor_scalar(w_in_g[:, h, :], w_in_raw[:, h, :], gamma_col[:, h:h + 1], None, ALU.mult)
                last = v.tensor_copy(beta_wide[:, h, :], beta_col[:, h:h + 1].broadcast_to([P, P]))
            done(last, "setup_dve")
            dve.wait_ge(S["setup_pe"], 1)
            v.tensor_tensor(bias_kv[:, :], scores[0][:, :, :].rearrange("p a d -> p (a d)"), bias_kv_raw[:, :], ALU.add)
            for b in range(2):
                last = v.tensor_tensor(bias_q[:, :, b], scores[1][:, 0, 0:HALVES], bias_q_raw[:, :], ALU.add)
            done(last, "setup_dve")
            dve.wait_ge(S["setup_dve"], 2)

            def stats(t, src, ok, pre, s_t, m_t):
                need(ok, t)
                done(v.bn_stats(s_t[:, :], src), pre + "_bn")
                wait_apart(dve, S[pre + "_bn"], t.count(1, 1))
                done(v.bn_aggr(m_t[:, :], s_t[:, :]), pre + "_mv_ok")
                need(pre + "_mv_ok", t)

            def x_stats_of(u):
                i = u.c % 2
                dve.wait_ge(D2["x_dma"][i], u.loads(1))
                if (u + -2).exists(tiles):
                    need("affine_ok", u + -2)
                    need("xn_ok", u + -2)
                done(v.bn_stats(x_stats[i][:, :], x_in[i][:, :]), "x_bn")
                wait_apart(dve, S["x_bn"], u.count(1, 1))
                done(v.bn_aggr(x_mv[i][:, :], x_stats[i][:, :]), "x_mv_ok")
                need("x_mv_ok", u)
                v.tensor_scalar(x_var[i][:, 0:1], x_mv[i][:, 1:2], 1.0, EPS, ALU.mult, ALU.add)
                v.tensor_scalar(x_var[i][:, 1:2], x_mv[i][:, 1:2], 1.0 + EPS, EPS * EPS, ALU.mult, ALU.add)
                done(v.tensor_scalar(x_nmean[i][:, :], x_mv[i][:, 0:1], -1.0, None, ALU.mult), "x_var_ok")

            def reduce_head(t, p, j):
                n = 2 * p + j + 1
                need("scores_mm", t, 16, n)
                done(v.tensor_reduce(neg_max[p // 4][:, j, 2 * (p % 4):2 * (p % 4) + 2], scores[j][:, :, :], AX.X, ALU.max,
                                     negate=True), "row_max_ok")

            def step(s):
                B = s + -3
                for p in range(PAIRS):
                    if B.exists(tiles):
                        reduce_head(B, p, 0)
                    if p in (0, 4):
                        t, g = max_group(s, p)
                        if t.exists(tiles):
                            need("max_mm", t, 2, g + 1)
                            if (t + -1).exists(tiles):
                                dve.wait_ge(D2["max_dma"][g], (t + -1).count(32, 32))
                            done(v.tensor_copy(max_rows[g][:, :], max_ps), "max_rows_ok")
                    if p == 1 and (s + -2).exists(tiles):
                        t = s + -2
                        i = t.c % 2
                        need("wo_mm", t)
                        need("base_ok", t)
                        if (t + -2).exists(tiles):
                            need("q_full_ok", t + -2)
                            need("x1_kept", t + -2)
                        done(v.tensor_tensor(x1[i][:, :], work_a, base[i][:, :], ALU.add), "x1_ok")
                    if p == 2 and (s + -2).exists(tiles):
                        t = s + -2
                        i = t.c % 2
                        stats(t, x1[i][:, :], "x1_ok", "q", q_stats, q_mv)
                        if (t + -2).exists(tiles):
                            need("q_full_ok", t + -2)
                        v.tensor_scalar(q_var[i][:, :], q_mv[:, 1:2], float(DH), DH * EPS, ALU.mult, ALU.add)
                        done(v.tensor_scalar(q_nmean[i][:, :], q_mv[:, 0:1], -1.0, None, ALU.mult), "q_var_ok")
                    if p == 3 and (s + 1).exists(tiles):
                        x_stats_of(s + 1)
                    if p == 5 and s.exists(tiles):
                        i = s.c % 2
                        if (s + -2).exists(tiles):
                            need("kv_prod_ok", s + -2)
                            need("norms_ok", s + -2)
                        need("kv_mm", s)
                        done(v.tensor_tensor(kv[i][:, :, :], work[:, :, :], bias_kv[:, :].rearrange(
                            "p (a d) -> p a d", a=2), ALU.add), "kv_ok")
                    if p == 6 and (s + -6).exists(tiles):
                        t = s + -6
                        i = t.c % 2
                        need("attn_ok", t)
                        need("x1_kept", t)
                        if (t + -2).exists(tiles):
                            dve.wait_ge(D2["x2_dma"][i], (t + -2).loads(1))
                        done(v.scalar_tensor_tensor(x2[i][:, :], attn[i][:, :], xgamma[:, :], rows_all[:, t.number(), 0:D],
                                                    ALU.mult, ALU.add), "x2_ok")
                        stats(t, x2[i][:, :], "x2_ok", "m", m_stats, m_mv)
                        v.tensor_scalar(m_var[i][:, :], m_mv[:, 1:2], 1.0, EPS, ALU.mult, ALU.add)
                        done(v.tensor_scalar(m_nmean[i][:, :], m_mv[:, 0:1], -1.0, None, ALU.mult), "m_var_ok")
                    if B.exists(tiles):
                        reduce_head(B, p, 1)
                    if p == 6 and (s + -1).exists(tiles):
                        t = s + -1
                        i = t.c % 2
                        need("a_mm", t)
                        if (t + -2).exists(tiles):
                            need("y_ok", t + -2)
                        done(v.tensor_scalar(a_scale[i][:, :, :], work_b[:, 0:4].rearrange("p (h b) -> p h b", h=HALVES),
                                             0.5, 0.5, ALU.mult, ALU.add), "a_scale_ok")
                        need("a_scale_ok", t)
                        done(v.tensor_tensor(a_bias[i][:, :, :], a_scale[i][:, :, :], bias_q[:, :, :], ALU.mult),
                             "a_bias_ok")
                    if B.exists(tiles):
                        if p % 4 == 3:
                            g = p // 4
                            need("row_max_ok", B, 16, 2 * p + 2)
                            if (B + -1).exists(tiles):
                                need("max_mm", B + -1, 2, g + 1)
                            done(v.tensor_copy(max_parts[g][:, :, 0, :], neg_max[g][:, :, :]), "max_hi_ok")
                            need("max_hi_ok", B, 2, g + 1)
                            done(v.tensor_tensor(max_parts[g][:, :, 1, :], neg_max[g][:, :, :],
                                                 max_parts[g][:, :, 0, :], ALU.subtract), "max_mid_ok")
                    if p == 4:
                        t = s + -5
                        if t.exists(tiles):
                            i = t.c % 2
                            dve.wait_ge(D2["sums_dma"][i], t.loads(1))
                            if (t + -2).exists(tiles):
                                dve.wait_ge(D2["inverses_dma"][i], (t + -2).loads(1))
                            done(v.reciprocal(inv_sums[i][:, :], sums[i][:, :]), "inv_sums_ok")
                    if p == 7:
                        t = s + -6
                        if t.exists(tiles):
                            need("m_rstd_ok", t)
                            done(v.tensor_scalar(rows_all[:, t.number(), 0:D], x2[t.c % 2][:, :], m_nmean[t.c % 2][:, :],
                                                 m_rstd[t.c % 2][:, :], ALU.add, ALU.mult), "m_ok")

            x_stats_of(Tile(None, 0))
            run_steps(dve, tiles, SKEW, step)

            phase1_over(dve)
            for n in range(1, tiles // 2, 2):
                dve.wait_ge(S["mT_mm"], n + 1)
                if n >= 2:
                    dve.wait_ge(S["logitsT_mm"], n - 1)
                done(v.tensor_copy(mT[1][:, :, :, :].rearrange("p h b t -> p (h b t)"), banks[1]), "mT_dve")

            links = [0]

            def link(ins):
                links[0] += 1
                ins.then_inc(S["route_dve"], 1)
                dve.wait_ge(S["route_dve"], links[0])

            def wide(name):
                return flat[name][:, :].rearrange("p (t o) -> p t o", o=1).broadcast_to([P, tiles, EXPERTS])

            def per_token(row):
                return row.rearrange("p (o e) -> p o e", o=1).broadcast_to([P, tiles, EXPERTS])

            r = {n: route[n][:, :, :] for n in route}
            v.tensor_copy(rows_all[:, :, TOKEN_ID], token_no)
            dve.wait_ge(S["logit_mm"], 1)
            for slot in range(tiles // 8):
                ps = banks[4 + slot // 2][:, D * (slot % 2):D * (slot % 2 + 1)].rearrange("p (b c e) -> p b c e", b=2, c=4)
                last = v.tensor_copy(route["logit"][:, 8 * slot:8 * slot + 8, :].rearrange("p (c b) e -> p b c e", b=2),
                                     ps[:, :, :, 0:EXPERTS])
            link(last)
            for k, (src, hot) in enumerate((("logit", "hot0"), ("rest", "hot1"))):
                link(v.tensor_reduce(flat[f"top{k}"][:, :], r[src], AX.X, ALU.max))
                link(v.tensor_tensor(r["t0"], r[src], wide(f"top{k}"), ALU.is_equal))
                link(v.scalar_tensor_tensor(r["key"], r["t0"], -100.0, per_token(expert_no), ALU.mult, ALU.add))
                link(v.tensor_reduce(flat[f"id{k}"][:, :], r["key"], AX.X, ALU.min))
                link(v.tensor_tensor(r[hot], r["key"], wide(f"id{k}"), ALU.is_equal))
                if k == 0:
                    v.tensor_tensor(r["p0"], r["logit"], wide("top0"), ALU.subtract)
                    link(v.scalar_tensor_tensor(r["rest"], r["hot0"], -3.0e38, r["logit"], ALU.mult, ALU.add))
            link(v.tensor_tensor(r["both"], r["hot0"], r["hot1"], ALU.add))
            assert links[0] == before_count
            dve.wait_ge(S["prob_ok"], 1)
            v.tensor_reduce(flat["z"][:, :], r["prob"], AX.X, ALU.add)
            link(v.tensor_tensor(r["g0"], r["both"], r["prob"], ALU.mult))
            link(v.reciprocal(flat["rz"][:, :], flat["z"][:, :]))
            v.tensor_tensor(rows_all[:, :, GATES:ROW], r["g0"], wide("rz"), ALU.mult)
            dve.wait_ge(S["count_mm"], 1)
            link(v.tensor_copy(per_expert["total"][:, :, :],
                               banks[1][:, 0:EXPERTS * tiles].rearrange("p (t e) -> p e t", e=EXPERTS)))
            link(v.tensor_tensor_scan(per_expert["through"][:, :, :].rearrange("p e t -> p (e t)"), not_first,
                                      per_expert["total"][:, :, :].rearrange("p e t -> p (e t)"), 0.0,
                                      ALU.mult, ALU.add))
            link(v.tensor_tensor(per_expert["before"][:, :, :], per_expert["through"][:, :, :],
                                 per_expert["total"][:, :, :], ALU.subtract))
            link(v.tensor_tensor(r["pos"], banks[0][:, 0:EXPERTS * tiles].rearrange("p (t e) -> p t e", e=EXPERTS),
                                 per_expert["before"][:, :, :].rearrange("p e t -> p t e"), ALU.add))
            v.tensor_tensor(r["slot"], r["pos"], per_token(expert_base), ALU.add)
            link(v.tensor_scalar(r["e0"], r["pos"], float(capacity), FAR, ALU.is_ge, ALU.mult))
            link(v.tensor_tensor(r["e1"], r["e0"], r["slot"], ALU.add))
            v.tensor_tensor(r["t0"], r["hot0"], r["e1"], ALU.mult)
            link(v.tensor_tensor(r["t1"], r["hot1"], r["e1"], ALU.mult))
            for k in range(TOP_K):
                last = v.tensor_reduce(flat[f"slot{k}"][:, :], r[f"t{k}"], AX.X, ALU.add)
            link(last)
            for k in range(TOP_K):
                last = v.tensor_copy(slot_no[k][:, :], flat[f"slot{k}"][:, :])
            done(last, "slot_ok")

            def turn(k, e, par):
                dve.wait_ge(slots_dma[par], 16 * k + 16)
                for i in range(Y_RING):
                    wait_past(dve, add_dma[i], (e - 1) * (16 * y_uses))
                wait_past(dve, S["y_act"], (e - 1) * n_y[0])
                v.tensor_copy(y_id[par][:, :], slots_in[par][:, :, TOKEN_ID])
                done(v.tensor_copy(y_gate[par][:, :], slots_in[par][:, :, bass.ds(GATES + e, 1)].rearrange(
                    "p n o -> p (n o)")), "meta_ok")
                for n in range(1, len(xT_parts), 2):
                    first, size = xT_parts[n]
                    dve.wait_ge(S["xT_mm"], e * len(xT_parts) + (n + 1))
                    done(v.tensor_copy(xT[par][:, :, P * first:P * (first + size)],
                                       banks[7][:, 0:HALVES * P * size].rearrange("p (h t) -> p h t", h=HALVES)), "xT_dve")

            def hidden(e, par, g):
                first, size = groups[g]
                for f in range(1, FF, 2):
                    m = g * FF + f
                    dve.wait_ge(S["h_mm"], e * (len(groups) * FF) + (m + 1))
                    if f == 1:
                        wait_past(dve, S["y_mm"], hT_free(e, g))
                    done(v.tensor_scalar(hT[g % 2][:, f, 0:P * size], banks[m % 4][:, 0:P * size], 0.0, None, ALU.max),
                         "h_dve")

            def outputs(e, par, g):
                for q, first, size in chunks_of(g):
                    if q % 2:
                        dve.wait_ge(S["y_mm"], e * len(y_chunks) + (q + 1))
                        dve.wait_ge(S["meta_ok"], e + 1)
                        for b in range(size):
                            n = first + b
                            wait_past(dve, add_dma[n % Y_RING], e * (16 * y_uses) + 16 * (n // Y_RING))
                            done(v.tensor_scalar(y[n % Y_RING][:, :], banks[5][:, D * b:D * (b + 1)],
                                                 y_gate[par][:, n:n + 1], None, ALU.mult), "y_dve")

            def expert(k, e, par, more):
                hidden(e, par, 0)
                for g in range(1, len(groups)):
                    hidden(e, par, g)
                    outputs(e, par, g - 1)
                    if g == 1 and more:
                        turn(k + par, e + 1, 1 - par)
                outputs(e, par, len(groups) - 1)

            turn(0, 0, 0)
            run_experts(dve, expert)

        @block.tensor
        def _(pe):
            def need(name, t, per_tile=1, n=1):
                pe.wait_ge(S[name], t.count(per_tile, n))

            def done(ins, name):
                ins.then_inc(S[name], 1)

            mm = nc.tensor.matmul

            pe.wait_ge(S["setup_dve"], 1)
            for h in range(HALVES):
                mm(scores[0][:, :, :].rearrange("p a d -> p (a d)"), beta_wide[:, h, :], w_in_raw[:, h, D:3 * D],
                   start=h == 0, stop=h == HALVES - 1)
            for o in range(HALVES):
                for h in range(HALVES):
                    last = mm(scores[1][:, 0, o:o + 1], w_in_raw[:, h, P * o:P * (o + 1)], beta_col[:, h:h + 1],
                              start=h == 0, stop=h == HALVES - 1)
            done(last, "setup_pe")
            pe.wait_ge(S["setup_pool"], 1)
            pe.wait_ge(S["setup_dve"], 2)

            def max_turn(s, p):
                t, g = max_group(s, p)
                if t.exists(tiles):
                    need("max_mid_ok", t, 2, g + 1)
                    if g or (t + -1).exists(tiles):
                        before, gb = (t, 0) if g else (t + -1, 1)
                        need("max_rows_ok", before, 2, gb + 1)
                    if g == 1:
                        if (t + 2).exists(tiles):
                            need("vT_ok", t + 2)
                    done(nc.tensor.transpose(max_ps, max_parts[g][:, :, :, :].rearrange(
                        "p j m q -> p (j m q)"), ident_bf[:, :]), "max_mm")

            def scores_mms(B, p, j):
                if B.exists(tiles):
                    if p == 0 and j == 0:
                        pe.wait_ge(D2["q_op_dma"][B.c % 2], B.loads(2))
                        pe.wait_ge(D2["k_op_dma"][B.c % 2], B.loads(2))
                    if B.it is not None or B.c > 0 or p > 0:
                        need("row_max_ok", B, 16, 2 * p + j - 1)
                    rows = slice(0, 64 * j + OPK)
                    for h in range(2):
                        last = mm(scores[j][:, h, :], q_op[B.c % RING][rows, p, P * h:P * (h + 1)],
                                  k_op[B.c % RING][j][rows, p, :], start=True, stop=True)
                    done(last, "scores_mm")

            def scoresT_mms(t, pc, j):
                if t.exists(tiles):
                    if pc % 4 == 0 and j == 0:
                        pe.wait_ge(D2["max_dma"][pc // 4], t.count(32, 32))
                    n = 2 * pc + j
                    if n >= 3:
                        need("probs_ok", t, 16, n - 2)
                    elif (t + -1).exists(tiles):
                        need("probs_ok", t + -1, 16, (16, 14, 15)[n])
                    for h in range(2):
                        last = mm(scoresT[n % 3][:, h, :], k_op[t.c % RING][j][:, pc, P * h:P * (h + 1)],
                                  q_op[t.c % RING][:, pc, :], start=True, stop=True)
                    done(last, "scoresT_mm")

            def pv_mms(s, p, h):
                t, g = (s + -4, p // 2 - 1) if p else (s + -5, 3)
                if t.exists(tiles):
                    if h == 0:
                        need("probs_ok", t, 16, 4 * g + 4)
                        need("vT_ok", t)
                        if g % 2 == 0 and (t.it is not None or 2 * t.c + g // 2 >= 1):
                            need("pv_ok", t, 2, g // 2)
                    for c in range(4):
                        j, pair = c % 2, 2 * g + c // 2
                        last = mm(pv_ps[32 * c:32 * c + 32, g % 2, :], vT[t.c % RING][:, h, HEADS * j + pair, :],
                                  probs[(2 * pair + j) % PROBS][:, h, :], start=h == 0, stop=h == 1,
                                  skip_group_check=True)
                    if h:
                        done(last, "pv_mm")

            def step(s):
                B, v, u = s + -3, s + -1, s + -2
                for p in range(PAIRS):
                    for j in range(2):
                        scores_mms(B, p, j)
                        scoresT_mms(s + -4, p, j)
                        if p in (0, 4) and j == 0:
                            max_turn(s, p)
                        if (p % 2, j) == (0, 1):
                            pv_mms(s, p, 0)
                        if (p % 2, j) == (1, 0):
                            pv_mms(s, p - 1, 1)
                        if (p, j) == (0, 0) and u.exists(tiles):
                            need("y_ok", u)
                            if v.exists(tiles):
                                need("kv_ok", v)
                            for h in range(HALVES):
                                last = mm(work_a, yT[u.c % 2][:, h, :], w_out_sb[:, h, :], start=h == 0, stop=h == 1)
                            done(last, "wo_mm")
                        if (p, j) == (2, 0) and s.exists(tiles):
                            need("xn_ok", s)
                            if v.exists(tiles):
                                need("kv_ok", v)
                            if u.exists(tiles):
                                need("x1_ok", u)
                            for h in range(HALVES):
                                last = nc.tensor.transpose(work_a[:, P * h:P * (h + 1)],
                                                           xn[s.c % 2][:, P * h:P * (h + 1)], ident)
                            done(last, "xnT_mm")
                        if (p, j) in ((3, 1), (4, 0)) and s.exists(tiles):
                            need("xnT_ok", s)
                            h = 1 - j
                            last = mm(work[:, :, :].rearrange("p a d -> p (a d)"), xnT[s.c % 2][:, h, :],
                                      w_in_g[:, h, D:3 * D], start=h == 0, stop=h == 1)
                            if h:
                                done(last, "kv_mm")
                        if (p, j) == (5, 1) and v.exists(tiles):
                            need("c_parts_ok", v)
                            if B.exists(tiles):
                                need("max_rows_ok", B, 2, 1)
                            for h in range(HALVES):
                                last = nc.tensor.transpose(turn_ps[:, 0, P * h:P * (h + 1)],
                                                           c_in[v.c % RING][:, P * h:P * (h + 1)], ident)
                            done(last, "cT_mm")
                        if (p, j) in ((5, 1), (6, 0)) and v.exists(tiles):
                            i, o = v.c % 2, 1 - j
                            if o == 0 and s.exists(tiles):
                                need("kv_ok", s)
                            for h in range(HALVES):
                                last = mm(work_a[:, P * o:P * (o + 1)], w_in_g[:, h, P * o:P * (o + 1)],
                                          xnT[i][:, h, :], start=h == 0, stop=h == 1)
                            if o:
                                done(last, "qT_mm")
                                need("kv_prod_ok", v)
                                need("row_weight_ok", v)
                                for h in range(HALVES):
                                    last = mm(work_b[:, 2 * h:2 * h + 2], kv_prod[i][:, P * h:P * (h + 1)],
                                              row_weight[i][:, :], start=True, stop=True)
                                done(last, "a_mm")

            run_steps(pe, tiles, SKEW, step)

            transpose = nc.tensor.transpose
            phase1_over(pe)
            pe.wait_ge(S["wg_dma"], 16)
            mT_sems = (S["mT_act"], S["mT_dve"])
            for n in range(tiles // 2 + 1):
                if n < tiles // 2:
                    if n >= 2:
                        pe.wait_ge(mT_sems[n % 2], n // 2)
                    for h in range(HALVES):
                        for b in range(2):
                            last = transpose(banks[n % 2][:, D * h + P * b:D * h + P * (b + 1)],
                                             rows_all[:, 2 * n + b, P * h:P * (h + 1)], ident_keep[:, :])
                    done(last, "mT_mm")
                if n > 0:
                    m = n - 1
                    pe.wait_ge(mT_sems[m % 2], m // 2 + 1)
                    c, slot = m % 4, m // 4
                    for h in range(HALVES):
                        last = mm(banks[2 + slot // 2][32 * c:32 * c + 32, D * (slot % 2):D * (slot % 2 + 1)],
                                  wg_sb[:, h, :], mT[m % 2][:, h, :, :].rearrange("p b t -> p (b t)"),
                                  start=h == 0, stop=h == 1, skip_group_check=True)
                    done(last, "logitsT_mm")
            pe.wait_ge(S["logitsT_ok"], tiles // 16)
            for slot in range(tiles // 8):
                for b in range(2):
                    last = transpose(banks[4 + slot // 2][:, D * (slot % 2) + P * b:D * (slot % 2) + P * (b + 1)],
                                     logitsT[:, slot, b, :], ident_keep[:, :])
            done(last, "logit_mm")
            pe.wait_ge(S["route_dve"], before_count)
            for i, which in enumerate((earlier, ones[:, :])):
                last = mm(banks[i][:, 0:EXPERTS * tiles], which, route["both"][:, :, :].rearrange("p t e -> p (t e)"),
                          start=True, stop=True)
            done(last, "count_mm")

            def turn(k, e, par):
                pe.wait_ge(slots_dma[par], 16 * k + 16)
                for n, (first, size) in enumerate(xT_parts):
                    wait_past(pe, S[("xT_act", "xT_dve")[n % 2]], e * n_xT[n % 2] + n // 2)
                    for h in range(HALVES):
                        for b in range(size):
                            last = transpose(banks[6 + n % 2][:, P * (size * h + b):P * (size * h + b + 1)],
                                             slots_in[par][:, first + b, P * h:P * (h + 1)], ident_keep[:, :])
                    done(last, "xT_mm")

            def hidden(e, par, g):
                first, size = groups[g]
                for f in range(FF):
                    m = g * FF + f
                    wait_past(pe, S[("h_act", "h_dve")[f % 2]], e * n_h + (m // 2 - 1))
                    for h in range(HALVES):
                        last = mm(banks[m % 4][:, 0:P * size], w1_sb[par][:, h, P * f:P * (f + 1)],
                                  xT[par][:, h, P * first:P * (first + size)], start=h == 0, stop=h == 1)
                    done(last, "h_mm")

            def outputs(e, par, g):
                for name in ("h_act", "h_dve"):
                    pe.wait_ge(S[name], e * n_h + (g + 1) * FF // 2)
                for q, first, size in chunks_of(g):
                    wait_past(pe, S[("y_act", "y_dve")[q % 2]], e * n_y[q % 2] + y_before(q))
                    for b in range(size):
                        o = P * (first + b - groups[g][0])
                        for f in range(FF):
                            last = mm(banks[4 + q % 2][:, D * b:D * (b + 1)], hT[g % 2][:, f, o:o + P],
                                      w2_sb[par][:, f, :], start=f == 0, stop=f == FF - 1)
                    done(last, "y_mm")

            def expert(k, e, par, more):
                pe.wait_ge(w_dma[par], 32 * k + 32)
                pe.wait_ge(S["xT_act"], (e + 1) * n_xT[0])
                pe.wait_ge(S["xT_dve"], (e + 1) * n_xT[1])
                hidden(e, par, 0)
                for g in range(1, len(groups)):
                    hidden(e, par, g)
                    outputs(e, par, g - 1)
                    if g == 1 and more:
                        turn(k + par, e + 1, 1 - par)
                outputs(e, par, len(groups) - 1)

            turn(0, 0, 0)
            run_experts(pe, expert)


_INS = ["x", "ctx_2048", "L0_attn_W_in", "L0_attn_b_in", "L0_attn_W_out", "L0_attn_b_out", "L0_attn_gamma",
        "L0_attn_beta", "L0_xattn_gamma", "L0_ffn_Wg", "L0_ffn_w1", "L0_ffn_w2"]


def constants():
    import numpy as np
    rot = D // 2
    inv_freq = (1.0 / 10000.0 ** (np.arange(0, rot, 2, dtype=np.float32) / rot)).astype(np.float32)
    angles = np.repeat(np.arange(SEQ, dtype=np.float32)[:, None] * inv_freq[None, :], 2, axis=-1)
    cos, sin = np.cos(angles).astype(np.float32), np.sin(angles).astype(np.float32)
    sin[:, 0::2] *= -1
    both = lambda a: np.tile(np.concatenate([a, a], axis=1), (2, 1))
    mask = np.zeros((P, 2), np.float32)
    mask[:SEQ, 0] = mask[SEQ:, 1] = 1.0
    return np.ascontiguousarray(np.concatenate([np.eye(P, dtype=np.float32), both(cos), both(sin), mask], axis=1))


def route_constants(tiles):
    import numpy as np
    capacity = -(-5 * tiles * P * TOP_K // (4 * EXPERTS))
    row = np.arange(P)[:, None]
    earlier = row < np.arange(P)[None, :]
    not_first = np.tile(np.arange(tiles) > 0, EXPERTS)[None, :].repeat(P, 0)
    experts = np.arange(EXPERTS)[None, :].repeat(P, 0)
    return np.ascontiguousarray(np.concatenate([earlier, not_first, experts, experts * capacity,
                                                row + P * np.arange(tiles)[None, :]], axis=1).astype(np.float32))


def kernel(**inputs):
    import numpy as np
    import concourse.bacc as bacc
    from concourse.bass_utils import run_bass_kernel_spmd

    nc = bacc.Bacc("TRN2", target_bir_lowering=False, num_devices=1)
    tiles = inputs["x"].shape[0] * SEQ // P
    laid_out = {name: np.ascontiguousarray(inputs[name]) for name in _INS}
    laid_out["L0_xattn_gamma"] = laid_out["L0_xattn_gamma"].reshape(1)
    laid_out["constants"] = constants()
    laid_out["route_constants"] = route_constants(tiles)
    arrays, args = {}, []
    for name, a in laid_out.items():
        arrays[f"in_{name}"] = a
        args.append(nc.dram_tensor(f"in_{name}", a.shape, mybir.dt.from_np(a.dtype), kind="ExternalInput").ap())
    args.append(nc.dram_tensor("out_0", (tiles * P, D), mybir.dt.float32, kind="ExternalOutput").ap())
    decoder_block(nc, tiles, *args)
    r = run_bass_kernel_spmd(nc, [arrays], core_ids=[0])
    return r.results[0]["out_0"].reshape(inputs["x"].shape)
```

```python
import concourse.bass as bass
from concourse import mybir
from contextlib import ExitStack

P = 128
D = 256
HALVES = D // P
SEQ = 64
HEADS = 8
DH = SEQ // HEADS
PAIRS = HEADS
TERMS = 6
OPK = TERMS * DH
EPS = 1e-5
RING = 4
SKEW = 7
PROBS = 8
EXPERTS = 8
TOP_K = 2
D_FF = 1024
FF = D_FF // P
TOKEN_ID = D
GATES = D + 1
ROW = GATES + EXPERTS
Y_RING = 5
FAR = 1.0e6

TWO_BF16_ONES = 1.0 + 0x3F80 / 2 ** 23


class Tile:

    def __init__(self, it, c):
        self.it, self.c = it, c

    def __add__(self, n):
        return Tile(self.it, self.c + n)

    def exists(self, tiles):
        return self.it is not None or 0 <= self.c < tiles

    def number(self):
        return self.c if self.it is None else self.it * RING + self.c

    def count(self, per_tile, n):
        fixed = per_tile * self.c + n
        return fixed if self.it is None else self.it * (RING * per_tile) + fixed

    def loads(self, dmas):
        fixed = 16 * dmas * (self.c // 2 + 1)
        return fixed if self.it is None else self.it * (16 * dmas * RING // 2) + fixed


def run_steps(engine, tiles, skew, step):
    for s in range(2 * RING):
        step(Tile(None, s))
    with engine.Fori(2, tiles // RING - 1) as it:
        for c in range(RING):
            step(Tile(it, c))
    for s in range(tiles - RING, tiles + skew):
        step(Tile(None, s))


def decoder_block(nc, tiles, x, ctx_in, w_in, b_in, w_out, b_out, ln_gamma, ln_beta, xattn_gamma, wg, w1, w2,
                  consts, route_consts, out):
    F32, BF16, F32R = mybir.dt.float32, mybir.dt.bfloat16, mybir.dt.float32r
    ALU, ACT, AX = mybir.AluOpType, mybir.ActivationFunctionType, mybir.AxisListType

    x_tiles = x.rearrange("(t b) s d -> t (b s) d", b=2)
    ctx_tiles = ctx_in.rearrange("(t b) s d -> t (b s) d", b=2)
    out_tiles = out[0:tiles * P, :].rearrange("(t p) d -> t p d", p=P)
    w_in_v = w_in.rearrange("(c p) n -> p c n", p=P)
    w_out_v = w_out.rearrange("(c p) n -> p c n", p=P)
    half_rows = "(c p) -> p c"

    def dram(name, shape, dtype):
        return nc.dram_tensor(name, shape, dtype, kind="Internal").ap()

    q_terms = [dram(f"q_terms{i}", (P, TERMS, D), BF16) for i in range(2)]
    k_terms = [dram(f"k_terms{i}", (P, TERMS, D), BF16) for i in range(2)]
    attended = [dram(f"attended{i}", (2 * HEADS, DH + 1, D), F32) for i in range(2)]
    inverses = [dram(f"inverses{i}", (2 * HEADS, D), F32) for i in range(2)]

    ctx = ExitStack()
    with ctx:
        def sb(name, shape, dt=F32):
            return ctx.enter_context(nc.sbuf_tensor(name, shape, dt))

        def pb(name, shape, dt=F32):
            return ctx.enter_context(nc.psum_tensor(name, shape, dt))

        def sem(name):
            return ctx.enter_context(nc.semaphore(name))

        capacity = -(-5 * tiles * P * TOP_K // (4 * EXPERTS))
        blocks = capacity // P
        assert blocks * P == capacity and blocks % Y_RING == 0 and tiles % 8 == 0
        groups = [(b, min(2, blocks - b)) for b in range(0, blocks, 2)]
        n_slots = EXPERTS * capacity
        slots_dram = dram("slots_dram", (n_slots, ROW), F32)

        route_sb = sb("route_sb", [P, P + EXPERTS * tiles + 2 * EXPERTS + tiles + 1 + blocks])
        earlier = route_sb[:, 0:P]
        not_first = route_sb[:, P:P + EXPERTS * tiles]
        expert_no = route_sb[:, P + EXPERTS * tiles:P + EXPERTS * (tiles + 1)]
        expert_base = route_sb[:, P + EXPERTS * (tiles + 1):P + EXPERTS * (tiles + 2)]
        token_no = route_sb[:, P + EXPERTS * (tiles + 2):P + EXPERTS * (tiles + 2) + tiles]
        spare_no = route_sb[:, P + EXPERTS * (tiles + 2) + tiles:P + EXPERTS * (tiles + 2) + tiles + 1]
        block_rows = route_sb[:, P + EXPERTS * (tiles + 2) + tiles + 1:]
        ones = sb("ones", [P, P])
        wg_sb = sb("wg_sb", [P, HALVES, 32])
        ident_keep = sb("ident_keep", [P, P])
        empty_row = sb("empty_row", [P, ROW])

        no_y = sb("no_y", [P, D])
        id_shift = sb("id_shift", [P, blocks])
        y_id = [sb(f"y_id{i}", [P, blocks], mybir.dt.int32) for i in range(2)]
        y_gate = [sb(f"y_gate{i}", [P, blocks]) for i in range(2)]

        routed = ctx.enter_context(ExitStack())
        rows_all = routed.enter_context(nc.sbuf_tensor("rows_all", [P, tiles, ROW], F32))

        w_in_raw = routed.enter_context(nc.sbuf_tensor("w_in_raw", [P, HALVES, 3 * D], F32))
        mT = [w_in_raw[:, i, 0:2 * D].rearrange("p (h b t) -> p h b t", h=HALVES, b=2) for i in range(2)]
        logitsT = routed.enter_context(nc.sbuf_tensor("logitsT", [P, tiles // 8, 2, P], F32))

        phase1 = ctx.enter_context(ExitStack())

        def sb(name, shape, dt=F32):
            return phase1.enter_context(nc.sbuf_tensor(name, shape, dt))

        const_sb = sb("const_sb", [P, 128 + 256 + 256 + 2])
        ident = const_sb[:, 0:128]
        cos_kv = const_sb[:, 128:384].rearrange("p (a d) -> p a d", a=2)
        sin_kv = const_sb[:, 384:640].rearrange("p (a d) -> p a d", a=2)
        row_mask = const_sb[:, 640:642]
        ident_bf = sb("ident_bf", [P, P], BF16)
        w_in_g = sb("w_in_g", [P, HALVES, 3 * D])
        w_out_sb = sb("w_out_sb", [P, HALVES, D])
        gamma_col = sb("gamma_col", [P, HALVES])
        beta_col = sb("beta_col", [P, HALVES])
        beta_wide = sb("beta_wide", [P, HALVES, P])
        bias_kv_raw = sb("bias_kv_raw", [P, 2 * D])
        bias_kv = sb("bias_kv", [P, 2 * D])
        bias_q_raw = sb("bias_q_raw", [P, HALVES])
        bias_q = sb("bias_q", [P, HALVES, 2])
        b_out_sb = sb("b_out_sb", [P, D])
        xgamma = sb("xgamma", [P, 1])
        minus_half = sb("minus_half", [P, 2])

        x_in = [sb(f"x_in{i}", [P, D]) for i in range(2)]
        c_in = [sb(f"c_in{i}", [P, D]) for i in range(RING)]
        x_stats = [sb(f"x_stats{i}", [P, 6]) for i in range(2)]
        x_mv = [sb(f"x_mv{i}", [P, 2]) for i in range(2)]
        x_var = [sb(f"x_var{i}", [P, 2]) for i in range(2)]
        x_nmean = [sb(f"x_nmean{i}", [P, 1]) for i in range(2)]
        x_rstd = [sb(f"x_rstd{i}", [P, 2]) for i in range(2)]
        base_affine = [sb(f"base_affine{i}", [P, 2]) for i in range(2)]
        xn = [sb(f"xn{i}", [P, D]) for i in range(2)]
        base0 = [sb(f"base0{i}", [P, D]) for i in range(2)]
        base = [sb(f"base{i}", [P, D]) for i in range(2)]
        xnT = [sb(f"xnT{i}", [P, HALVES, P]) for i in range(2)]
        kv = [sb(f"kv{i}", [P, 2, D]) for i in range(2)]
        rot_cos = sb("rot_cos", [P, 2, P])
        rot_sin = sb("rot_sin", [P, 2, P])
        rot = [sb(f"rot{i}", [P, 2, P]) for i in range(2)]
        kv_prod = [sb(f"kv_prod{i}", [P, D]) for i in range(2)]
        squares = sb("squares", [P, 2, D])
        norms2 = [sb(f"norms2{i}", [P, 2]) for i in range(2)]
        inv_norms = [sb(f"inv_norms{i}", [P, 2]) for i in range(2)]
        row_weight = [sb(f"row_weight{i}", [P, 2]) for i in range(2)]
        a_scale = [sb(f"a_scale{i}", [P, HALVES, 2]) for i in range(2)]
        a_bias = [sb(f"a_bias{i}", [P, HALVES, 2]) for i in range(2)]
        yT = [sb(f"yT{i}", [P, HALVES, P]) for i in range(2)]

        x1 = [sb(f"x1{i}", [P, D]) for i in range(2)]
        q_stats = sb("q_stats", [P, 6])
        q_mv = sb("q_mv", [P, 2])
        q_var = [sb(f"q_var{i}", [P, 1]) for i in range(2)]
        q_nmean = [sb(f"q_nmean{i}", [P, 1]) for i in range(2)]
        q_rstd = [sb(f"q_rstd{i}", [P, 1]) for i in range(2)]
        q_full = [sb(f"q_full{i}", [P, D]) for i in range(2)]
        q_rest = [sb(f"q_rest{i}", [P, D]) for i in range(2)]
        q_parts = [sb(f"q_parts{i}", [P, 3, D], BF16) for i in range(2)]
        c_rest = [sb(f"c_rest{i}", [P, D]) for i in range(2)]
        c_parts = [sb(f"c_parts{i}", [P, 3, D], BF16) for i in range(2)]
        q_op = [sb(f"q_op{i}", [P, PAIRS, D], BF16) for i in range(RING)]
        k_op = [[sb(f"k_op{i}_{j}", [P, PAIRS, D], BF16) for j in range(2)] for i in range(RING)]
        vT = [sb(f"vT{i}", [P, 2, 2 * HEADS, 32]) for i in range(RING)]
        neg_max = [sb(f"neg_max{i}", [P, 2, 8]) for i in range(2)]
        max_parts = [sb(f"max_parts{i}", [P, 2, 2, 8], BF16) for i in range(2)]
        max_rows = [sb(f"max_rows{i}", [32, P], BF16) for i in range(2)]
        probs = [sb(f"probs{i}", [P, 2, D]) for i in range(PROBS)]
        pv_sb = [sb(f"pv_sb{i}", [P, 4, D]) for i in range(2)]
        sums = [sb(f"sums{i}", [P, 32]) for i in range(2)]
        inv_sums = [sb(f"inv_sums{i}", [P, 32]) for i in range(2)]
        numer = [sb(f"numer{i}", [P, D]) for i in range(2)]
        inv_wide = [sb(f"inv_wide{i}", [P, D]) for i in range(2)]
        attn = [sb(f"attn{i}", [P, D]) for i in range(2)]
        x2 = [sb(f"x2{i}", [P, D]) for i in range(2)]
        m_stats = sb("m_stats", [P, 6])
        m_mv = sb("m_mv", [P, 2])
        m_var = [sb(f"m_var{i}", [P, 1]) for i in range(2)]
        m_nmean = [sb(f"m_nmean{i}", [P, 1]) for i in range(2)]
        m_rstd = [sb(f"m_rstd{i}", [P, 1]) for i in range(2)]

        scores = [pb(f"scores{i}", [P, 2, D]) for i in range(2)]
        scoresT = [pb(f"scoresT{i}", [P, 2, D]) for i in range(3)]
        pv_ps = pb("pv_ps", [P, 2, D])
        work = pb("work", [P, 2, D])
        work_a, work_b = work[:, 0, :], work[:, 1, :]
        turn_ps = pb("turn_ps", [P, 2, D])
        max_ps = turn_ps[:, 1, 0:64].bitcast(BF16)[0:32, 0:P]

        phase1.close()

        def sb(name, shape, dt=F32):
            return routed.enter_context(nc.sbuf_tensor(name, shape, dt))

        route = {n: sb(f"r_{n}", [P, tiles, EXPERTS]) for n in
                 ("logit", "miss", "key", "hot0", "rest", "hot1", "both", "prob", "pos", "slot", "t0", "t1", "p0", "p1",
                  "e0", "e1", "g0", "g1")}
        per_expert = {n: sb(f"x_{n}", [P, EXPERTS, tiles]) for n in ("total", "through", "before")}
        flat = {n: sb(f"f_{n}", [P, tiles]) for n in
                ("top0", "top1", "id0", "id1", "z", "rz", "pos0", "pos1", "slot0", "slot1", "full0", "full1", "x0", "x1",
                 "p0", "p1", "g0", "g1")}
        slot_no = [sb(f"slot_no{k}", [P, tiles], mybir.dt.int32) for k in range(TOP_K)]
        routed.close()

        def sb(name, shape, dt=F32):
            return ctx.enter_context(nc.sbuf_tensor(name, shape, dt))

        hT_hi = [sb(f"hT_hi{i}", [P, FF, 2 * P], F32R) for i in range(2)]
        hT_lo = [sb(f"hT_lo{i}", [P, FF, 2 * P], F32R) for i in range(2)]
        xT_hi = [sb(f"xT_hi{i}", [P, HALVES, capacity], F32R) for i in range(2)]
        xT_lo = [sb(f"xT_lo{i}", [P, HALVES, capacity], F32R) for i in range(2)]
        y = [sb(f"y{i}", [P, D]) for i in range(Y_RING)]
        slots_in = sb("slots_in", [P, blocks, ROW])
        w_raw = sb("w_raw", [P, 2, HALVES * D_FF])
        w_hi = [sb(f"w_hi{i}", [P, 2, HALVES * D_FF], F32R) for i in range(2)]
        w_lo = [sb(f"w_lo{i}", [P, 2, HALVES * D_FF], F32R) for i in range(2)]

        def w1_of(w):
            return w[:, 0, :].rearrange("p (c f) -> p c f", c=HALVES)

        def w2_of(w):
            return w[:, 1, :].rearrange("p (c n) -> p c n", c=FF)

        banks = [b[:, :, :].rearrange("p a d -> p (a d)") for b in
                 (scores[0], scores[1], scoresT[0], scoresT[1], scoresT[2], pv_ps, work, turn_ps)]

        names = ["setup_in", "setup_dve", "setup_pe", "setup_pool", "x_bn", "x_mv_ok", "x_var_ok", "x_rstd_ok", "affine_ok",
                 "xn_ok", "base0_ok", "base_ok", "xnT_mm", "xnT_ok", "kv_mm", "kv_ok", "qT_mm",
                 "rot_cos_ok", "rot_sin_ok", "rot_ok", "kv_prod_ok", "norm_k_ok", "norms_ok", "inv_norms_ok", "row_weight_ok",
                 "a_mm", "a_scale_ok", "a_bias_ok", "y_ok", "wo_mm", "x1_ok", "x1_kept", "q_bn", "q_mv_ok", "q_var_ok",
                 "q_rstd_ok", "q_full_ok", "q_hi_ok", "q_rest_ok", "q_mid_ok", "q_parts_ok", "c_hi_ok", "c_rest_ok",
                 "c_mid_ok", "c_parts_ok", "cT_mm", "vT_ok", "scores_mm", "row_max_ok", "max_hi_ok", "max_mid_ok",
                 "max_mm", "max_rows_ok", "scoresT_mm", "probs_ok", "pv_mm", "pv_ok", "inv_sums_ok", "attn_ok",
                 "x2_ok", "m_bn", "m_mv_ok", "m_var_ok", "m_rstd_ok", "m_ok",
                 "fixed_ok", "blank_ok", "blank_dma", "spare_dma", "id_shift_ok", "wg_dma",
                 "mT_mm", "mT_ok", "logitsT_mm", "logitsT_ok", "logit_mm", "route_dve", "prob_ok", "count_mm",
                 "slot_ok", "scatter_dma", "xT_mm", "xT_hi_ok", "xT_lo_ok", "meta_ok",
                 "w_hi_ok", "w_lo_ok", "h_mm", "h_hi_ok", "h_lo_ok", "y_mm",
                 "y_act", "y_dve"]
        S = {n: sem(n) for n in names}
        pair_names = ["x_dma", "c_dma", "q_terms_dma", "k_terms_dma", "q_op_dma", "k_op_dma", "max_dma",
                      "attended_dma", "sums_dma", "inverses_dma", "back_dma", "x2_dma"]
        D2 = {n: [sem(f"{n}{i}") for i in range(2)] for n in pair_names}
        w_dma = sem("w_dma")
        slots_dma = sem("slots_dma")
        add_dma = [sem(f"add_dma{i}") for i in range(Y_RING)]

        block = ctx.enter_context(nc.Block())

        def scoresT_bank(n):
            return n % 3 if n < 15 else 1

        def max_group(s, p):
            return (s + -3, 0) if p else (s + -4, 1)

        SETUP_LOADS = 11
        before_exp, before_count = 7, 13
        xT_parts = [(b, min(2, blocks - b)) for b in range(0, blocks, 2)]
        y_chunks = groups
        n_y = [sum(size for _, size in y_chunks[side::2]) for side in range(2)]
        turn_at = {g: [n for n in range(len(xT_parts)) if 1 + n * (len(groups) - 1) // len(xT_parts) == g]
                   for g in range(1, len(groups))}
        all_parts = range(len(xT_parts))
        pieces = [(i, 512 * k) for i in range(2) for k in range(HALVES * D_FF // 512)]
        y_uses = blocks // Y_RING

        def y_before(q):
            return sum(size for _, size in y_chunks[q % 2:q:2])

        def hT_free(e, g):
            if g >= 2:
                return e * len(groups) + (g - 1)
            before = max(i for i in range(len(groups)) if i % 2 == g % 2)
            return (e - 1) * len(groups) + (before + 1)

        def run_experts(engine, expert):
            for par in range(2):
                expert(par, par, True)
            with engine.Fori(1, EXPERTS // 2 - 1) as it:
                for par in range(2):
                    expert(it * 2 + par, par, True)
            for par in range(2):
                expert(EXPERTS - 2 + par, par, par == 0)

        def wait_past(engine, sem, value):
            if not isinstance(value, int) or value > 0:
                engine.wait_ge(sem, value)

        def wait_apart(engine, sem, value):
            if not isinstance(value, int):
                value = engine.to_reg(value)
                engine.wait_ge(S["setup_in"], 16 * SETUP_LOADS)
            engine.wait_ge(sem, value)

        def phase1_over(engine):
            engine.wait_ge(S["m_ok"], tiles)
            for last in (tiles - 2, tiles - 1):
                engine.wait_ge(D2["x2_dma"][last % 2], Tile(None, last).loads(1))

        @block.sync
        def _(sp):
            def need(name, t, per_tile=1, n=1):
                wait_apart(sp, S[name], t.count(per_tile, n))

            def landed(name, t, dmas):
                wait_apart(sp, D2[name][t.c % 2], t.loads(dmas))

            def put(name, t, dst, src):
                sp.dma_start(dst, src).then_inc(D2[name][t.c % 2], 16)

            for dst, src in ((const_sb[:, :], consts), (w_in_raw[:, :, :], w_in_v), (w_out_sb[:, :, :], w_out_v),
                             (gamma_col[:, :], ln_gamma.rearrange(half_rows, p=P)),
                             (beta_col[:, :], ln_beta.rearrange(half_rows, p=P)),
                             (bias_kv_raw[:, :], b_in[D:3 * D].partition_broadcast(P)),
                             (bias_q_raw[:, :], b_in[0:D].rearrange(half_rows, p=P)),
                             (b_out_sb[:, :], b_out.partition_broadcast(P)),
                             (xgamma[:, :], xattn_gamma.partition_broadcast(P)), (route_sb[:, :], route_consts),
                             (ident_keep[:, :], consts[:, 0:P])):
                with nc.allow_non_contiguous_dma(reason="vectors laid out over the partitions, once"):
                    sp.dma_start(dst, src).then_inc(S["setup_in"], 16)

            def write_terms(name, t, terms, parts, slots):
                for first, part, repeat in slots:
                    m = repeat if repeat > 0 else -repeat
                    src = parts[:, part:part + m, :] if repeat > 0 else \
                        parts[:, part:part + 1, :].broadcast_to([P, m, D])
                    put(name, t, terms[:, first:first + m, :], src)

            def max_rows_out(s, p):
                t, g = max_group(s, p)
                if t.exists(tiles):
                    need("max_rows_ok", t, 2, g + 1)
                    for j in range(2):
                        sp.dma_start(q_op[t.c % RING][64 * j + OPK:64 * j + OPK + 2, 4 * g:4 * g + 4, :],
                                     max_rows[g][16 * j:16 * j + 16, :]).then_inc(D2["max_dma"][g], 16)

            def load_inputs(u):
                if (u + -2).exists(tiles):
                    need("base0_ok", u + -2)
                    need("xn_ok", u + -2)
                    need("c_parts_ok", u + -2)
                if (u + -4).exists(tiles):
                    need("cT_mm", u + -4)
                put("x_dma", u, x_in[u.c % 2][:, :], x_tiles[u.number()])
                put("c_dma", u, c_in[u.c % RING][:, :], ctx_tiles[u.number()])

            load_inputs(Tile(None, 0))

            def load_weights(e):
                sp.dma_start(w1_of(w_raw), w1.rearrange("e (c p) f -> e p c f", p=P)[e]).then_inc(w_dma, 16)
                sp.dma_start(w2_of(w_raw), w2.rearrange("e (c p) n -> e p c n", p=P)[e]).then_inc(w_dma, 16)

            def step(s):
                t, u, v, w = s + -6, s + -1, s + -2, s + -5
                if s.it is None and s.c < EXPERTS:
                    sp.wait_ge(S["blank_ok"], 1)
                    sp.dma_start(slots_dram[capacity * s.c:capacity * (s.c + 1), :].rearrange("(b p) n -> p b n", p=P),
                                 empty_row[:, :].rearrange("p (o n) -> p o n", o=1).broadcast_to([P, blocks, ROW])
                                 ).then_inc(S["blank_dma"], 16)
                if s.it is None and s.c == EXPERTS - 1:
                    sp.dma_start(out[tiles * P:(tiles + blocks) * P, :].rearrange("(b p) d -> p b d", p=P),
                                 no_y[:, :].rearrange("p (o d) -> p o d", o=1).broadcast_to([P, blocks, D])
                                 ).then_inc(S["spare_dma"], 16)
                if s.it is None and s.c == 2:
                    with nc.allow_non_contiguous_dma(reason="the router's weights, once"):
                        sp.dma_start(wg_sb[:, :, 0:EXPERTS], wg.rearrange("(c p) n -> p c n", p=P)
                                     ).then_inc(S["wg_dma"], 16)
                if (s + 1).exists(tiles):
                    load_inputs(s + 1)
                if u.exists(tiles):
                    need("c_parts_ok", u)
                    if (u + -2).exists(tiles):
                        landed("k_op_dma", u + -2, 2)
                    write_terms("k_terms_dma", u, k_terms[u.c % 2], c_parts[u.c % 2],
                                ((0, 0, 3), (3, 0, 2), (5, 0, 1)))
                if t.exists(tiles):
                    landed("inverses_dma", t, 1)
                    if (t + -2).exists(tiles):
                        need("attn_ok", t + -2)
                    put("back_dma", t, numer[t.c % 2][:, :], attended[t.c % 2][:, 0:DH, :])
                    put("back_dma", t, inv_wide[t.c % 2][:, :],
                        inverses[t.c % 2].rearrange("h (o f) -> h o f", o=1).broadcast_to([2 * HEADS, DH, D]))
                max_rows_out(s, 0)
                if v.exists(tiles):
                    if (v + -4).exists(tiles):
                        need("scoresT_mm", v + -4, 16, 16)
                    landed("k_terms_dma", v, 3)
                    if v.it is None and v.c < RING:
                        sp.wait_ge(S["setup_dve"], 1)
                        if v.c >= 2:
                            sp.wait_ge(S["fixed_ok"], 5 * (v.c - 2) + 5)
                    for j in range(2):
                        put("k_op_dma", v, k_op[v.c % RING][j][64 * j:64 * j + OPK, :, :],
                            k_terms[v.c % 2][64 * j:64 * j + 64].rearrange("(h d) m f -> (d m) h f", d=DH))
                if w.exists(tiles):
                    need("pv_ok", w, 2, 2)
                    if (w + -2).exists(tiles):
                        landed("back_dma", w + -2, 2)
                        landed("sums_dma", w + -2, 1)
                    for c in range(4):
                        dst = attended[w.c % 2].rearrange("(j g q) r f -> j g q r f", j=2, q=2)[c % 2, :, c // 2]
                        put("attended_dma", w, dst.rearrange("g r f -> r g f"),
                            pv_sb[w.c % 2][32 * c:32 * c + DH + 1, :, :])
                if v.exists(tiles):
                    need("q_parts_ok", v)
                    if (v + -2).exists(tiles):
                        landed("q_op_dma", v + -2, 2)
                    write_terms("q_terms_dma", v, q_terms[v.c % 2], q_parts[v.c % 2],
                                ((0, 0, -3), (3, 1, -2), (5, 2, 1)))
                if w.exists(tiles):
                    landed("attended_dma", w, 4)
                    put("sums_dma", w, sums[w.c % 2][:, :],
                        attended[w.c % 2][:, DH, :].rearrange("h (c f) -> h c f", c=8))
                max_rows_out(s, 4)
                if v.exists(tiles):
                    landed("q_terms_dma", v, 3)
                    for j in range(2):
                        put("q_op_dma", v, q_op[v.c % RING][64 * j:64 * j + OPK, :, :],
                            q_terms[v.c % 2][64 * j:64 * j + 64].rearrange("(h d) m f -> (d m) h f", d=DH))
                if t.exists(tiles):
                    need("x2_ok", t)
                    put("x2_dma", t, out_tiles[t.number()], x2[t.c % 2][:, :])
                if w.exists(tiles):
                    need("inv_sums_ok", w)
                    if (w + -2).exists(tiles):
                        landed("back_dma", w + -2, 2)
                    put("inverses_dma", w, inverses[w.c % 2].rearrange("h (c f) -> h c f", c=8),
                        inv_sums[w.c % 2][:, :])

            run_steps(sp, tiles, SKEW, step)
            for last in (tiles - 2, tiles - 1):
                landed("x2_dma", Tile(None, last), 1)

            phase1_over(sp)
            load_weights(0)

            def load_slots(e):
                sp.dma_start(slots_in[:, :, :],
                             slots_dram[bass.ds(e * capacity, capacity), :].rearrange("(b p) n -> p b n", p=P)
                             ).then_inc(slots_dma, 16)

            def expert(e, par, more):
                if more:
                    wait_apart(sp, S["w_lo_ok"], (e + 1) * len(pieces))
                    load_weights(e + 1)
                    wait_apart(sp, S["meta_ok"], e + 1)
                    wait_apart(sp, S["xT_mm"], (e + 1) * len(xT_parts))
                    load_slots(e + 1)

            sp.wait_ge(S["scatter_dma"], 16 * TOP_K * tiles)
            load_slots(0)
            run_experts(sp, expert)
            for r in range(Y_RING):
                sp.wait_ge(add_dma[r], 16 * y_uses * EXPERTS)

        @block.gpsimd
        def _(pool):
            def need(name, t, per_tile=1, n=1):
                pool.wait_ge(S[name], t.count(per_tile, n))

            def need_apart(name, t):
                wait_apart(pool, S[name], t.count(1, 1))

            def done(ins, name):
                ins.then_inc(S[name], 1)

            g = nc.gpsimd
            g.memset(minus_half[:, :], -0.5)
            for i in range(RING):
                g.memset(vT[i][:, :, :, :], 1.0)
            g.memset(ones[:, :], 1.0)
            g.memset(wg_sb[:, :, :], 0.0)
            g.memset(empty_row[:, :], 0.0)
            g.memset(no_y[:, :], 0.0)
            done(g.memset(base_affine[0][:, :], 0.0), "setup_pool")
            pool.wait_ge(S["setup_pool"], 1)

            def fixed_rows(i):
                for n, (target, rows, value) in enumerate(
                        ((k_op[i][0], slice(0, 64), TWO_BF16_ONES), (k_op[i][0], slice(64, P), 0.0),
                         (k_op[i][1], slice(64, P), TWO_BF16_ONES), (k_op[i][1], slice(0, 64), 0.0),
                         (q_op[i], slice(0, P), 0.0))):
                    done(g.memset(target[rows, :, :].bitcast(F32), value), "fixed_ok")
                    pool.wait_ge(S["fixed_ok"], 5 * (i - 2) + n + 1)

            fixed_rows(2)
            pool.wait_ge(S["setup_in"], 16 * SETUP_LOADS)
            done(g.tensor_copy(empty_row[:, TOKEN_ID:TOKEN_ID + 1], spare_no), "blank_ok")

            def split(t, full, rest, parts, pre):
                done(g.tensor_scalar(parts[:, 0, :], full[:, :], 1.0, 1.0, ALU.mult, ALU.mult), pre + "_hi_ok")
                need(pre + "_hi_ok", t)
                done(g.tensor_tensor(rest[:, :], full[:, :], parts[:, 0, :], ALU.subtract), pre + "_rest_ok")
                need_apart(pre + "_rest_ok", t)
                done(g.tensor_scalar(parts[:, 1, :], rest[:, :], 1.0, 1.0, ALU.mult, ALU.mult), pre + "_mid_ok")
                need(pre + "_mid_ok", t)
                done(g.tensor_tensor(parts[:, 2, :], rest[:, :], parts[:, 1, :], ALU.subtract), pre + "_parts_ok")

            def step(s):
                if s.exists(tiles):
                    i = s.c % 2
                    need("x_var_ok", s)
                    done(g.tensor_tensor(x_rstd[i][:, :], x_var[i][:, :], minus_half[:, :], ALU.pow), "x_rstd_ok")
                    need_apart("x_rstd_ok", s)
                    if (s + -2).exists(tiles):
                        need_apart("xnT_mm", s + -2)
                    done(g.tensor_scalar(xn[i][:, :], x_in[i][:, :], x_nmean[i][:, :], x_rstd[i][:, 1:2],
                                         ALU.add, ALU.mult), "xn_ok")
                m = s + -7
                if m.exists(tiles):
                    i = m.c % 2
                    need("m_var_ok", m)
                    done(g.tensor_tensor(m_rstd[i][:, :], m_var[i][:, :], minus_half[:, 0:1], ALU.pow), "m_rstd_ok")
                u = s + -1
                if u.exists(tiles):
                    i = u.c % 2
                    need("kv_ok", u)
                    turned = kv[i][:, :, 0:P].rearrange("p a (n e) -> p a n e", e=2)
                    sines = sin_kv.rearrange("p a (n e) -> p a n e", e=2)
                    target = rot_sin[:, :, :].rearrange("p a (n e) -> p a n e", e=2)
                    if (u + -1).exists(tiles):
                        need("rot_ok", u + -1)
                    done(g.tensor_tensor(rot_cos[:, :, :], kv[i][:, :, 0:P], cos_kv, ALU.mult), "rot_cos_ok")
                    for e in range(2):
                        last = g.tensor_tensor(target[:, :, :, e], turned[:, :, :, 1 - e], sines[:, :, :, e], ALU.mult)
                    done(last, "rot_sin_ok")
                    if (u + -2).exists(tiles):
                        need("a_mm", u + -2)
                    g.tensor_tensor(kv_prod[i][:, P:D], kv[i][:, 0, P:D], kv[i][:, 1, P:D], ALU.mult)
                    need("rot_cos_ok", u)
                    need("rot_sin_ok", u)
                    done(g.tensor_tensor(rot[i][:, :, :], rot_cos[:, :, :], rot_sin[:, :, :], ALU.add), "rot_ok")
                    need("norms_ok", u)
                    done(g.tensor_tensor(inv_norms[i][:, :], norms2[i][:, :], minus_half[:, :], ALU.pow), "inv_norms_ok")
                    need("rot_ok", u)
                    done(g.tensor_tensor(kv_prod[i][:, 0:P], rot[i][:, 0, :], rot[i][:, 1, :], ALU.mult), "kv_prod_ok")
                    need_apart("inv_norms_ok", u)
                    done(g.tensor_scalar(row_weight[i][:, :], row_mask, inv_norms[i][:, 0:1], inv_norms[i][:, 1:2],
                                         ALU.mult, ALU.mult), "row_weight_ok")
                v = s + -2
                if v.exists(tiles):
                    i = v.c % 2
                    need("q_var_ok", v)
                    done(g.tensor_tensor(q_rstd[i][:, :], q_var[i][:, :], minus_half[:, 0:1], ALU.pow), "q_rstd_ok")
                    need_apart("q_rstd_ok", v)
                    done(g.tensor_scalar(q_full[i][:, :], x1[i][:, :], q_nmean[i][:, :], q_rstd[i][:, :],
                                         ALU.add, ALU.mult), "q_full_ok")
                    if (v + -2).exists(tiles):
                        wait_apart(pool, D2["q_terms_dma"][i], (v + -2).loads(3))
                    need_apart("q_full_ok", v)
                    split(v, q_full[i], q_rest[i], q_parts[i], "q")
                t = s + -6
                if t.exists(tiles):
                    i = t.c % 2
                    pool.wait_ge(D2["back_dma"][i], t.loads(2))
                    if (t + -2).exists(tiles):
                        need("x2_ok", t + -2)
                    done(g.tensor_tensor(attn[i][:, :], numer[i][:, :], inv_wide[i][:, :], ALU.mult), "attn_ok")
                if s.exists(tiles):
                    i = s.c % 2
                    g.tensor_scalar(base_affine[i][:, 0:1], x_rstd[i][:, 0:1], 1.0, 1.0, ALU.mult, ALU.add)
                    done(g.tensor_tensor(base_affine[i][:, 1:2], x_rstd[i][:, 0:1], x_nmean[i][:, :], ALU.mult),
                         "affine_ok")
                    wait_apart(pool, D2["c_dma"][i], s.loads(1))
                    if (s + -2).exists(tiles):
                        need_apart("x1_ok", s + -2)
                        wait_apart(pool, D2["k_terms_dma"][i], (s + -2).loads(3))
                    need_apart("affine_ok", s)
                    done(g.tensor_scalar(base0[i][:, :], x_in[i][:, :], base_affine[i][:, 0:1],
                                         base_affine[i][:, 1:2], ALU.mult, ALU.add), "base0_ok")
                    split(s, c_in[s.c % RING], c_rest[i], c_parts[i], "c")
                    need("base0_ok", s)
                    done(g.tensor_tensor(base[i][:, :], base0[i][:, :], b_out_sb[:, :], ALU.add), "base_ok")
                if s.it is None and s.c == 0:
                    need("base_ok", s)
                    fixed_rows(3)

            pool.wait_ge(S["blank_ok"], 1)
            run_steps(pool, tiles, SKEW, step)

            pool.wait_ge(S["blank_dma"], 16 * EXPERTS)
            pool.wait_ge(S["slot_ok"], 1)
            pool.wait_ge(S["spare_dma"], 16)
            for k in range(TOP_K):
                for t in range(tiles):
                    g.indirect_dma_start(
                        out=slots_dram[:, :], out_offset=bass.IndirectOffsetOnAxis(ap=slot_no[k][:, t:t + 1], axis=0),
                        in_=rows_all[:, t, :], in_offset=None, bounds_check=n_slots - 1, oob_is_err=False
                    ).then_inc(S["scatter_dma"], 16)
            for last in (tiles - 2, tiles - 1):
                pool.wait_ge(D2["x2_dma"][last % 2], Tile(None, last).loads(1))

            def expert(e, par, more):
                for r in range(Y_RING):
                    wait_past(pool, add_dma[r], e * (16 * y_uses))
                pool.wait_ge(S["meta_ok"], e + 1)
                for q, (first, size) in enumerate(y_chunks):
                    for b in range(size):
                        n = first + b
                        wait_apart(pool, S[("y_act", "y_dve")[q % 2]], e * n_y[q % 2] + (y_before(q) + b + 1))
                        g.indirect_dma_start(
                            out=out[:, :], out_offset=bass.IndirectOffsetOnAxis(ap=y_id[par][:, n:n + 1], axis=0),
                            in_=y[n % Y_RING][:, :], in_offset=None, bounds_check=(tiles + blocks) * P - 1,
                            compute_op=ALU.add).then_inc(add_dma[n % Y_RING], 16)

            run_experts(pool, expert)

        @block.scalar
        def _(act):
            def need(name, t, per_tile=1, n=1):
                act.wait_ge(S[name], t.count(per_tile, n))

            def done(ins, name):
                ins.then_inc(S[name], 1)

            a = nc.scalar

            act.wait_ge(S["setup_pool"], 1)

            def exp_head(t, n):
                if t.exists(tiles):
                    if t.it is not None or 16 * t.c + n >= PROBS:
                        before, m = (t, n - PROBS) if n >= PROBS else (t + -1, n - PROBS + 16)
                        need("pv_mm", before, 4, m // 4 + 1)
                    need("scoresT_mm", t, 16, n + 1)
                    done(a.activation(probs[n % PROBS][:, :, :], scoresT[scoresT_bank(n)][:, :, :], ACT.Exp), "probs_ok")

            def square(t, m):
                i = t.c % 2
                if m == 0:
                    need("kv_ok", t)
                    if (t + -2).exists(tiles):
                        need("inv_norms_ok", t + -2)
                if (t + -1).exists(tiles):
                    need(("norm_k_ok", "norms_ok")[m], t + -1)
                done(a.activation(squares[:, m, :], kv[i][:, m, :], ACT.Square, accum_out=norms2[i][:, m:m + 1]),
                     ("norm_k_ok", "norms_ok")[m])

            def scale_queries(t, h):
                i = t.c % 2
                if h == 0:
                    need("qT_mm", t)
                    need("a_bias_ok", t)
                    if (t + -2).exists(tiles):
                        need("wo_mm", t + -2)
                for b in range(2):
                    last = a.activation(yT[i][:, h, SEQ * b:SEQ * (b + 1)],
                                        work_a[:, P * h + SEQ * b:P * h + SEQ * (b + 1)], ACT.Identity,
                                        bias=a_bias[i][:, h, b:b + 1], scale=a_scale[i][:, h, b:b + 1])
                if h:
                    done(last, "y_ok")

            def step(s):
                v = s + -1
                for p in range(PAIRS):
                    if p == 7 and v.exists(tiles):
                        scale_queries(v, 1)
                    exp_head(s + -4, 2 * p)
                    if p == 5 and s.exists(tiles):
                        square(s, 0)
                    if p == 6 and s.exists(tiles):
                        square(s, 1)
                    exp_head(s + -4, 2 * p + 1)
                    if p == 6 and v.exists(tiles):
                        scale_queries(v, 0)
                    w, h = (s + -5, 1) if p == 1 else (s + -4, 0)
                    if p in (1, 5) and w.exists(tiles):
                        need("pv_mm", w, 4, 2 * h + 2)
                        if (w + -2).exists(tiles):
                            act.wait_ge(D2["attended_dma"][w.c % 2], (w + -2).loads(4))
                        done(a.copy(pv_sb[w.c % 2][:, 2 * h:2 * h + 2, :], pv_ps[:, :, :]), "pv_ok")
                    if p == 3 and (s + -2).exists(tiles):
                        need("x1_ok", s + -2)
                        done(a.copy(rows_all[:, (s + -2).number(), 0:D], x1[s.c % 2][:, :]), "x1_kept")
                    if p == 2 and s.exists(tiles):
                        need("xnT_mm", s)
                        if (s + -2).exists(tiles):
                            need("qT_mm", s + -2)
                        done(a.copy(xnT[s.c % 2][:, :, :], work_a.rearrange("p (h t) -> p h t", h=HALVES)), "xnT_ok")
                    if p == 7 and v.exists(tiles):
                        need("cT_mm", v)
                        if (v + -4).exists(tiles):
                            need("pv_mm", v + -4, 4, 4)
                        done(a.copy(vT[v.c % RING][:, :, :, 0:DH],
                                    turn_ps[:, 0, :].rearrange("p (l h d) -> p l h d", l=2, d=DH)), "vT_ok")

            run_steps(act, tiles, SKEW, step)

            def split_weights(e, par):
                act.wait_ge(w_dma, 32 * e + 32)
                wait_past(act, S["y_mm"], (e - 1) * len(groups))
                for i, first in pieces:
                    done(a.copy(w_hi[par][:, i, first:first + 512], w_raw[:, i, first:first + 512]), "w_hi_ok")

            for n in range(tiles // 2):
                act.wait_ge(S["mT_mm"], n + 1)
                if n >= 2:
                    act.wait_ge(S["logitsT_mm"], n - 1)
                done(a.copy(mT[n % 2][:, :, :, :].rearrange("p h b t -> p (h b t)"), banks[n % 2]), "mT_ok")
            act.wait_ge(S["logitsT_mm"], tiles // 2)
            for half in range(tiles // 16):
                done(a.copy(logitsT[:, :, :, :].rearrange("p s b t -> p (s b t)")[:, 512 * half:512 * (half + 1)],
                            banks[2 + half]), "logitsT_ok")
            split_weights(0, 0)
            act.wait_ge(S["route_dve"], before_exp)
            done(a.activation(route["prob"][:, :, :], route["p0"][:, :, :], ACT.Exp), "prob_ok")

            def turn(e, par, parts):
                for n in parts:
                    first, size = xT_parts[n]
                    act.wait_ge(S["xT_mm"], e * len(xT_parts) + (n + 1))
                    done(a.copy(xT_hi[par][:, :, P * first:P * (first + size)],
                                banks[6 + n % 2][:, 0:HALVES * P * size].rearrange("p (h t) -> p h t", h=HALVES)),
                         "xT_hi_ok")

            def hidden(e, g):
                cols = P * groups[g][1]
                for k in range(FF // 2):
                    m = g * FF // 2 + k
                    act.wait_ge(S["h_mm"], e * (len(groups) * FF // 2) + (m + 1))
                    if k == 0:
                        wait_past(act, S["y_mm"], hT_free(e, g))
                    done(a.activation(hT_hi[g % 2][:, 2 * k:2 * k + 2, 0:cols],
                                      banks[m % 4][:, 0:2 * cols].rearrange("p (f t) -> p f t", f=2), ACT.Relu),
                         "h_hi_ok")

            def outputs(e, par, g):
                first, size = groups[g]
                if g % 2 == 0:
                    act.wait_ge(S["y_mm"], e * len(groups) + (g + 1))
                    act.wait_ge(S["meta_ok"], e + 1)
                    for b in range(size):
                        n = first + b
                        wait_past(act, add_dma[n % Y_RING], e * (16 * y_uses) + 16 * (n // Y_RING))
                        done(a.activation(y[n % Y_RING][:, :], banks[4][:, D * b:D * (b + 1)], ACT.Copy,
                                          scale=y_gate[par][:, n:n + 1]), "y_act")

            def expert(e, par, more):
                hidden(e, 0)
                for g in range(1, len(groups)):
                    hidden(e, g)
                    if more:
                        turn(e + 1, 1 - par, turn_at[g])
                    outputs(e, par, g - 1)
                    if g == 1 and more:
                        split_weights(e + 1, 1 - par)
                outputs(e, par, len(groups) - 1)

            turn(0, 0, all_parts)
            run_experts(act, expert)

        @block.vector
        def _(dve):
            def need(name, t, per_tile=1, n=1):
                dve.wait_ge(S[name], t.count(per_tile, n))

            def done(ins, name):
                ins.then_inc(S[name], 1)

            v = nc.vector

            for i in range(2):
                v.memset(q_op[i][:, :, :].bitcast(F32), 0.0)
                for j in range(2):
                    v.memset(k_op[i][j][64 * j:64 * j + 64, :, :].bitcast(F32), TWO_BF16_ONES)
                    v.memset(k_op[i][j][64 - 64 * j:128 - 64 * j, :, :].bitcast(F32), 0.0)
            dve.wait_ge(S["setup_in"], 16 * SETUP_LOADS)
            v.tensor_copy(ident_bf[:, :], ident)
            for h in range(HALVES):
                v.tensor_scalar(w_in_g[:, h, :], w_in_raw[:, h, :], gamma_col[:, h:h + 1], None, ALU.mult)
                last = v.tensor_copy(beta_wide[:, h, :], beta_col[:, h:h + 1].broadcast_to([P, P]))
            done(last, "setup_dve")
            dve.wait_ge(S["setup_pe"], 1)
            v.tensor_tensor(bias_kv[:, :], scores[0][:, :, :].rearrange("p a d -> p (a d)"), bias_kv_raw[:, :], ALU.add)
            for b in range(2):
                last = v.tensor_tensor(bias_q[:, :, b], scores[1][:, 0, 0:HALVES], bias_q_raw[:, :], ALU.add)
            done(last, "setup_dve")
            dve.wait_ge(S["setup_dve"], 2)

            def reduce_head(t, p, j):
                n = 2 * p + j + 1
                need("scores_mm", t, 16, n)
                done(v.tensor_reduce(neg_max[p // 4][:, j, 2 * (p % 4):2 * (p % 4) + 2], scores[j][:, :, :], AX.X, ALU.max,
                                     negate=True), "row_max_ok")

            def x1_add(t):
                i = t.c % 2
                need("wo_mm", t)
                need("base_ok", t)
                if (t + -2).exists(tiles):
                    need("q_full_ok", t + -2)
                    need("x1_kept", t + -2)
                done(v.tensor_tensor(x1[i][:, :], work_a, base[i][:, :], ALU.add), "x1_ok")

            def q_bn(t):
                need("x1_ok", t)
                done(v.bn_stats(q_stats[:, :], x1[t.c % 2][:, :]), "q_bn")

            def q_aggr(t):
                wait_apart(dve, S["q_bn"], t.count(1, 1))
                done(v.bn_aggr(q_mv[:, :], q_stats[:, :]), "q_mv_ok")

            def q_scale(t):
                i = t.c % 2
                need("q_mv_ok", t)
                if (t + -2).exists(tiles):
                    need("q_full_ok", t + -2)
                v.tensor_scalar(q_var[i][:, :], q_mv[:, 1:2], float(DH), DH * EPS, ALU.mult, ALU.add)
                done(v.tensor_scalar(q_nmean[i][:, :], q_mv[:, 0:1], -1.0, None, ALU.mult), "q_var_ok")

            def x_bn(t):
                i = t.c % 2
                dve.wait_ge(D2["x_dma"][i], t.loads(1))
                if (t + -2).exists(tiles):
                    need("affine_ok", t + -2)
                    need("xn_ok", t + -2)
                done(v.bn_stats(x_stats[i][:, :], x_in[i][:, :]), "x_bn")

            def x_aggr(t):
                wait_apart(dve, S["x_bn"], t.count(1, 1))
                done(v.bn_aggr(x_mv[t.c % 2][:, :], x_stats[t.c % 2][:, :]), "x_mv_ok")

            def x_scale(t):
                i = t.c % 2
                need("x_mv_ok", t)
                v.tensor_scalar(x_var[i][:, 0:1], x_mv[i][:, 1:2], 1.0, EPS, ALU.mult, ALU.add)
                v.tensor_scalar(x_var[i][:, 1:2], x_mv[i][:, 1:2], 1.0 + EPS, EPS * EPS, ALU.mult, ALU.add)
                done(v.tensor_scalar(x_nmean[i][:, :], x_mv[i][:, 0:1], -1.0, None, ALU.mult), "x_var_ok")

            def kv_bias(t):
                i = t.c % 2
                if (t + -2).exists(tiles):
                    need("kv_prod_ok", t + -2)
                    need("norms_ok", t + -2)
                need("kv_mm", t)
                done(v.tensor_tensor(kv[i][:, :, :], work[:, :, :], bias_kv[:, :].rearrange("p (a d) -> p a d", a=2),
                                     ALU.add), "kv_ok")

            def x2_add(t):
                i = t.c % 2
                need("attn_ok", t)
                need("x1_kept", t)
                if (t + -2).exists(tiles):
                    dve.wait_ge(D2["x2_dma"][i], (t + -2).loads(1))
                done(v.scalar_tensor_tensor(x2[i][:, :], attn[i][:, :], xgamma[:, :], rows_all[:, t.number(), 0:D],
                                            ALU.mult, ALU.add), "x2_ok")

            def m_bn(t):
                need("x2_ok", t)
                done(v.bn_stats(m_stats[:, :], x2[t.c % 2][:, :]), "m_bn")

            def m_aggr(t):
                wait_apart(dve, S["m_bn"], t.count(1, 1))
                done(v.bn_aggr(m_mv[:, :], m_stats[:, :]), "m_mv_ok")

            def m_scale(t):
                need("m_mv_ok", t)
                v.tensor_scalar(m_var[t.c % 2][:, :], m_mv[:, 1:2], 1.0, EPS, ALU.mult, ALU.add)
                done(v.tensor_scalar(m_nmean[t.c % 2][:, :], m_mv[:, 0:1], -1.0, None, ALU.mult), "m_var_ok")

            def m_out(t):
                need("m_rstd_ok", t)
                done(v.tensor_scalar(rows_all[:, t.number(), 0:D], x2[t.c % 2][:, :], m_nmean[t.c % 2][:, :],
                                     m_rstd[t.c % 2][:, :], ALU.add, ALU.mult), "m_ok")

            def a_factor(t):
                need("a_mm", t)
                if (t + -2).exists(tiles):
                    need("y_ok", t + -2)
                done(v.tensor_scalar(a_scale[t.c % 2][:, :, :], work_b[:, 0:4].rearrange("p (h b) -> p h b", h=HALVES),
                                     0.5, 0.5, ALU.mult, ALU.add), "a_scale_ok")

            def a_times_bias(t):
                need("a_scale_ok", t)
                done(v.tensor_tensor(a_bias[t.c % 2][:, :, :], a_scale[t.c % 2][:, :, :], bias_q[:, :, :], ALU.mult),
                     "a_bias_ok")

            def invert_sums(t):
                i = t.c % 2
                dve.wait_ge(D2["sums_dma"][i], t.loads(1))
                if (t + -2).exists(tiles):
                    dve.wait_ge(D2["inverses_dma"][i], (t + -2).loads(1))
                done(v.reciprocal(inv_sums[i][:, :], sums[i][:, :]), "inv_sums_ok")

            def rows_of_maxima(t, g):
                need("max_mm", t, 2, g + 1)
                if (t + -1).exists(tiles):
                    dve.wait_ge(D2["max_dma"][g], (t + -1).count(32, 32))
                done(v.tensor_copy(max_rows[g][:, :], max_ps), "max_rows_ok")

            def max_hi(t, g):
                need("row_max_ok", t, 16, 8 * g + 8)
                if (t + -1).exists(tiles):
                    need("max_mm", t + -1, 2, g + 1)
                done(v.tensor_copy(max_parts[g][:, :, 0, :], neg_max[g][:, :, :]), "max_hi_ok")

            def max_mid(t, g):
                need("max_hi_ok", t, 2, g + 1)
                done(v.tensor_tensor(max_parts[g][:, :, 1, :], neg_max[g][:, :, :], max_parts[g][:, :, 0, :],
                                     ALU.subtract), "max_mid_ok")

            def follow(s, p, j):
                def on(back, work_on, *more):
                    t = s + -back
                    if t.exists(tiles):
                        work_on(t, *more)
                if (p, j) == (0, 0):
                    on(4, max_mid, 1)
                elif (p, j) == (0, 1):
                    on(2, x1_add)
                elif (p, j) == (1, 0):
                    on(2, q_bn)
                    on(4, rows_of_maxima, 1)
                elif (p, j) == (1, 1):
                    on(2, q_aggr)
                    on(2, q_scale)
                elif (p, j) == (2, 1):
                    on(-1, x_bn)
                    on(7, m_out)
                elif (p, j) == (3, 0):
                    on(-1, x_aggr)
                elif (p, j) == (3, 1):
                    on(-1, x_scale)
                    on(3, max_hi, 0)
                elif (p, j) == (4, 0):
                    on(3, max_mid, 0)
                elif (p, j) == (4, 1):
                    on(3, rows_of_maxima, 0)
                    on(0, kv_bias)
                elif (p, j) == (5, 0):
                    on(6, x2_add)
                elif (p, j) == (5, 1):
                    on(6, m_bn)
                elif (p, j) == (6, 0):
                    on(6, m_aggr)
                    on(1, a_factor)
                elif (p, j) == (6, 1):
                    on(6, m_scale)
                    on(1, a_times_bias)
                elif (p, j) == (7, 0):
                    on(5, invert_sums)
                elif (p, j) == (7, 1):
                    on(3, max_hi, 1)

            def step(s):
                for p in range(PAIRS):
                    for j in range(2):
                        if (s + -3).exists(tiles):
                            reduce_head(s + -3, p, j)
                        follow(s, p, j)

            for first in (x_bn, x_aggr, x_scale):
                first(Tile(None, 0))
            run_steps(dve, tiles, SKEW, step)

            phase1_over(dve)
            def split_weights(e, par):
                wait_past(dve, S["y_mm"], (e - 1) * len(groups))
                for n, (i, first) in enumerate(pieces):
                    dve.wait_ge(S["w_hi_ok"], e * len(pieces) + (n + 1))
                    done(v.tensor_tensor(w_lo[par][:, i, first:first + 512], w_raw[:, i, first:first + 512],
                                         w_hi[par][:, i, first:first + 512].bitcast(F32), ALU.subtract), "w_lo_ok")

            links = [0]

            def link(ins):
                links[0] += 1
                ins.then_inc(S["route_dve"], 1)
                dve.wait_ge(S["route_dve"], links[0])

            def wide(name):
                return flat[name][:, :].rearrange("p (t o) -> p t o", o=1).broadcast_to([P, tiles, EXPERTS])

            def per_token(row):
                return row.rearrange("p (o e) -> p o e", o=1).broadcast_to([P, tiles, EXPERTS])

            r = {n: route[n][:, :, :] for n in route}
            v.tensor_copy(rows_all[:, :, TOKEN_ID], token_no)
            dve.wait_ge(S["logit_mm"], 1)
            for slot in range(tiles // 8):
                ps = banks[4 + slot // 2][:, D * (slot % 2):D * (slot % 2 + 1)].rearrange("p (b c e) -> p b c e", b=2, c=4)
                last = v.tensor_copy(route["logit"][:, 8 * slot:8 * slot + 8, :].rearrange("p (c b) e -> p b c e", b=2),
                                     ps[:, :, :, 0:EXPERTS])
            link(last)
            for k, (src, hot) in enumerate((("logit", "hot0"), ("rest", "hot1"))):
                link(v.tensor_reduce(flat[f"top{k}"][:, :], r[src], AX.X, ALU.max))
                link(v.tensor_tensor(r["t0"], r[src], wide(f"top{k}"), ALU.is_equal))
                link(v.scalar_tensor_tensor(r["key"], r["t0"], -100.0, per_token(expert_no), ALU.mult, ALU.add))
                link(v.tensor_reduce(flat[f"id{k}"][:, :], r["key"], AX.X, ALU.min))
                link(v.tensor_tensor(r[hot], r["key"], wide(f"id{k}"), ALU.is_equal))
                if k == 0:
                    v.tensor_tensor(r["p0"], r["logit"], wide("top0"), ALU.subtract)
                    link(v.scalar_tensor_tensor(r["rest"], r["hot0"], -3.0e38, r["logit"], ALU.mult, ALU.add))
            link(v.tensor_tensor(r["both"], r["hot0"], r["hot1"], ALU.add))
            assert links[0] == before_count
            dve.wait_ge(S["prob_ok"], 1)
            v.tensor_reduce(flat["z"][:, :], r["prob"], AX.X, ALU.add)
            link(v.tensor_tensor(r["g0"], r["both"], r["prob"], ALU.mult))
            link(v.reciprocal(flat["rz"][:, :], flat["z"][:, :]))
            v.tensor_tensor(rows_all[:, :, GATES:ROW], r["g0"], wide("rz"), ALU.mult)
            dve.wait_ge(S["count_mm"], 1)
            link(v.tensor_copy(per_expert["total"][:, :, :],
                               banks[1][:, 0:EXPERTS * tiles].rearrange("p (t e) -> p e t", e=EXPERTS)))
            link(v.tensor_tensor_scan(per_expert["through"][:, :, :].rearrange("p e t -> p (e t)"), not_first,
                                      per_expert["total"][:, :, :].rearrange("p e t -> p (e t)"), 0.0,
                                      ALU.mult, ALU.add))
            link(v.tensor_tensor(per_expert["before"][:, :, :], per_expert["through"][:, :, :],
                                 per_expert["total"][:, :, :], ALU.subtract))
            link(v.tensor_tensor(r["pos"], banks[0][:, 0:EXPERTS * tiles].rearrange("p (t e) -> p t e", e=EXPERTS),
                                 per_expert["before"][:, :, :].rearrange("p e t -> p t e"), ALU.add))
            v.tensor_tensor(r["slot"], r["pos"], per_token(expert_base), ALU.add)
            link(v.tensor_scalar(r["e0"], r["pos"], float(capacity), FAR, ALU.is_ge, ALU.mult))
            link(v.tensor_tensor(r["e1"], r["e0"], r["slot"], ALU.add))
            v.tensor_tensor(r["t0"], r["hot0"], r["e1"], ALU.mult)
            link(v.tensor_tensor(r["t1"], r["hot1"], r["e1"], ALU.mult))
            for k in range(TOP_K):
                last = v.tensor_reduce(flat[f"slot{k}"][:, :], r[f"t{k}"], AX.X, ALU.add)
            link(last)
            for k in range(TOP_K):
                last = v.tensor_copy(slot_no[k][:, :], flat[f"slot{k}"][:, :])
            done(last, "slot_ok")

            def turn(e, par, parts):
                if 0 in parts:
                    dve.wait_ge(slots_dma, 16 * e + 16)
                    for i in range(Y_RING):
                        wait_past(dve, add_dma[i], (e - 1) * (16 * y_uses))
                    wait_past(dve, S["y_act"], (e - 1) * n_y[0])
                    done(v.scalar_tensor_tensor(id_shift[:, :], slots_in[:, :, TOKEN_ID], float(tiles * P), block_rows,
                                                ALU.is_ge, ALU.mult), "id_shift_ok")
                    dve.wait_ge(S["id_shift_ok"], e + 1)
                    v.tensor_tensor(y_id[par][:, :], slots_in[:, :, TOKEN_ID], id_shift[:, :], ALU.add)
                    done(v.tensor_copy(y_gate[par][:, :], slots_in[:, :, bass.ds(GATES + e, 1)].rearrange(
                        "p n o -> p (n o)")), "meta_ok")
                for n in parts:
                    first, size = xT_parts[n]
                    dve.wait_ge(S["xT_hi_ok"], e * len(xT_parts) + (n + 1))
                    cols = slice(P * first, P * (first + size))
                    done(v.tensor_tensor(xT_lo[par][:, :, cols], banks[6 + n % 2][:, 0:HALVES * P * size].rearrange(
                        "p (h t) -> p h t", h=HALVES), xT_hi[par][:, :, cols].bitcast(F32), ALU.subtract), "xT_lo_ok")

            def hidden(e, g):
                cols = P * groups[g][1]
                for k in range(FF // 2):
                    m = g * FF // 2 + k
                    dve.wait_ge(S["h_hi_ok"], e * (len(groups) * FF // 2) + (m + 1))
                    if k == 0:
                        wait_past(dve, S["y_mm"], hT_free(e, g))
                    done(v.scalar_tensor_tensor(hT_lo[g % 2][:, 2 * k:2 * k + 2, 0:cols],
                                                banks[m % 4][:, 0:2 * cols].rearrange("p (f t) -> p f t", f=2), 0.0,
                                                hT_hi[g % 2][:, 2 * k:2 * k + 2, 0:cols].bitcast(F32),
                                                ALU.max, ALU.subtract), "h_lo_ok")

            def outputs(e, par, g):
                first, size = groups[g]
                if g % 2:
                    dve.wait_ge(S["y_mm"], e * len(groups) + (g + 1))
                    dve.wait_ge(S["meta_ok"], e + 1)
                    for b in range(size):
                        n = first + b
                        wait_past(dve, add_dma[n % Y_RING], e * (16 * y_uses) + 16 * (n // Y_RING))
                        done(v.tensor_scalar(y[n % Y_RING][:, :], banks[5][:, D * b:D * (b + 1)],
                                             y_gate[par][:, n:n + 1], None, ALU.mult), "y_dve")

            def expert(e, par, more):
                hidden(e, 0)
                for g in range(1, len(groups)):
                    hidden(e, g)
                    if more:
                        turn(e + 1, 1 - par, turn_at[g])
                    outputs(e, par, g - 1)
                    if g == 1 and more:
                        split_weights(e + 1, 1 - par)
                outputs(e, par, len(groups) - 1)

            split_weights(0, 0)
            turn(0, 0, all_parts)
            run_experts(dve, expert)

        @block.tensor
        def _(pe):
            def need(name, t, per_tile=1, n=1):
                pe.wait_ge(S[name], t.count(per_tile, n))

            def done(ins, name):
                ins.then_inc(S[name], 1)

            mm = nc.tensor.matmul

            pe.wait_ge(S["setup_dve"], 1)
            for h in range(HALVES):
                mm(scores[0][:, :, :].rearrange("p a d -> p (a d)"), beta_wide[:, h, :], w_in_raw[:, h, D:3 * D],
                   start=h == 0, stop=h == HALVES - 1)
            for o in range(HALVES):
                for h in range(HALVES):
                    last = mm(scores[1][:, 0, o:o + 1], w_in_raw[:, h, P * o:P * (o + 1)], beta_col[:, h:h + 1],
                              start=h == 0, stop=h == HALVES - 1)
            done(last, "setup_pe")
            pe.wait_ge(S["setup_pool"], 1)
            pe.wait_ge(S["setup_dve"], 2)

            def max_turn(s, p):
                t, g = max_group(s, p)
                if t.exists(tiles):
                    need("max_mid_ok", t, 2, g + 1)
                    if g or (t + -1).exists(tiles):
                        before, gb = (t, 0) if g else (t + -1, 1)
                        need("max_rows_ok", before, 2, gb + 1)
                    if g == 1:
                        if (t + 2).exists(tiles):
                            need("vT_ok", t + 2)
                    done(nc.tensor.transpose(max_ps, max_parts[g][:, :, :, :].rearrange(
                        "p j m q -> p (j m q)"), ident_bf[:, :]), "max_mm")

            def scores_mms(B, p, j):
                if B.exists(tiles):
                    if p == 0 and j == 0:
                        pe.wait_ge(D2["q_op_dma"][B.c % 2], B.loads(2))
                        pe.wait_ge(D2["k_op_dma"][B.c % 2], B.loads(2))
                    if B.it is not None or B.c > 0 or p > 0:
                        need("row_max_ok", B, 16, 2 * p + j - 1)
                    rows = slice(0, 64 * j + OPK)
                    for h in range(2):
                        last = mm(scores[j][:, h, :], q_op[B.c % RING][rows, p, P * h:P * (h + 1)],
                                  k_op[B.c % RING][j][rows, p, :], start=True, stop=True)
                    done(last, "scores_mm")

            def scoresT_mms(t, pc, j):
                if t.exists(tiles):
                    if pc % 4 == 0 and j == 0:
                        pe.wait_ge(D2["max_dma"][pc // 4], t.count(32, 32))
                    n = 2 * pc + j
                    if n >= 3:
                        need("probs_ok", t, 16, max(m for m in range(n) if scoresT_bank(m) == scoresT_bank(n)) + 1)
                    elif (t + -1).exists(tiles):
                        need("probs_ok", t + -1, 16, (13, 16, 15)[n])
                    for h in range(2):
                        last = mm(scoresT[scoresT_bank(n)][:, h, :], k_op[t.c % RING][j][:, pc, P * h:P * (h + 1)],
                                  q_op[t.c % RING][:, pc, :], start=True, stop=True)
                    done(last, "scoresT_mm")

            def pv_mms(s, p, h):
                t, g = (s + -4, p // 2 - 1) if p else (s + -5, 3)
                if t.exists(tiles):
                    if h == 0:
                        need("probs_ok", t, 16, 4 * g + 4)
                        need("vT_ok", t)
                        if g % 2 == 0 and (t.it is not None or 2 * t.c + g // 2 >= 1):
                            need("pv_ok", t, 2, g // 2)
                    for c in range(4):
                        j, pair = c % 2, 2 * g + c // 2
                        last = mm(pv_ps[32 * c:32 * c + 32, g % 2, :], vT[t.c % RING][:, h, HEADS * j + pair, :],
                                  probs[(2 * pair + j) % PROBS][:, h, :], start=h == 0, stop=h == 1,
                                  skip_group_check=True)
                    if h:
                        done(last, "pv_mm")

            def step(s):
                B, v, u = s + -3, s + -1, s + -2
                for p in range(PAIRS):
                    for j in range(2):
                        scores_mms(B, p, j)
                        scoresT_mms(s + -4, p, j)
                        if p in (0, 4) and j == 1:
                            max_turn(s, p)
                        if (p % 2, j) == (0, 1):
                            pv_mms(s, p, 0)
                        if (p % 2, j) == (1, 0):
                            pv_mms(s, p - 1, 1)
                        if (p, j) == (0, 0) and u.exists(tiles):
                            need("y_ok", u)
                            if v.exists(tiles):
                                need("kv_ok", v)
                            for h in range(HALVES):
                                last = mm(work_a, yT[u.c % 2][:, h, :], w_out_sb[:, h, :], start=h == 0, stop=h == 1)
                            done(last, "wo_mm")
                        if (p, j) == (2, 0) and s.exists(tiles):
                            need("xn_ok", s)
                            if v.exists(tiles):
                                need("kv_ok", v)
                            if u.exists(tiles):
                                need("x1_ok", u)
                            for h in range(HALVES):
                                last = nc.tensor.transpose(work_a[:, P * h:P * (h + 1)],
                                                           xn[s.c % 2][:, P * h:P * (h + 1)], ident)
                            done(last, "xnT_mm")
                        if (p, j) in ((3, 1), (4, 0)) and s.exists(tiles):
                            need("xnT_ok", s)
                            h = 1 - j
                            last = mm(work[:, :, :].rearrange("p a d -> p (a d)"), xnT[s.c % 2][:, h, :],
                                      w_in_g[:, h, D:3 * D], start=h == 0, stop=h == 1)
                            if h:
                                done(last, "kv_mm")
                        if (p, j) == (5, 1) and v.exists(tiles):
                            need("c_parts_ok", v)
                            if B.exists(tiles):
                                need("max_rows_ok", B, 2, 1)
                            for h in range(HALVES):
                                last = nc.tensor.transpose(turn_ps[:, 0, P * h:P * (h + 1)],
                                                           c_in[v.c % RING][:, P * h:P * (h + 1)], ident)
                            done(last, "cT_mm")
                        if (p, j) in ((5, 1), (6, 0)) and v.exists(tiles):
                            i, o = v.c % 2, 1 - j
                            if o == 0 and s.exists(tiles):
                                need("kv_ok", s)
                            for h in range(HALVES):
                                last = mm(work_a[:, P * o:P * (o + 1)], w_in_g[:, h, P * o:P * (o + 1)],
                                          xnT[i][:, h, :], start=h == 0, stop=h == 1)
                            if o:
                                done(last, "qT_mm")
                                need("kv_prod_ok", v)
                                need("row_weight_ok", v)
                                for h in range(HALVES):
                                    last = mm(work_b[:, 2 * h:2 * h + 2], kv_prod[i][:, P * h:P * (h + 1)],
                                              row_weight[i][:, :], start=True, stop=True)
                                done(last, "a_mm")

            run_steps(pe, tiles, SKEW, step)

            transpose = nc.tensor.transpose
            pe.wait_ge(S["row_max_ok"], 16 * tiles)
            pe.wait_ge(S["probs_ok"], 16 * tiles)
            pe.wait_ge(S["wg_dma"], 16)
            for n in range(tiles // 2 + 1):
                if n < tiles // 2:
                    pe.wait_ge(S["m_ok"], 2 * n + 2)
                    if n >= 2:
                        pe.wait_ge(S["mT_ok"], n - 1)
                    for h in range(HALVES):
                        for b in range(2):
                            last = transpose(banks[n % 2][:, D * h + P * b:D * h + P * (b + 1)],
                                             rows_all[:, 2 * n + b, P * h:P * (h + 1)], ident_keep[:, :])
                    done(last, "mT_mm")
                if n > 0:
                    m = n - 1
                    pe.wait_ge(S["mT_ok"], m + 1)
                    c, slot = m % 4, m // 4
                    for h in range(HALVES):
                        last = mm(banks[2 + slot // 2][32 * c:32 * c + 32, D * (slot % 2):D * (slot % 2 + 1)],
                                  wg_sb[:, h, :], mT[m % 2][:, h, :, :].rearrange("p b t -> p (b t)"),
                                  start=h == 0, stop=h == 1, skip_group_check=True)
                    done(last, "logitsT_mm")
            pe.wait_ge(S["logitsT_ok"], tiles // 16)
            phase1_over(pe)
            for slot in range(tiles // 8):
                for b in range(2):
                    last = transpose(banks[4 + slot // 2][:, D * (slot % 2) + P * b:D * (slot % 2) + P * (b + 1)],
                                     logitsT[:, slot, b, :], ident_keep[:, :])
            done(last, "logit_mm")
            pe.wait_ge(S["route_dve"], before_count)
            for i, which in enumerate((earlier, ones[:, :])):
                last = mm(banks[i][:, 0:EXPERTS * tiles], which, route["both"][:, :, :].rearrange("p t e -> p (t e)"),
                          start=True, stop=True)
            done(last, "count_mm")

            def turn(e, par, parts):
                pe.wait_ge(slots_dma, 16 * e + 16)
                for n in parts:
                    first, size = xT_parts[n]
                    wait_past(pe, S["xT_lo_ok"], e * len(xT_parts) + (n - 1))
                    for h in range(HALVES):
                        for b in range(size):
                            last = transpose(banks[6 + n % 2][:, P * (size * h + b):P * (size * h + b + 1)],
                                             slots_in[:, first + b, P * h:P * (h + 1)], ident_keep[:, :])
                    done(last, "xT_mm")

            def split_mms(out, terms):
                for n, (lhsT, rhs) in enumerate(terms):
                    last = mm(out, lhsT, rhs, start=n == 0, stop=n == len(terms) - 1)
                return last

            def hidden(e, par, g):
                first, size = groups[g]
                cols = slice(P * first, P * (first + size))
                for k in range(FF // 2):
                    m = g * FF // 2 + k
                    wait_past(pe, S["h_lo_ok"], e * (len(groups) * FF // 2) + (m - 3))
                    for f in range(2):
                        fs = slice(P * (2 * k + f), P * (2 * k + f + 1))
                        last = split_mms(banks[m % 4][:, P * size * f:P * size * (f + 1)],
                                         [(w1_of(w)[:, h, fs], x[:, h, cols]) for h in range(HALVES)
                                          for w, x in ((w_hi[par], xT_hi[par]), (w_hi[par], xT_lo[par]),
                                                       (w_lo[par], xT_hi[par]))])
                    done(last, "h_mm")

            def outputs(e, par, g):
                pe.wait_ge(S["h_lo_ok"], e * (len(groups) * FF // 2) + (g + 1) * FF // 2)
                wait_past(pe, S[("y_act", "y_dve")[g % 2]], e * n_y[g % 2] + y_before(g))
                for b in range(groups[g][1]):
                    rows = slice(P * b, P * (b + 1))
                    last = split_mms(banks[4 + g % 2][:, D * b:D * (b + 1)],
                                     [(h[:, f, rows], w2_of(w)[:, f, :]) for f in range(FF)
                                      for h, w in ((hT_hi[g % 2], w_hi[par]), (hT_hi[g % 2], w_lo[par]),
                                                   (hT_lo[g % 2], w_hi[par]))])
                done(last, "y_mm")

            def expert(e, par, more):
                pe.wait_ge(S["w_lo_ok"], (e + 1) * len(pieces))
                pe.wait_ge(S["xT_lo_ok"], (e + 1) * len(xT_parts))
                hidden(e, par, 0)
                for g in range(1, len(groups)):
                    hidden(e, par, g)
                    if more:
                        turn(e + 1, 1 - par, turn_at[g])
                    outputs(e, par, g - 1)
                outputs(e, par, len(groups) - 1)

            turn(0, 0, all_parts)
            run_experts(pe, expert)


_INS = ["x", "ctx_2048", "L0_attn_W_in", "L0_attn_b_in", "L0_attn_W_out", "L0_attn_b_out", "L0_attn_gamma",
        "L0_attn_beta", "L0_xattn_gamma", "L0_ffn_Wg", "L0_ffn_w1", "L0_ffn_w2"]


def constants():
    import numpy as np
    rot = D // 2
    inv_freq = (1.0 / 10000.0 ** (np.arange(0, rot, 2, dtype=np.float32) / rot)).astype(np.float32)
    angles = np.repeat(np.arange(SEQ, dtype=np.float32)[:, None] * inv_freq[None, :], 2, axis=-1)
    cos, sin = np.cos(angles).astype(np.float32), np.sin(angles).astype(np.float32)
    sin[:, 0::2] *= -1
    both = lambda a: np.tile(np.concatenate([a, a], axis=1), (2, 1))
    mask = np.zeros((P, 2), np.float32)
    mask[:SEQ, 0] = mask[SEQ:, 1] = 1.0
    return np.ascontiguousarray(np.concatenate([np.eye(P, dtype=np.float32), both(cos), both(sin), mask], axis=1))


def route_constants(tiles):
    import numpy as np
    capacity = -(-5 * tiles * P * TOP_K // (4 * EXPERTS))
    row = np.arange(P)[:, None]
    earlier = row < np.arange(P)[None, :]
    not_first = np.tile(np.arange(tiles) > 0, EXPERTS)[None, :].repeat(P, 0)
    experts = np.arange(EXPERTS)[None, :].repeat(P, 0)
    block_rows = np.arange(0, capacity, P)[None, :].repeat(P, 0)
    return np.ascontiguousarray(np.concatenate([earlier, not_first, experts, experts * capacity,
                                                row + P * np.arange(tiles)[None, :], row + P * tiles, block_rows],
                                               axis=1).astype(np.float32))


def kernel(**inputs):
    import numpy as np
    import concourse.bacc as bacc
    from concourse.bass_utils import run_bass_kernel_spmd

    nc = bacc.Bacc("TRN2", target_bir_lowering=False, num_devices=1)
    tiles = inputs["x"].shape[0] * SEQ // P
    laid_out = {name: np.ascontiguousarray(inputs[name]) for name in _INS}
    laid_out["L0_xattn_gamma"] = laid_out["L0_xattn_gamma"].reshape(1)
    laid_out["constants"] = constants()
    laid_out["route_constants"] = route_constants(tiles)
    arrays, args = {}, []
    for name, a in laid_out.items():
        arrays[f"in_{name}"] = a
        args.append(nc.dram_tensor(f"in_{name}", a.shape, mybir.dt.from_np(a.dtype), kind="ExternalInput").ap())
    spare = route_constants(tiles).shape[1] - (P + EXPERTS * (tiles + 2) + tiles + 1)
    args.append(nc.dram_tensor("out_0", ((tiles + spare) * P, D), mybir.dt.float32, kind="ExternalOutput").ap())
    decoder_block(nc, tiles, *args)
    r = run_bass_kernel_spmd(nc, [arrays], core_ids=[0])
    return r.results[0]["out_0"][:tiles * P].reshape(inputs["x"].shape)
```
